# Optimizing a Trainium2 kernel written in Bass

```python
import numpy as np
import jax
import jax.numpy as jnp

def _softmax(x, axis=-1):
    return jax.nn.softmax(x, axis=axis)

def _gelu(x):
    return jax.nn.gelu(x, approximate=True)

def _silu(x):
    return jax.nn.silu(x)

def _sigmoid(x):
    return jax.nn.sigmoid(x)

def _layernorm(x, axis=-1, eps=1e-05):
    m = jnp.mean(x, axis=axis, keepdims=True)
    v = jnp.var(x, axis=axis, keepdims=True)
    return (x - m) / jnp.sqrt(v + eps)

def _scatter_add(tgt, idx, src, axis=0):
    return tgt.at[idx].add(src)

def _segment_sum(src, seg, n):
    return jax.ops.segment_sum(src, seg, n)
kernel_name = 'mk_perceiver_d1_seqx_r2_88ca54'

def setup_inputs(seed: int=0):
    np.random.seed(seed)
    _w = jnp.asarray

    def _rec_inputs():
        import jax
        import jax.numpy as jnp
        _rk = jax.random.key(seed)
        x = -0.0003929 + 0.9999 * jax.random.normal(jax.random.fold_in(_rk, 1), (8, 64, 512), jnp.float32)
        _lenS = 64 - jax.random.randint(jax.random.fold_in(_rk, 7), (8,), 0, max(1, 64 // 4) + 1, jnp.int32)
        _lenS2 = 512 - jax.random.randint(jax.random.fold_in(_rk, 8), (8,), 0, max(1, 512 // 4) + 1, jnp.int32)
        _ctx_1024P = jax.random.normal(jax.random.fold_in(_rk, 11), (8, 16, 512), jnp.float32)
        _ctx_1024c = jax.random.dirichlet(jax.random.fold_in(_rk, 511), 0.3 * jnp.ones((16,), jnp.float32), (8, 512))
        _ctx_1024t = jnp.einsum('bsk,bkd->bsd', _ctx_1024c, _ctx_1024P)
        _ctx_1024t = _ctx_1024t * jax.lax.rsqrt(jnp.mean(jnp.square(_ctx_1024t)) + 1e-12) * 0.953939
        ctx_1024 = -1.39393e-06 + 0.999914 * (_ctx_1024t + 0.3 * jax.random.normal(jax.random.fold_in(_rk, 611), (8, 512, 512), jnp.float32))
        return (x, ctx_1024)
    x, ctx_1024 = _rec_inputs()

    def _L0_xattn_setup():
        import jax, jax.numpy as jnp
        import numpy as np
        B, C_LEN, Q_LEN, D = (8, 1024, 256, 512)
        key = jax.random.key(seed)
        ks = jax.random.split(key, 10)
        scale = 1.0 / np.sqrt(D)
        return {'c': jax.random.normal(ks[0], (B, C_LEN, D), dtype=jnp.float32), 'q': jax.random.normal(ks[1], (B, Q_LEN, D), dtype=jnp.float32), 'w_cq': jax.random.normal(ks[2], (D,), dtype=jnp.float32) * scale, 'b_cq': jax.random.normal(ks[3], (), dtype=jnp.float32) * scale, 'w_c': jax.random.normal(ks[4], (D,), dtype=jnp.float32) * scale, 'b_c': jax.random.normal(ks[5], (), dtype=jnp.float32) * scale, 'w_q': jax.random.normal(ks[6], (D,), dtype=jnp.float32) * scale, 'b_q': jax.random.normal(ks[7], (), dtype=jnp.float32) * scale, 'W_l': jax.random.normal(ks[8], (D, 4 * D), dtype=jnp.float32) * (1.0 / np.sqrt(4 * D)), 'b_l': jax.random.normal(ks[9], (D,), dtype=jnp.float32) * (1.0 / np.sqrt(4 * D))}
    _L0_xattn_all = _L0_xattn_setup()
    _L0_xattn_in = {k: v for k, v in _L0_xattn_all.items() if k in ('w_cq', 'b_cq', 'w_c', 'b_c', 'w_q', 'b_q', 'W_l', 'b_l')}
    del _L0_xattn_all

    def _L0_attn_setup():
        import jax, jax.numpy as jnp
        import numpy as np
        import math
        D_MODEL = 512
        NUM_HEADS = 16
        HEAD_DIM = D_MODEL // NUM_HEADS
        B, S = (2, 1024)

        def _causal_attn(q, k, v):
            scale = 1.0 / math.sqrt(q.shape[-1])
            scores = jnp.einsum('bthd,bshd->bhts', q, k) * scale
            t = q.shape[1]
            mask = jnp.tril(jnp.ones((t, t), dtype=bool))
            scores = jnp.where(mask, scores, -jnp.inf)
            attn = jax.nn.softmax(scores, axis=-1)
            return jnp.einsum('bhts,bshd->bthd', attn, v)
        key = jax.random.key(seed)
        ks = jax.random.split(key, 7)
        sc = 0.02
        return {'x': jax.random.normal(ks[0], (B, S, D_MODEL), dtype=jnp.float32), 'Wqkv_w': jax.random.normal(ks[1], (3 * D_MODEL, D_MODEL), dtype=jnp.float32) * sc, 'Wqkv_b': jnp.zeros((3 * D_MODEL,), dtype=jnp.float32), 'conv_w': jax.random.normal(ks[2], (D_MODEL, D_MODEL, 3), dtype=jnp.float32) * sc, 'conv_b': jnp.zeros((D_MODEL,), dtype=jnp.float32), 'out_w': jax.random.normal(ks[3], (D_MODEL, D_MODEL), dtype=jnp.float32) * sc, 'out_b': jnp.zeros((D_MODEL,), dtype=jnp.float32)}
    _L0_attn_all = _L0_attn_setup()
    _L0_attn_in = {k: v for k, v in _L0_attn_all.items() if k in ('Wqkv_w', 'Wqkv_b', 'conv_w', 'conv_b', 'out_w', 'out_b')}
    del _L0_attn_all

    def _L0_ffn_setup():
        import jax, jax.numpy as jnp
        import numpy as np
        B, S, D, E, F = (2, 512, 512, 14, 1024)
        key = jax.random.key(seed)
        k0, k1, k2, k3 = jax.random.split(key, 4)
        h = jax.random.normal(k0, (B, S, D), jnp.float32)
        gate_w = jax.random.normal(k1, (E, D), jnp.float32) * 0.02
        w1 = jax.random.normal(k2, (E, D, F), jnp.float32) * (1.0 / np.sqrt(D).astype(np.float32))
        b1 = jnp.zeros((E, F), jnp.float32)
        w2 = jax.random.normal(k3, (E, F, D), jnp.float32) * (1.0 / np.sqrt(F).astype(np.float32))
        b2 = jnp.zeros((E, D), jnp.float32)
        return {'h': h, 'gate_w': gate_w, 'w1': w1, 'b1': b1, 'w2': w2, 'b2': b2}
    _L0_ffn_all = _L0_ffn_setup()
    _L0_ffn_in = {k: v for k, v in _L0_ffn_all.items() if k in ('gate_w', 'w1', 'b1', 'w2', 'b2')}
    del _L0_ffn_all
    return {'x': x, 'ctx_1024': ctx_1024, 'L0_xattn_w_cq': _L0_xattn_in['w_cq'], 'L0_xattn_b_cq': _L0_xattn_in['b_cq'], 'L0_xattn_w_c': _L0_xattn_in['w_c'], 'L0_xattn_b_c': _L0_xattn_in['b_c'], 'L0_xattn_w_q': _L0_xattn_in['w_q'], 'L0_xattn_b_q': _L0_xattn_in['b_q'], 'L0_xattn_W_l': _L0_xattn_in['W_l'], 'L0_xattn_b_l': _L0_xattn_in['b_l'], 'L0_attn_Wqkv_w': _L0_attn_in['Wqkv_w'], 'L0_attn_Wqkv_b': _L0_attn_in['Wqkv_b'], 'L0_attn_conv_w': _L0_attn_in['conv_w'], 'L0_attn_conv_b': _L0_attn_in['conv_b'], 'L0_attn_out_w': _L0_attn_in['out_w'], 'L0_attn_out_b': _L0_attn_in['out_b'], 'L0_ffn_gate_w': _L0_ffn_in['gate_w'], 'L0_ffn_w1': _L0_ffn_in['w1'], 'L0_ffn_b1': _L0_ffn_in['b1'], 'L0_ffn_w2': _L0_ffn_in['w2'], 'L0_ffn_b2': _L0_ffn_in['b2']}

def reference(x, ctx_1024, L0_xattn_w_cq, L0_xattn_b_cq, L0_xattn_w_c, L0_xattn_b_c, L0_xattn_w_q, L0_xattn_b_q, L0_xattn_W_l, L0_xattn_b_l, L0_attn_Wqkv_w, L0_attn_Wqkv_b, L0_attn_conv_w, L0_attn_conv_b, L0_attn_out_w, L0_attn_out_b, L0_ffn_gate_w, L0_ffn_w1, L0_ffn_b1, L0_ffn_w2, L0_ffn_b2):
    import jax
    import jax.numpy as jnp

    def _L0_xattn_ref(c, q, w_cq, b_cq, w_c, b_c, w_q, b_q, W_l, b_l):
        import jax, jax.numpy as jnp
        import numpy as np
        B, C_LEN, Q_LEN, D = (8, 1024, 256, 512)
        cq = jnp.einsum('bcd,bqd,d->bcq', c, q, w_cq) + b_cq
        s = (c @ w_c + b_c)[:, :, None] + (q @ w_q + b_q)[:, None, :] + cq
        a = jax.nn.softmax(s, axis=2)
        c2q_att = jnp.einsum('bcq,bqd->bcd', a, q)
        b_att = jax.nn.softmax(jnp.max(s, axis=2), axis=1)
        q2c_att = jnp.einsum('bc,bcd->bd', b_att, c)[:, None, :]
        x = jnp.concatenate([c, c2q_att, c * c2q_att, c * q2c_att], axis=-1)
        z = x @ W_l.T + b_l
        return z

    def _L0_attn_ref(x, Wqkv_w, Wqkv_b, conv_w, conv_b, out_w, out_b):
        import jax, jax.numpy as jnp
        import numpy as np
        import math
        D_MODEL = 512
        NUM_HEADS = 16
        HEAD_DIM = D_MODEL // NUM_HEADS
        B, S = (2, 1024)

        def _causal_attn(q, k, v):
            scale = 1.0 / math.sqrt(q.shape[-1])
            scores = jnp.einsum('bthd,bshd->bhts', q, k) * scale
            t = q.shape[1]
            mask = jnp.tril(jnp.ones((t, t), dtype=bool))
            scores = jnp.where(mask, scores, -jnp.inf)
            attn = jax.nn.softmax(scores, axis=-1)
            return jnp.einsum('bhts,bshd->bthd', attn, v)
        b, s, d = x.shape
        qkv = x @ Wqkv_w.T + Wqkv_b
        qkv = qkv.reshape(b, s, 3, NUM_HEADS, HEAD_DIM)
        q, k, v = (qkv[:, :, 0], qkv[:, :, 1], qkv[:, :, 2])
        ctx = _causal_attn(q, k, v)
        ctx_c = ctx.reshape(b, s, d).transpose(0, 2, 1)
        conv_out = jax.lax.conv_general_dilated(ctx_c, conv_w, window_strides=(1,), padding=[(1, 1)], dimension_numbers=('NCH', 'OIH', 'NCH')) + conv_b[None, :, None]
        q2 = conv_out.transpose(0, 2, 1).reshape(b, s, NUM_HEADS, HEAD_DIM)
        ctx2 = _causal_attn(q2, k, v)
        out = ctx2.reshape(b, s, d) @ out_w.T + out_b
        return out

    def _L0_ffn_ref(h, gate_w, w1, b1, w2, b2):
        import jax, jax.numpy as jnp
        import numpy as np
        B, S, D, E, F = (2, 512, 512, 14, 1024)
        Bb, Ss, Dd = h.shape
        x = h.reshape(Bb * Ss, Dd)
        logits = x @ gate_w.T
        probs = jax.nn.softmax(logits, axis=-1)
        top2_p, top2_i = jax.lax.top_k(probs, 2)
        w = top2_p / jnp.maximum(top2_p.sum(-1, keepdims=True), 1e-10)
        hh = jnp.einsum('nd,edf->nef', x, w1) + b1
        hh = jax.nn.gelu(hh, approximate=False)
        all_out = jnp.einsum('nef,efd->ned', hh, w2) + b2
        n = jnp.arange(x.shape[0])
        out0 = all_out[n, top2_i[:, 0]]
        out1 = all_out[n, top2_i[:, 1]]
        moe_out = w[:, 0:1] * out0 + w[:, 1:2] * out1
        result = jnp.clip(x + moe_out, -100.0, 100.0).reshape(Bb, Ss, Dd)
        return result
    x = x + _L0_xattn_ref(_layernorm(x, axis=-1), ctx_1024, L0_xattn_w_cq, L0_xattn_b_cq, L0_xattn_w_c, L0_xattn_b_c, L0_xattn_w_q, L0_xattn_b_q, L0_xattn_W_l, L0_xattn_b_l)
    x = x + _L0_attn_ref(_layernorm(x, axis=-1), L0_attn_Wqkv_w, L0_attn_Wqkv_b, L0_attn_conv_w, L0_attn_conv_b, L0_attn_out_w, L0_attn_out_b)
    x = x + _L0_ffn_ref(_layernorm(x, axis=-1), L0_ffn_gate_w, L0_ffn_w1, L0_ffn_b1, L0_ffn_w2, L0_ffn_b2)
    return x

_drawn_inputs = setup_inputs


def setup_inputs(seed=0):
    import zlib

    import numpy as np

    out = dict(_drawn_inputs(seed))
    spreads = {'L0_attn_Wqkv_b': (0.0, 0.1),
     'L0_attn_conv_b': (0.0, 2.0),
     'L0_attn_out_b': (0.0, 0.1),
     'L0_ffn_b1': (0.0, 0.372),
     'L0_ffn_b2': (0.0, 0.1)}
    factors = {'L0_attn_conv_w': 6.044}
    for name, (base, spread) in spreads.items():
        noise = np.random.default_rng([zlib.crc32(name.encode()), seed]).standard_normal(out[name].shape)
        drawn = base * np.exp(spread * noise) if base else spread * noise
        out[name] = jnp.asarray(drawn.astype(out[name].dtype))
    for name, factor in factors.items():
        out[name] = (out[name] * factor).astype(out[name].dtype)
    return out
```

```python
from contextlib import ExitStack

import concourse.bass as bass
from concourse import mybir

F32 = mybir.dt.float32
F32R = mybir.dt.float32r
I32 = mybir.dt.int32
U32 = mybir.dt.uint32
ALU = mybir.AluOpType
ACT = mybir.ActivationFunctionType
AX = mybir.AxisListType

P = 128
B, S = 8, 64
D = 512
Q = 512
KT = D // P
N = B * S
NT = N // P
H, DH = 16, 32
HR = P // DH
E, F = 14, 1024
FT = F // P
MAX_BLOCKS = E + (2 * N - 1) // P + 1
OVER = MAX_BLOCKS - E
EPS = 1e-5
MASKED = -1e30
CLIP = 100.0
CONSTS = 10
PARAMS = 12
Q2C = 300
SCALE = float(DH) ** -0.5


def perceiver_kernel(nc, t, out):
    ctx = ExitStack()
    with ctx:
        def sb(name, shape, dt=F32):
            return ctx.enter_context(nc.sbuf_tensor(name, shape, dt))

        def sem(name):
            return ctx.enter_context(nc.semaphore(name))

        h_dram = nc.dram_tensor("h_dram", [N, D], F32).ap()
        token_of_slot = nc.dram_tensor("token_of_slot", [MAX_BLOCKS * P, 1], I32).ap()
        y_dram = nc.dram_tensor("y_dram", [MAX_BLOCKS * P, D], F32).ap()

        ident = sb("ident", [P, P])
        ones = sb("ones", [P, P])
        before = sb("before", [P, P])
        expert_row_i = sb("expert_row_i", [P, E], I32); over_row_i = sb("over_row_i", [P, OVER], I32)
        causal = sb("causal", [P, S])
        eps = sb("eps", [P, 1])
        expert_row = sb("expert_row", [P, E])
        over_row = sb("over_row", [P, OVER])
        token_id = sb("token_id", [P, NT], I32)
        zeros_i = sb("zeros_i", [P, MAX_BLOCKS], I32)

        wcq = sb("wcq", [P, KT]); wq = sb("wq", [P, KT]); wc = sb("wc", [P, KT])
        scal = sb("scal", [P, 3]); bsum = sb("bsum", [P, 1])
        qkv_b = sb("qkv_b", [P, 3 * KT]); conv_b = sb("conv_b", [P, KT])
        gate = sb("gate", [P, KT, E])
        bl_row = sb("bl_row", [P, D]); ob_row = sb("ob_row", [P, D])
        b2_sb = sb("b2_sb", [E, D])

        x_res = sb("x_res", [P, NT, D])
        cn = sb("cn", [P, NT, D])
        cT = sb("cT", [P, KT, N])
        w1 = sb("w1", [P, 2, KT * F])
        w2 = sb("w2", [P, 2, FT * D])
        wl = w2[:, :, :].rearrange("p a (k n) -> p (a k) n", n=D)
        w1_tiles = w1[:, :, :].rearrange("p a (k n) -> p (a k) n", n=D)
        conv = w1_tiles[:, 0:3 * KT, :]
        wo = w1_tiles[:, 3 * KT:4 * KT, :]
        wqkv = sb("wqkv", [P, KT, 3 * D])

        A1 = sb("A1", [P, 2 * 2 * KT * Q])
        ctxT = A1[:, 0:2 * KT * Q].rearrange("p (j k q) -> p j k q", j=2, k=KT)
        ctxN = A1[:, 2 * KT * Q:].rearrange("p (j k d) -> p j k d", j=2, k=KT)
        qT = A1[:, 0:2048].rearrange("p (k n) -> p k n", k=KT)
        kT = A1[:, 2048:4096].rearrange("p (k n) -> p k n", k=KT)
        vN = A1[:, 4096:6144].rearrange("p (t n) -> p t n", t=NT)
        vX = A1[:, 6144:8192].rearrange("p (t n) -> p t n", t=NT)
        got = A1[:, 0:2 * NT * D].rearrange("p (t c d) -> p t c d", t=NT, c=2)
        A2 = sb("A2", [P, 3 * KT * N + KT * B * (S + 2)])
        cwT = A2[:, 0:2048].rearrange("p (k n) -> p k n", k=KT)
        c2qT = A2[:, 2048:4096].rearrange("p (k n) -> p k n", k=KT)
        ccT = A2[:, 4096:6144].rearrange("p (k n) -> p k n", k=KT)
        cqT = A2[:, 6144:8192].rearrange("p (k n) -> p k n", k=KT)
        oT = A2[:, 6144:].rearrange("p (k b s) -> p k b s", k=KT, b=B)
        sco = A2[:, 0:2048].rearrange("p (u r k) -> p u r k", u=2, k=S)
        prb = A2[:, 2048:4096].rearrange("p (u r k) -> p u r k", u=2, k=S)
        prT = A2[:, 4096:6144].rearrange("p (u c n) -> p u c n", u=2, n=P)
        xg = A2[:, 0:1024].rearrange("p (u d) -> p u d", u=2)
        xgT = A2[:, 1024:2048].rearrange("p (u k n) -> p u k n", u=2, k=KT)
        hpre = A2[:, 2048:3072]
        hT = A2[:, 3072:5120].rearrange("p (u f n) -> p u f n", u=2, f=FT)
        ysb = A2[:, 5120:6144].rearrange("p (u d) -> p u d", u=2)
        zero_rows = A2[:, 6144:6144 + D]
        base = A2[:, 6144:8192].rearrange("p (t d) -> p t d", t=NT)
        att = sb("att", [P, Q]); attT = sb("attT", [P, KT, P]); c2q = sb("c2q", [P, D])

        st = sb("st", [P, NT, 6]); mv = sb("mv", [P, NT, 2])
        sd = sb("sd", [P, NT]); rstd = sb("rstd", [P, NT])
        nmax = sb("nmax", [P, NT]); asum = sb("asum", [P, NT]); arec = sb("arec", [P, NT])
        msum = sb("msum", [P, NT])
        mT = sb("mT", [NT, 2, S]); mmax = sb("mmax", [NT, 2]); msb = sb("msb", [NT, 2])
        batt = sb("batt", [P, NT, 2]); q2cT = sb("q2cT", [P, KT, B])
        hmax = sb("hmax", [P, H]); hsum = sb("hsum", [P, 2, H]); hrec = sb("hrec", [P, 2, H])
        lg = sb("lg", [P, NT, E]); lmax = sb("lmax", [P, NT]); lsum = sb("lsum", [P, NT])
        top = sb("top", [P, NT, 8]); topi = sb("topi", [P, NT, 8], U32); topf = sb("topf", [P, NT, 2])
        wsum = sb("wsum", [P, NT]); wk = sb("wk", [P, NT, 2])
        oh = sb("oh", [P, 2, NT, E]); sel = sb("sel", [P, NT, E]); wsel = sb("wsel", [P, NT, E])
        wtmp = sb("wtmp", [P, NT, E]); wselT = sb("wselT", [E, NT, P])
        pos = sb("pos", [P, NT, E]); cnt = sb("cnt", [P, E]); nb = sb("nb", [P, E])
        nbt = sb("nbt", [P, E]); incl = sb("incl", [P, E]); start_over = sb("start_over", [P, E])
        far = sb("far", [P, NT, E]); slot = sb("slot", [P, NT, E]); near = sb("near", [P, E])
        slot_k = sb("slot_k", [P, 2, NT]); slot_i = sb("slot_i", [P, 2, NT], I32)
        bm1 = sb("bm1", [P, OVER, E]); bm2 = sb("bm2", [P, OVER, E])
        blk_f = sb("blk_f", [P, MAX_BLOCKS]); blk_i = sb("blk_i", [P, MAX_BLOCKS], I32)
        np_f = sb("np_f", [P, 4]); np_s = sb("np_s", [P, 2]); pairs_i = sb("pairs_i", [P, 2], I32)
        b1_sb = sb("b1_sb", [P, 2, FT]); tok_sb = sb("tok_sb", [P, 2], I32)

        pb = [ctx.enter_context(nc.psum_tensor(f"bank{i}", [P, 512], F32)) for i in range(8)]
        Z = pb[0:4]
        SC, TR, CQ, MI = pb[4:8]
        PT, PO = pb[4:6], pb[6:8]
        HP, HT, XT, YP = (pb[0:2], pb[2:4]), pb[4:6], pb[6], pb[7]

        x_in, wqkv_in, conv_in, wo_in, params_in = map(sem, ("x_in", "wqkv_in", "conv_in", "wo_in", "params_in"))
        ctxT_in, ctxN_in = sem("ctxT_in"), sem("ctxN_in")
        wl_in = [sem(f"wl_in{i}") for i in range(4)]
        w1_in, w2_in, b1_in = ([sem(f"{w}_in{u}") for u in range(2)] for w in ("w1", "w2", "b1"))
        consts, pool_step = sem("consts"), sem("pool_step")
        dve_step, act_step = sem("dve_step"), sem("act_step")
        var_ready, root_ready, normed = sem("var_ready"), sem("root_ready"), sem("normed")
        cT_psum, cT_ready, cw_ready = sem("cT_psum"), sem("cT_ready"), sem("cw_ready")
        s_psum, nmax_ready, exp_done, r_psum = map(sem, ("s_psum", "nmax_ready", "exp_done", "r_psum"))
        aT_psum, aT_ready, cq_psum, c2q_ready = map(sem, ("aT_psum", "aT_ready", "cq_psum", "c2q_ready"))
        c2qT_psum, c2qT_ready, cc_ready = map(sem, ("c2qT_psum", "c2qT_ready", "cc_ready"))
        m_ready, mT_psum, msub_ready, mexp_done = map(sem, ("m_ready", "mT_psum", "msub_ready", "mexp_done"))
        mn_ready, mn_psum, batt_ready, q2c_psum = map(sem, ("mn_ready", "mn_psum", "batt_ready", "q2c_psum"))
        cqT_ready, z_psum, pads_ready = sem("cqT_ready"), sem("z_psum"), sem("pads_ready")
        qk_psum, qk_ready, v_psum, v_ready, vx_in = map(sem, ("qk_psum", "qk_ready", "v_psum", "v_ready", "vx_in"))
        sc_psum, sc_ready, sub_ready, pexp_done = map(sem, ("sc_psum", "sc_ready", "sub_ready", "pexp_done"))
        hrec_ready, pr_ready, pT_psum, pT_ready = map(sem, ("hrec_ready", "pr_ready", "pT_psum", "pT_ready"))
        o_psum, o_ready, q2_psum, q2_ready, out_psum = map(sem, ("o_psum", "o_ready", "q2_psum", "q2_ready", "out_psum"))
        h_stored, lg_psum, lsub_ready, lexp_done = map(sem, ("h_stored", "lg_psum", "lsub_ready", "lexp_done"))
        sel_ready, count_psum, wsel_ready, wselT_psum = map(sem, ("sel_ready", "count_psum", "wsel_ready", "wselT_psum"))
        b2_psum, base_ready = sem("b2_psum"), sem("base_ready")
        slots_ready, blocks_ready, zeroed, scattered = map(sem, ("slots_ready", "blocks_ready", "zeroed", "scattered"))
        zero_made, y_zeroed = sem("zero_made"), sem("y_zeroed")
        tok_in, tok_turn = sem("tok_in"), sem("tok_turn")
        x_gathered = [sem(f"x_gathered{u}") for u in range(2)]
        xT_psum, xT_ready, h_psum, hpre_ready = map(sem, ("xT_psum", "xT_ready", "h_psum", "hpre_ready"))
        hT_psum, gelu_done, y_psum = map(sem, ("hT_psum", "gelu_done", "y_psum"))
        y_taken = sem("y_taken")
        y_free = [sem(f"y_free{u}") for u in range(2)]
        y_gathered = [sem(f"y_gathered{n}") for n in range(NT)]
        final_ready, out_stored = sem("final_ready"), sem("out_stored")

        block = ctx.enter_context(nc.Block())

        def tile(n):
            return slice(n * P, (n + 1) * P)

        def pair_count(eng):
            eng.wait_ge(blocks_ready, 1)
            return eng.value_load(pairs_i[0:1, 0:1], min_val=E // 2, max_val=MAX_BLOCKS // 2)

        def expert_of(eng, b):
            return eng.value_load(blk_i[0:1, bass.ds(b, 1)], min_val=0, max_val=E - 1)

        @block.sync
        def _(sp):
            sp.dma_start(x_res[:, :, :], t["x"].rearrange("(t p) d -> p t d", p=P)).then_inc(x_in, 16)

            def load_ctxT(n):
                if n:
                    sp.wait_ge(s_psum, n)
                for j in range(2):
                    sp.dma_start(ctxT[:, j], t["ctxT"][2 * n + j].rearrange("(k p) q -> p k q", p=P)) \
                        .then_inc(ctxT_in, 16)

            def load_ctxN(n):
                if n:
                    sp.wait_ge(cq_psum, n)
                for j in range(2):
                    sp.dma_start(ctxN[:, j], t["ctx"][2 * n + j].rearrange("(k p) d -> p k d", p=P)) \
                        .then_inc(ctxN_in, 16)

            def load_wl(part):
                sp.dma_start(wl[:, KT * part:KT * (part + 1), :],
                             t["wlT"][D * part:D * (part + 1), :].rearrange("(k p) n -> p k n", p=P)) \
                    .then_inc(wl_in[part], 16)

            load_ctxT(0)
            load_wl(0)
            load_ctxN(0)
            load_ctxT(1)
            load_wl(1)
            load_wl(2)
            load_ctxN(1)
            load_ctxT(2)
            load_wl(3)
            load_ctxN(2)
            load_ctxT(3)
            sp.dma_start(wqkv[:, :, :], t["wqkvT"].rearrange("(k p) n -> p k n", p=P)).then_inc(wqkv_in, 16)
            load_ctxN(3)
            sp.dma_start(conv, t["convT"].rearrange("(k p) n -> p k n", p=P)).then_inc(conv_in, 16)
            sp.dma_start(wo, t["woT"].rearrange("(k p) n -> p k n", p=P)).then_inc(wo_in, 16)
            sp.wait_ge(z_psum, NT)
            for u in range(2):
                sp.dma_start(w2[:, u, :].rearrange("p (k f) -> p k f", k=FT),
                             t["w2"][u].rearrange("(k p) f -> p k f", p=P)).then_inc(w2_in[u], 16)
            sp.wait_ge(v_ready, NT)
            for j in range(2):
                sp.dma_start(vX[S * (1 - j):S * (2 - j)], vN[S * j:S * (j + 1)]).then_inc(vx_in, 16)
            sp.wait_ge(out_psum, NT)
            for u in range(2):
                sp.dma_start(w1[:, u, :].rearrange("p (k f) -> p k f", k=KT),
                             t["w1"][u].rearrange("(k p) f -> p k f", p=P)).then_inc(w1_in[u], 16)
                sp.dma_start(b1_sb[:, u, :], t["b1T"][u]).then_inc(b1_in[u], 16)
            pairs = pair_count(sp)
            with sp.Fori(1, pairs) as i:
                for u in range(2):
                    e = expert_of(sp, 2 * i + u)
                    sp.wait_ge(h_psum, 2 * i + u - 1)
                    sp.dma_start(w1[:, u, :].rearrange("p (k f) -> p k f", k=KT),
                                 t["w1"][bass.ds(e, 1)].rearrange("o (k p) f -> p (o k) f", p=P)) \
                        .then_inc(w1_in[u], 16)
            for n in range(NT):
                sp.wait_ge(final_ready, n + 1)
                sp.dma_start(out[tile(n), :], got[:, n, 0, :]).then_inc(out_stored, 16)
            sp.wait_ge(out_stored, 16 * NT)

        @block.scalar
        def _(act):
            for dst, src in ((wcq, "wcqT"), (wq, "wqT"), (wc, "wcT"), (qkv_b, "qkv_bT"), (conv_b, "conv_bT")):
                act.dma_start(dst[:, :], t[src]).then_inc(params_in, 16)
            for i, name in enumerate(("b_cq", "b_c", "b_q")):
                act.dma_start(scal[:, i:i + 1], t[name].to_broadcast([P, 1])).then_inc(params_in, 16)
            act.dma_start(bl_row[:, :], t["b_l"].to_broadcast([P, D])).then_inc(params_in, 16)
            act.dma_start(ob_row[:, :], t["out_b"].to_broadcast([P, D])).then_inc(params_in, 16)
            act.dma_start(gate[:, :, :], t["gateT"].rearrange("(k p) e -> p k e", p=P)).then_inc(params_in, 16)
            act.dma_start(b2_sb[:, :], t["b2"]).then_inc(params_in, 16)

            def roots(l):
                if l == 0:
                    act.wait_ge(consts, CONSTS)
                act.wait_ge(var_ready, NT * (l + 1))
                nc.scalar.activation(sd[:, :], mv[:, :, 1], ACT.Sqrt, bias=eps[:, 0:1]).then_inc(root_ready, 1)

            def copy_cT(l, n):
                act.wait_ge(cT_psum, NT * l + n + 1)
                nc.scalar.activation(cT[:, :, tile(n)], (TR if n % 2 == 0 else MI)[:, :].rearrange(
                    "p (k n) -> p k n", k=KT), ACT.Copy).then_inc(cT_ready, 1)

            roots(0)
            for n in range(NT):
                copy_cT(0, n)
            for n in range(NT):
                act.wait_ge(nmax_ready, n + 1)
                if n:
                    act.wait_ge(aT_psum, n)
                nc.scalar.activation(att[:, :], SC[:, :], ACT.Exp, bias=nmax[:, n:n + 1],
                                     accum_out=asum[:, n:n + 1]).then_inc(exp_done, 1)
                act.wait_ge(aT_psum, n + 1)
                if n:
                    act.wait_ge(cq_psum, n)
                nc.scalar.activation(attT[:, :, :], TR[:, :].rearrange("p (k n) -> p k n", k=KT),
                                     ACT.Copy).then_inc(aT_ready, 1)
                act.wait_ge(c2qT_psum, n + 1)
                nc.scalar.activation(c2qT[:, :, tile(n)], TR[:, :].rearrange("p (k n) -> p k n", k=KT),
                                     ACT.Copy).then_inc(c2qT_ready, 1)
            act.wait_ge(msub_ready, 1)
            nc.scalar.activation(mT[:, :, :], mT[:, :, :], ACT.Exp).then_inc(mexp_done, 1)

            roots(1)
            for n in range(NT):
                copy_cT(1, n)
            for f in range(2 * KT):
                act.wait_ge(qk_psum, f + 1)
                nc.scalar.activation((qT if f < KT else kT)[:, f % KT, :], pb[f % 4][:, :], ACT.Identity,
                                     bias=qkv_b[:, f:f + 1]).then_inc(qk_ready, 1)
            for n in range(NT):
                act.wait_ge(v_psum, n + 1)
                nc.scalar.activation(vN[:, n, :], pb[n][:, :], ACT.Copy).then_inc(v_ready, 1)

            def attention(a):
                for n in range(NT):
                    m = NT * a + n
                    act.wait_ge(sub_ready, m + 1)
                    if m >= 2:
                        act.wait_ge(pr_ready, m - 1)
                    nc.scalar.activation(prb[:, m % 2], sco[:, m % 2], ACT.Exp, scale=SCALE) \
                        .then_inc(pexp_done, 1)
                    act.wait_ge(pT_psum, m + 1)
                    if m >= 2:
                        act.wait_ge(o_psum, m - 1)
                    for i in range(2):
                        nc.scalar.activation(prT[:, m % 2, 4 * i:4 * i + 4, :],
                                             PT[i][:, :].rearrange("p (c n) -> p c n", n=P),
                                             ACT.Copy).then_inc(pT_ready, 1)

            attention(0)
            for f in range(KT):
                act.wait_ge(q2_psum, f + 1)
                nc.scalar.activation(qT[:, f, :], pb[f][:, :], ACT.Identity, bias=conv_b[:, f:f + 1]) \
                    .then_inc(q2_ready, 1)
            attention(1)

            roots(2)
            for n in range(NT):
                copy_cT(2, n)
            act.wait_ge(lsub_ready, 1)
            nc.scalar.activation(lg[:, :, :], lg[:, :, :], ACT.Exp).then_inc(lexp_done, 1)

            def gelu(b, u, loaded):
                act.wait_ge(hT_psum, b + 1)
                for f in range(FT):
                    if f == 0:
                        act.wait_ge(b1_in[u], loaded)
                    ins = nc.scalar.activation(hT[:, u, f, :], HT[f // 4][:, tile(f % 4)], ACT.Gelu,
                                               bias=b1_sb[:, u, f:f + 1])
                ins.then_inc(gelu_done, 1)

            def store_y(b, u):
                act.wait_ge(y_taken, b + 2)
                act.dma_start(y_dram.rearrange("(b p) d -> b p d", p=P)[bass.ds(b, 1)]
                              .rearrange("o p d -> p (o d)"), ysb[:, u, :]).then_inc(y_free[u], 16)

            pairs = pair_count(act)
            gelu(0, 0, 16)
            with act.Fori(1, pairs) as i:
                for u in range(2):
                    if u == 0:
                        gelu(2 * i - 1, 1, 16 * i)
                    else:
                        gelu(2 * i, 0, 16 * i + 16)
                    store_y(2 * i - 2 + u, u)
                    e = expert_of(act, 2 * i + u)
                    act.dma_start(w2[:, u, :].rearrange("p (k f) -> p k f", k=FT),
                                  t["w2"][bass.ds(e, 1)].rearrange("o (k p) f -> p (o k) f", p=P)) \
                        .then_inc(w2_in[u], 16)
                    act.wait_ge(gelu_done, 2 * i + u - 1)
                    act.dma_start(b1_sb[:, u, :], t["b1T"][bass.ds(e, 1)].rearrange("o p f -> p (o f)")) \
                        .then_inc(b1_in[u], 16)
            last = act.value_load(pairs_i[0:1, 1:2], min_val=E // 2 - 1, max_val=MAX_BLOCKS // 2 - 1)
            gelu(2 * last + 1, 1, 16 * last + 16)
            store_y(2 * last, 0)
            store_y(2 * last + 1, 1)

        @block.gpsimd
        def _(pool):
            nc.gpsimd.memset(ident[:, :], 0.0).then_inc(pool_step, 1)
            nc.gpsimd.memset(before[:, :], 1.0).then_inc(pool_step, 1)
            nc.gpsimd.memset(causal[:, :], 0.0).then_inc(pool_step, 1)
            nc.gpsimd.memset(zeros_i[:, :], 0).then_inc(pool_step, 1)
            pool.wait_ge(pool_step, 4)
            nc.gpsimd.affine_select(out=ident[:, :], in_=ident[:, :], pattern=[[-1, P]], compare_op=ALU.not_equal,
                                    fill=1.0, base=0, channel_multiplier=1).then_inc(consts, 1)
            pool.wait_ge(consts, 1)
            nc.gpsimd.affine_select(out=before[:, :], in_=before[:, :], pattern=[[1, P]], compare_op=ALU.is_gt,
                                    fill=0.0, base=0, channel_multiplier=-1).then_inc(consts, 1)
            for j in range(2):
                pool.wait_ge(consts, 2 + j)
                v = causal[S * j:S * (j + 1), :]
                nc.gpsimd.affine_select(out=v, in_=v, pattern=[[-1, S]], compare_op=ALU.is_ge, fill=MASKED,
                                        base=0, channel_multiplier=1).then_inc(consts, 1)
            pool.wait_ge(consts, 4)
            nc.gpsimd.memset(ones[:, :], 1.0).then_inc(consts, 1)
            nc.gpsimd.memset(eps[:, :], EPS).then_inc(consts, 1)
            nc.gpsimd.memset(batt[:, :, :], 0.0).then_inc(consts, 1)
            nc.gpsimd.iota(token_id[:, :], pattern=[[P, NT]], base=0, channel_multiplier=1).then_inc(consts, 1)
            nc.gpsimd.iota(expert_row_i[:, :], pattern=[[1, E]], base=0, channel_multiplier=0).then_inc(consts, 1)
            pool.wait_ge(consts, CONSTS - 1)
            nc.gpsimd.iota(over_row_i[:, :], pattern=[[1, OVER]], base=0, channel_multiplier=0).then_inc(consts, 1)
            pool.wait_ge(consts, 5)
            nc.gpsimd.memset(zero_rows, 0.0).then_inc(zero_made, 1)
            pool.wait_ge(zero_made, 1)
            for b in range(E, MAX_BLOCKS):
                pool.dma_start(y_dram[b * P:(b + 1) * P, :], zero_rows).then_inc(y_zeroed, 16)
            pool.dma_start(token_of_slot.rearrange("(p b) o -> p (b o)", p=P), zeros_i[:, :]).then_inc(zeroed, 16)

            def norm_probabilities(m):
                pool.wait_ge(hrec_ready, m + 1)
                nc.gpsimd.tensor_tensor(prb[:, m % 2], prb[:, m % 2],
                                        hrec[:, m % 2, :].unsqueeze(2).to_broadcast([P, H, S]),
                                        ALU.mult).then_inc(pr_ready, 1)

            pool.wait_ge(z_psum, NT)
            for side in (0, S + 1):
                nc.gpsimd.memset(oT[:, :, :, side:side + 1], 0.0).then_inc(pads_ready, 1)
            for m in range(2 * NT):
                norm_probabilities(m)

            pool.wait_ge(normed, 3 * NT)
            pool.dma_start(h_dram.rearrange("(t p) d -> p t d", p=P), cn[:, :, :]).then_inc(h_stored, 16)
            pool.wait_ge(slots_ready, 1)
            pool.wait_ge(zeroed, 16)
            for c in range(2):
                for n in range(NT):
                    pool.indirect_dma_start(token_of_slot, bass.IndirectOffsetOnAxis(ap=slot_i[:, c, n:n + 1], axis=0),
                                            token_id[:, n:n + 1], None).then_inc(scattered, 16)
            for u in range(2):
                nc.gpsimd.memset(ysb[:, u, :], 0.0).then_inc(y_free[u], 16)
            pairs = pair_count(pool)

            def gather_x(b, u):
                pool.dma_start(tok_sb[:, u:u + 1], token_of_slot.rearrange("(b p) o -> b p o", p=P)[
                    b if isinstance(b, int) else bass.ds(b, 1)].rearrange(
                    "p o -> p o" if isinstance(b, int) else "a p o -> p (a o)")).then_inc(tok_in, 16)
                pool.wait_ge(tok_in, 16 * b + 16)
                pool.sem_inc(tok_turn, 1)
                pool.indirect_dma_start(xg[:, u, :], None, h_dram,
                                        bass.IndirectOffsetOnAxis(ap=tok_sb[:, u:u + 1], axis=0)) \
                    .then_inc(x_gathered[u], 16)

            pool.wait_ge(scattered, 16 * 2 * NT)
            pool.wait_ge(h_stored, 16)
            for u in range(2):
                gather_x(u, u)
            with pool.Fori(1, pairs) as i:
                for u in range(2):
                    pool.wait_ge(xT_psum, 2 * i + u - 1)
                    pool.sem_inc(tok_turn, 1)
                    gather_x(2 * i + u, u)
            for u in range(2):
                pool.wait_ge(y_free[u], 16 * pairs + 16)
                pool.sem_inc(tok_turn, 1)
            for n in range(NT):
                for c in range(2):
                    pool.indirect_dma_start(got[:, n, c, :], None, y_dram,
                                            bass.IndirectOffsetOnAxis(ap=slot_i[:, c, n:n + 1], axis=0)) \
                        .then_inc(y_gathered[n], 16)

        @block.vector
        def _(dve):
            step = [0]

            def link(ins):
                step[0] += 1
                ins.then_inc(dve_step, 1)
                dve.wait_ge(dve_step, step[0])

            def norm(l, ready):
                for n in range(NT):
                    ready(n)
                    link(nc.vector.bn_stats(st[:, n, :], x_res[:, n, :]))
                    nc.vector.bn_aggr(mv[:, n, :], st[:, n, :]).then_inc(var_ready, 1)
                dve.wait_ge(root_ready, l + 1)
                link(nc.vector.reciprocal(rstd[:, :], sd[:, :]))
                for n in range(NT):
                    nc.vector.tensor_scalar(cn[:, n, :], x_res[:, n, :], mv[:, n, 0:1], rstd[:, n:n + 1],
                                            ALU.subtract, ALU.mult).then_inc(normed, 1)

            dve.wait_ge(x_in, 16)
            norm(0, lambda n: None)
            dve.wait_ge(params_in, 16 * PARAMS)
            dve.wait_ge(consts, CONSTS)
            link(nc.vector.tensor_copy(expert_row[:, :], expert_row_i[:, :]))
            link(nc.vector.tensor_copy(over_row[:, :], over_row_i[:, :]))
            link(nc.vector.tensor_reduce(bsum[:, :], scal[:, :], AX.X, ALU.add))
            for n in range(NT):
                dve.wait_ge(cT_ready, n + 1)
                for k in range(KT):
                    nc.vector.tensor_scalar(cwT[:, k, tile(n)], cT[:, k, tile(n)], wcq[:, k:k + 1], wq[:, k:k + 1],
                                            ALU.mult, ALU.add).then_inc(cw_ready, 1)
            for n in range(NT):
                dve.wait_ge(normed, NT)
                nc.vector.tensor_tensor(x_res[:, n, :], x_res[:, n, :], bl_row[:, :], ALU.add).then_inc(dve_step, 1)
                step[0] += 1
                dve.wait_ge(s_psum, n + 1)
                nc.vector.tensor_reduce(nmax[:, n:n + 1], SC[:, :], AX.X, ALU.max, negate=True) \
                    .then_inc(nmax_ready, 1)
                dve.wait_ge(exp_done, n + 1)
                link(nc.vector.reciprocal(arec[:, n:n + 1], asum[:, n:n + 1]))
                dve.wait_ge(cq_psum, n + 1)
                if n:
                    dve.wait_ge(c2qT_psum, n)
                nc.vector.tensor_scalar(c2q[:, :], CQ[:, :], arec[:, n:n + 1], None, ALU.mult) \
                    .then_inc(c2q_ready, 1)
                dve.wait_ge(c2qT_ready, n + 1)
                nc.vector.tensor_tensor(ccT[:, :, tile(n)], c2qT[:, :, tile(n)], cT[:, :, tile(n)],
                                        ALU.mult).then_inc(cc_ready, 1)
            dve.wait_ge(r_psum, NT)
            link(nc.vector.scalar_tensor_tensor(msum[:, :], nmax[:, :], -1.0, MI[:, 0:NT], ALU.mult, ALU.add))
            nc.vector.tensor_scalar(msum[:, :], msum[:, :], bsum[:, 0:1], None, ALU.add).then_inc(m_ready, 1)
            dve.wait_ge(mT_psum, 1)
            link(nc.vector.tensor_copy(mT[:, :, :], MI[0:NT, P:2 * P].rearrange("p (j s) -> p j s", j=2)))
            link(nc.vector.tensor_reduce(mmax[:, :], mT[:, :, :], AX.X, ALU.max))
            nc.vector.tensor_tensor(mT[:, :, :], mT[:, :, :], mmax[:, :].unsqueeze(2).to_broadcast([NT, 2, S]),
                                    ALU.subtract).then_inc(msub_ready, 1)
            dve.wait_ge(mexp_done, 1)
            link(nc.vector.tensor_reduce(msb[:, :], mT[:, :, :], AX.X, ALU.add))
            link(nc.vector.reciprocal(msb[:, :], msb[:, :]))
            nc.vector.tensor_tensor(mT[:, :, :], mT[:, :, :], msb[:, :].unsqueeze(2).to_broadcast([NT, 2, S]),
                                    ALU.mult).then_inc(mn_ready, 1)
            dve.wait_ge(mn_psum, 1)
            for j in range(2):
                nc.vector.tensor_copy(batt[S * j:S * (j + 1), :, j], MI[S * j:S * (j + 1), 2 * P:2 * P + NT]) \
                    .then_inc(batt_ready, 1)
            dve.wait_ge(q2c_psum, 1)
            dve.wait_ge(y_zeroed, 16 * OVER)
            link(nc.vector.tensor_copy(q2cT[:, :, :], MI[:, Q2C:Q2C + KT * B].rearrange("p (k b) -> p k b", k=KT)))
            nc.vector.tensor_tensor(cqT.rearrange("p k (b s) -> p (k b) s", s=S),
                                    cT[:, :, :].rearrange("p k (b s) -> p (k b) s", s=S),
                                    q2cT[:, :, :].rearrange("p k b -> p (k b)").unsqueeze(2)
                                    .to_broadcast([P, KT * B, S]), ALU.mult).then_inc(cqT_ready, 1)

            def add_z(n):
                dve.wait_ge(z_psum, n + 1)
                link(nc.vector.tensor_tensor(x_res[:, n, :], Z[n][:, :], x_res[:, n, :], ALU.add))

            norm(1, add_z)
            dve.wait_ge(normed, 2 * NT)
            for n in range(NT):
                link(nc.vector.tensor_tensor(x_res[:, n, :], x_res[:, n, :], ob_row[:, :], ALU.add))

            def attention(a):
                def softmax(n):
                    m = NT * a + n
                    u = m % 2
                    dve.wait_ge(sc_psum, m + 1)
                    if m >= 2:
                        dve.wait_ge(pexp_done, m - 1)
                    for r in range(HR):
                        ins = nc.vector.tensor_tensor(
                            sco[:, u, KT * r:KT * (r + 1), :],
                            pb[r][:, 0:KT * S].rearrange("p (c k) -> p c k", k=S),
                            causal[:, :].unsqueeze(1).to_broadcast([P, KT, S]), ALU.add)
                        ins.then_inc(sc_ready, 1)
                    dve.wait_ge(sc_ready, HR * (m + 1))
                    link(nc.vector.tensor_reduce(hmax[:, :], sco[:, u], AX.X, ALU.max))
                    nc.vector.tensor_tensor(sco[:, u], sco[:, u], hmax[:, :].unsqueeze(2).to_broadcast([P, H, S]),
                                            ALU.subtract).then_inc(sub_ready, 1)

                def sums(n):
                    m = NT * a + n
                    dve.wait_ge(pexp_done, m + 1)
                    if m >= 2:
                        dve.wait_ge(pr_ready, m - 1)
                    link(nc.vector.tensor_reduce(hsum[:, m % 2, :], prb[:, m % 2], AX.X, ALU.add))
                    nc.vector.reciprocal(hrec[:, m % 2, :], hsum[:, m % 2, :]).then_inc(hrec_ready, 1)

                def take_out(n):
                    m = NT * a + n
                    dve.wait_ge(o_psum, m + 1)
                    for c in range(KT):
                        src = PO[c % 2][:, (c // 2) * P:(c // 2 + 1) * P]
                        bias = qkv_b[:, 2 * KT + c:2 * KT + c + 1]
                        if a == 0:
                            nc.vector.tensor_scalar(oT[:, c, 2 * n:2 * n + 2, 1:S + 1],
                                                    src.rearrange("p (b s) -> p b s", b=2), bias, None,
                                                    ALU.add).then_inc(o_ready, 1)
                        else:
                            nc.vector.tensor_scalar(cT[:, c, tile(n)], src, bias, None,
                                                    ALU.add).then_inc(o_ready, 1)

                for n in range(NT + 1):
                    if n < NT:
                        softmax(n)
                    if n >= 1:
                        sums(n - 1)
                        if n >= 2:
                            take_out(n - 2)
                take_out(NT - 1)

            attention(0)
            dve.wait_ge(q2_psum, KT)
            attention(1)

            def add_out(n):
                dve.wait_ge(out_psum, n + 1)
                link(nc.vector.tensor_tensor(x_res[:, n, :], pb[n][:, :], x_res[:, n, :], ALU.add))

            norm(2, add_out)

            dve.wait_ge(lg_psum, 1)
            LG = pb[6][:, 0:NT * E].rearrange("p (t e) -> p t e", e=E)
            link(nc.vector.tensor_reduce(lmax[:, :], LG, AX.X, ALU.max))
            nc.vector.tensor_tensor(lg[:, :, :], LG, lmax[:, :].unsqueeze(2).to_broadcast([P, NT, E]),
                                    ALU.subtract).then_inc(lsub_ready, 1)
            dve.wait_ge(lexp_done, 1)
            link(nc.vector.tensor_reduce(lsum[:, :], lg[:, :, :], AX.X, ALU.add))
            link(nc.vector.reciprocal(lsum[:, :], lsum[:, :]))
            link(nc.vector.tensor_tensor(lg[:, :, :], lg[:, :, :], lsum[:, :].unsqueeze(2)
                                         .to_broadcast([P, NT, E]), ALU.mult))
            for n in range(NT):
                link(nc.vector.max(top[:, n, :], lg[:, n, :]))
                link(nc.vector.max_index(topi[:, n, :], top[:, n, :], lg[:, n, :]))
            link(nc.vector.tensor_copy(topf[:, :, :], topi[:, :, 0:2]))
            link(nc.vector.tensor_reduce(wsum[:, :], top[:, :, 0:2], AX.X, ALU.add))
            link(nc.vector.tensor_scalar(wsum[:, :], wsum[:, :], 1e-10, None, ALU.max))
            link(nc.vector.reciprocal(wsum[:, :], wsum[:, :]))
            link(nc.vector.tensor_tensor(wk[:, :, :], top[:, :, 0:2], wsum[:, :].unsqueeze(2)
                                         .to_broadcast([P, NT, 2]), ALU.mult))
            every = expert_row[:, :].unsqueeze(1).to_broadcast([P, NT, E])
            for c in range(2):
                link(nc.vector.tensor_tensor(oh[:, c], every, topf[:, :, c:c + 1].to_broadcast([P, NT, E]),
                                             ALU.is_equal))
            nc.vector.tensor_tensor(sel[:, :, :], oh[:, 0], oh[:, 1], ALU.add).then_inc(sel_ready, 1)
            link(nc.vector.tensor_tensor(wtmp[:, :, :], oh[:, 0], wk[:, :, 0:1].to_broadcast([P, NT, E]), ALU.mult))
            link(nc.vector.tensor_tensor(wsel[:, :, :], oh[:, 1], wk[:, :, 1:2].to_broadcast([P, NT, E]), ALU.mult))
            nc.vector.tensor_tensor(wsel[:, :, :], wsel[:, :, :], wtmp[:, :, :], ALU.add).then_inc(wsel_ready, 1)

            dve.wait_ge(count_psum, 1)
            link(nc.vector.tensor_copy(pos[:, :, :], pb[6][:, P:P + NT * E].rearrange("p (t e) -> p t e", e=E)))
            link(nc.vector.tensor_copy(cnt[:, :], pb[6][:, 2 * P:2 * P + E]))
            link(nc.vector.tensor_scalar(nb[:, :], cnt[:, :], float(P), None, ALU.is_gt))
            for c in range(2, NT):
                link(nc.vector.tensor_scalar(nbt[:, :], cnt[:, :], float(P * c), None, ALU.is_gt))
                link(nc.vector.tensor_tensor(nb[:, :], nb[:, :], nbt[:, :], ALU.add))
            link(nc.vector.tensor_tensor_scan(incl[:, :], ones[:, 0:E], nb[:, :], 0.0, ALU.mult, ALU.add))
            link(nc.vector.tensor_tensor(start_over[:, :], incl[:, :], nb[:, :], ALU.subtract))
            link(nc.vector.tensor_scalar(near[:, :], expert_row[:, :], float(P), None, ALU.mult))
            link(nc.vector.tensor_scalar(nbt[:, :], start_over[:, :], float(P), float(P * (E - 1)), ALU.mult, ALU.add))
            link(nc.vector.tensor_tensor(nbt[:, :], nbt[:, :], near[:, :], ALU.subtract))
            link(nc.vector.tensor_scalar(far[:, :, :], pos[:, :, :], float(P), None, ALU.is_ge))
            link(nc.vector.tensor_tensor(far[:, :, :], far[:, :, :], nbt[:, :].unsqueeze(1)
                                         .to_broadcast([P, NT, E]), ALU.mult))
            link(nc.vector.tensor_tensor(slot[:, :, :], pos[:, :, :], near[:, :].unsqueeze(1)
                                         .to_broadcast([P, NT, E]), ALU.add))
            link(nc.vector.tensor_tensor(slot[:, :, :], slot[:, :, :], far[:, :, :], ALU.add))
            for c in range(2):
                link(nc.vector.tensor_tensor(wtmp[:, :, :], oh[:, c], slot[:, :, :], ALU.mult))
                link(nc.vector.tensor_reduce(slot_k[:, c, :], wtmp[:, :, :], AX.X, ALU.add))
            nc.vector.tensor_copy(slot_i[:, :, :], slot_k[:, :, :]).then_inc(slots_ready, 1)
            js = over_row[:, :].unsqueeze(2).to_broadcast([P, OVER, E])
            link(nc.vector.tensor_tensor(bm1[:, :, :], js, start_over[:, :].unsqueeze(1)
                                         .to_broadcast([P, OVER, E]), ALU.is_ge))
            link(nc.vector.tensor_tensor(bm2[:, :, :], js, incl[:, :].unsqueeze(1)
                                         .to_broadcast([P, OVER, E]), ALU.is_lt))
            link(nc.vector.tensor_tensor(bm1[:, :, :], bm1[:, :, :], bm2[:, :, :], ALU.mult))
            link(nc.vector.tensor_tensor(bm1[:, :, :], bm1[:, :, :], expert_row[:, :].unsqueeze(1)
                                         .to_broadcast([P, OVER, E]), ALU.mult))
            link(nc.vector.tensor_copy(blk_f[:, 0:E], expert_row[:, :]))
            link(nc.vector.tensor_reduce(blk_f[:, E:MAX_BLOCKS], bm1[:, :, :], AX.X, ALU.add))
            link(nc.vector.tensor_copy(blk_i[:, :], blk_f[:, :]))
            for c in range(4):
                link(nc.vector.tensor_scalar(np_f[:, c:c + 1], incl[:, E - 1:E], 2.0 * c, None, ALU.is_gt))
            link(nc.vector.tensor_reduce(np_s[:, 0:1], np_f[:, :], AX.X, ALU.add))
            link(nc.vector.tensor_scalar(np_s[:, 1:2], np_s[:, 0:1], float(E // 2 - 1), None, ALU.add))
            link(nc.vector.tensor_scalar(np_s[:, 0:1], np_s[:, 0:1], float(E // 2), None, ALU.add))
            nc.vector.tensor_copy(pairs_i[:, :], np_s[:, :]).then_inc(blocks_ready, 1)
            dve.wait_ge(wselT_psum, 1)
            nc.vector.tensor_copy(wselT[:, :, :], pb[7][0:E, :].rearrange("e (t n) -> e t n", t=NT)) \
                .then_inc(y_taken, 1)
            for n in range(NT):
                dve.wait_ge(b2_psum, n + 1)
                nc.vector.tensor_tensor(base[:, n, :], pb[n][:, :], cn[:, n, :], ALU.add).then_inc(base_ready, 1)

            def take_xT(b, u):
                dve.wait_ge(xT_psum, b + 1)
                if not isinstance(b, int):
                    dve.wait_ge(h_psum, b - 1)
                nc.vector.tensor_copy(xgT[:, u], XT[:, :].rearrange("p (k n) -> p k n", k=KT)).then_inc(xT_ready, 1)

            def take_h(b, u):
                dve.wait_ge(h_psum, b + 1)
                if not isinstance(b, int) or b:
                    dve.wait_ge(hT_psum, b)
                for c in range(2):
                    nc.vector.tensor_copy(hpre[:, c * 512:(c + 1) * 512], HP[u][c][:, :]).then_inc(hpre_ready, 1)

            def take_y(b, u, turn):
                dve.wait_ge(y_psum, b + 1)
                dve.wait_ge(y_free[u], 16 * turn)
                nc.vector.tensor_copy(ysb[:, u, :], YP[:, :]).then_inc(y_taken, 1)

            pairs = pair_count(dve)
            take_xT(0, 0)
            take_h(0, 0)
            take_xT(1, 1)
            take_h(1, 1)
            with dve.Fori(1, pairs) as i:
                take_xT(2 * i, 0)
                take_h(2 * i, 0)
                take_xT(2 * i + 1, 1)
                take_y(2 * i - 2, 0, i)
                take_h(2 * i + 1, 1)
                take_y(2 * i - 1, 1, i)
            last = dve.value_load(pairs_i[0:1, 1:2], min_val=E // 2 - 1, max_val=MAX_BLOCKS // 2 - 1)
            for u in range(2):
                take_y(2 * last + u, u, last + 1)

            for n in range(NT):
                y0, y1 = got[:, n, 0, :], got[:, n, 1, :]
                dve.wait_ge(y_gathered[n], 32)
                link(nc.vector.tensor_scalar(y0, y0, wk[:, n, 0:1], None, ALU.mult))
                link(nc.vector.scalar_tensor_tensor(y0, y1, wk[:, n, 1:2], y0, ALU.mult, ALU.add))
                link(nc.vector.tensor_tensor(y0, y0, base[:, n, :], ALU.add))
                link(nc.vector.tensor_scalar(y0, y0, CLIP, -CLIP, ALU.min, ALU.max))
                nc.vector.tensor_tensor(y0, y0, x_res[:, n, :], ALU.add).then_inc(final_ready, 1)

        @block.tensor
        def _(pe):
            mm = nc.tensor.matmul

            def transposes(bank, src):
                for k in range(KT):
                    ins = nc.tensor.transpose(bank[:, tile(k)], src[:, tile(k)], ident[:, :])
                return ins

            def turn_normed(l):
                for n in range(NT):
                    pe.wait_ge(normed, NT * l + n + 1)
                    if n >= 2 or l:
                        pe.wait_ge(cT_ready, NT * l + n - 1 if n >= 2 else NT * l)
                    transposes(TR if n % 2 == 0 else MI, cn[:, n, :]).then_inc(cT_psum, 1)

            pe.wait_ge(consts, CONSTS)
            turn_normed(0)

            def scores(n):
                pe.wait_ge(cw_ready, KT * (n + 1))
                pe.wait_ge(ctxT_in, 32 * (n + 1))
                if n:
                    pe.wait_ge(exp_done, n)
                for k in range(KT):
                    for j in range(2):
                        ins = mm(SC[S * j:S * (j + 1), :], cwT[:, k, n * P + S * j:n * P + S * (j + 1)],
                                 ctxT[:, j, k, :], start=(k == 0), stop=(k == KT - 1))
                ins.then_inc(s_psum, 1)

            def project(n, part, src):
                if n == 0:
                    pe.wait_ge(wl_in[part], 16)
                for k in range(KT):
                    ins = mm(Z[n][:, :], src[:, k, tile(n)], wl[:, KT * part + k, :],
                             start=(part == 0 and k == 0), stop=(part == 3 and k == KT - 1))
                return ins

            def row_terms(n):
                if n == 0:
                    pe.wait_ge(cT_ready, NT)
                    pe.wait_ge(params_in, 16 * PARAMS)
                for k in range(KT):
                    ins = mm(MI[:, n:n + 1], cT[:, k, tile(n)], wc[:, k:k + 1], start=(k == 0), stop=(k == KT - 1))
                ins.then_inc(r_psum, 1)

            scores(0)
            project(0, 0, cT)
            row_terms(0)
            for n in range(NT):
                pe.wait_ge(exp_done, n + 1)
                if n:
                    pe.wait_ge(c2qT_ready, n)
                transposes(TR, att[:, :]).then_inc(aT_psum, 1)
                if n:
                    pe.wait_ge(cc_ready, n)
                    project(n - 1, 1, c2qT)
                    project(n - 1, 2, ccT)
                pe.wait_ge(aT_ready, n + 1)
                pe.wait_ge(ctxN_in, 32 * (n + 1))
                if n:
                    pe.wait_ge(c2q_ready, n)
                for k in range(KT):
                    for j in range(2):
                        ins = mm(CQ[S * j:S * (j + 1), :], attT[:, k, S * j:S * (j + 1)], ctxN[:, j, k, :],
                                 start=(k == 0), stop=(k == KT - 1))
                ins.then_inc(cq_psum, 1)
                if n + 1 < NT:
                    scores(n + 1)
                    project(n + 1, 0, cT)
                    row_terms(n + 1)
                pe.wait_ge(c2q_ready, n + 1)
                transposes(TR, c2q[:, :]).then_inc(c2qT_psum, 1)
            pe.wait_ge(m_ready, 1)
            nc.tensor.transpose(MI[0:NT, P:2 * P], msum[:, :], ident[:, :]).then_inc(mT_psum, 1)
            pe.wait_ge(cc_ready, NT)
            project(NT - 1, 1, c2qT)
            project(NT - 1, 2, ccT)
            pe.wait_ge(mn_ready, 1)
            nc.tensor.transpose(MI[:, 2 * P:2 * P + NT], mT[:, :, :].rearrange("n j s -> n (j s)"),
                                ident[0:NT, 0:NT]).then_inc(mn_psum, 1)
            pe.wait_ge(batt_ready, 2)
            for n in range(NT):
                for k in range(KT):
                    at = Q2C + k * B + 2 * n
                    ins = mm(MI[:, at:at + 2], cn[:, n, tile(k)], batt[:, n, :], start=True, stop=True)
            ins.then_inc(q2c_psum, 1)
            pe.wait_ge(cqT_ready, 1)
            for n in range(NT):
                project(n, 3, cqT).then_inc(z_psum, 1)

            turn_normed(1)
            pe.wait_ge(cT_ready, 2 * NT)
            pe.wait_ge(wqkv_in, 16)
            for f in range(2 * KT):
                if f >= KT:
                    pe.wait_ge(qk_ready, f - KT + 1)
                for k in range(KT):
                    ins = mm(pb[f % 4][:, :], wqkv[:, k, tile(f)], cT[:, k, :], start=(k == 0), stop=(k == KT - 1))
                ins.then_inc(qk_psum, 1)
            for n in range(NT):
                pe.wait_ge(qk_ready, KT + n + 1)
                for k in range(KT):
                    ins = mm(pb[n][:, :], cT[:, k, tile(n)], wqkv[:, k, 2 * D:3 * D], start=(k == 0), stop=(k == KT - 1))
                ins.then_inc(v_psum, 1)

            def attention(a):
                def scores(n):
                    m = NT * a + n
                    if m:
                        pe.wait_ge(sc_ready, HR * m)
                    for c in range(KT):
                        for r in range(HR):
                            for j in range(2):
                                rows = slice(DH * r, DH * (r + 1))
                                cols = slice(n * P + S * j, n * P + S * (j + 1))
                                ins = mm(pb[r][S * j:S * (j + 1), S * c:S * (c + 1)], qT[rows, c, cols],
                                         kT[rows, c, cols], start=True, stop=True)
                    ins.then_inc(sc_psum, 1)

                def values(n):
                    m = NT * a + n
                    u = m % 2
                    pe.wait_ge(pr_ready, m + 1)
                    if m:
                        pe.wait_ge(pT_ready, 2 * m)
                    for g in range(2 * HR):
                        ins = nc.tensor.transpose(PT[g // 4][:, tile(g % 4)],
                                                  prb[:, u, 2 * g:2 * g + 2, :].rearrange("p h k -> p (h k)"),
                                                  ident[:, :])
                    ins.then_inc(pT_psum, 1)

                def outputs(n):
                    m = NT * a + n
                    u = m % 2
                    pe.wait_ge(pT_ready, 2 * m + 2)
                    if m:
                        pe.wait_ge(o_ready, KT * m)
                    for r in range(HR):
                        for c in range(KT):
                            w = c % 2
                            h = HR * c + r
                            for j in range(2):
                                v = vN if w == j else vX
                                ins = mm(PO[w][DH * r:DH * (r + 1), (c // 2) * P + S * j:(c // 2) * P + S * (j + 1)],
                                         v[S * w:S * (w + 1), n, DH * h:DH * (h + 1)],
                                         prT[S * w:S * (w + 1), u, 2 * r + c // 2, S * j:S * (j + 1)],
                                         start=True, stop=True)
                    ins.then_inc(o_psum, 1)

                if a == 0:
                    pe.wait_ge(qk_ready, 2 * KT)
                    pe.wait_ge(v_ready, NT)
                scores(0)
                if a == 0:
                    pe.wait_ge(vx_in, 32)
                for n in range(NT):
                    if n + 1 < NT:
                        scores(n + 1)
                    values(n)
                    outputs(n)

            attention(0)
            pe.wait_ge(o_ready, KT * NT)
            pe.wait_ge(sc_ready, HR * NT)
            pe.wait_ge(conv_in, 16)
            pe.wait_ge(pads_ready, 2)
            for f in range(KT):
                for tap in range(3):
                    for k in range(KT):
                        ins = mm(pb[f][:, :].rearrange("p (b s) -> p b s", b=B), conv[:, KT * tap + k, tile(f)],
                                 oT[:, k, :, tap:tap + S], start=(tap == 0 and k == 0),
                                 stop=(tap == 2 and k == KT - 1))
                ins.then_inc(q2_psum, 1)
            pe.wait_ge(q2_ready, KT)
            attention(1)
            pe.wait_ge(o_ready, 2 * KT * NT)
            pe.wait_ge(sc_ready, 2 * HR * NT)
            pe.wait_ge(wo_in, 16)
            for n in range(NT):
                for k in range(KT):
                    ins = mm(pb[n][:, :], cT[:, k, tile(n)], wo[:, k, :],
                             start=(k == 0), stop=(k == KT - 1))
                ins.then_inc(out_psum, 1)

            turn_normed(2)
            pe.wait_ge(cT_ready, 3 * NT)
            for n in range(NT):
                for k in range(KT):
                    ins = mm(pb[6][:, n * E:(n + 1) * E], cT[:, k, tile(n)], gate[:, k, :],
                             start=(k == 0), stop=(k == KT - 1))
            ins.then_inc(lg_psum, 1)
            pe.wait_ge(sel_ready, 1)
            for n in range(NT + 1):
                at = P + n * E if n < NT else 2 * P
                for m in range(min(n + 1, NT)):
                    ins = mm(pb[6][:, at:at + E], (before if m == n else ones)[:, :], sel[:, m, :],
                             start=(m == 0), stop=(m == min(n, NT - 1)))
            ins.then_inc(count_psum, 1)
            pe.wait_ge(wsel_ready, 1)
            for n in range(NT):
                ins = nc.tensor.transpose(pb[7][0:E, tile(n)], wsel[:, n, :], ident[:, :])
            ins.then_inc(wselT_psum, 1)
            pe.wait_ge(y_taken, 1)
            for n in range(NT):
                mm(pb[n][:, :], wselT[:, n, :], b2_sb[:, :], start=True, stop=True).then_inc(b2_psum, 1)

            def turn_x(b, u, gathered):
                pe.wait_ge(x_gathered[u], gathered)
                if not isinstance(b, int) or b:
                    pe.wait_ge(xT_ready, b)
                transposes(XT, xg[:, u, :]).then_inc(xT_psum, 1)

            def hidden(b, u, loaded):
                pe.wait_ge(xT_ready, b + 1)
                pe.wait_ge(w1_in[u], loaded)
                if isinstance(b, int):
                    pe.wait_ge(base_ready, NT)
                else:
                    pe.wait_ge(hpre_ready, 2 * b - 2)
                for k in range(KT):
                    for c in range(2):
                        ins = mm(HP[u][c][:, :], xgT[:, u, k, :], w1[:, u, k * F + c * 512:k * F + (c + 1) * 512],
                                 start=(k == 0), stop=(k == KT - 1))
                ins.then_inc(h_psum, 1)

            def turn_hidden(b):
                pe.wait_ge(hpre_ready, 2 * b + 2)
                if not isinstance(b, int):
                    pe.wait_ge(gelu_done, b)
                for f in range(FT):
                    ins = nc.tensor.transpose(HT[f // 4][:, tile(f % 4)], hpre[:, tile(f)], ident[:, :])
                ins.then_inc(hT_psum, 1)

            def output(b, u, loaded):
                pe.wait_ge(gelu_done, b + 1)
                pe.wait_ge(w2_in[u], loaded)
                pe.wait_ge(y_taken, b + 1)
                for f in range(FT):
                    ins = mm(YP[:, :], hT[:, u, f, :], w2[:, u, f * D:(f + 1) * D], start=(f == 0), stop=(f == FT - 1))
                ins.then_inc(y_psum, 1)

            pairs = pair_count(pe)
            turn_x(0, 0, 16)
            hidden(0, 0, 16)
            turn_x(1, 1, 16)
            hidden(1, 1, 16)
            turn_hidden(0)
            with pe.Fori(1, pairs) as i:
                turn_x(2 * i, 0, 16 * i + 16)
                turn_hidden(2 * i - 1)
                hidden(2 * i, 0, 16 * i + 16)
                turn_x(2 * i + 1, 1, 16 * i + 16)
                output(2 * i - 2, 0, 16 * i)
                hidden(2 * i + 1, 1, 16 * i + 16)
                turn_hidden(2 * i)
                output(2 * i - 1, 1, 16 * i)
            last = pe.value_load(pairs_i[0:1, 1:2], min_val=E // 2 - 1, max_val=MAX_BLOCKS // 2 - 1)
            turn_hidden(2 * last + 1)
            output(2 * last, 0, 16 * last + 16)
            output(2 * last + 1, 1, 16 * last + 16)


_NAMES = ["x", "ctx", "ctxT", "wcqT", "wqT", "wcT", "b_cq", "b_c", "b_q", "wlT", "b_l", "wqkvT", "qkv_bT", "convT",
          "conv_bT", "woT", "out_b", "gateT", "w1", "b1T", "w2", "b2"]


def kernel(x, ctx_1024, L0_xattn_w_cq, L0_xattn_b_cq, L0_xattn_w_c, L0_xattn_b_c, L0_xattn_w_q, L0_xattn_b_q,
           L0_xattn_W_l, L0_xattn_b_l, L0_attn_Wqkv_w, L0_attn_Wqkv_b, L0_attn_conv_w, L0_attn_conv_b,
           L0_attn_out_w, L0_attn_out_b, L0_ffn_gate_w, L0_ffn_w1, L0_ffn_b1, L0_ffn_w2, L0_ffn_b2):
    import numpy as np
    import concourse.bacc as bacc
    from concourse.bass_utils import run_bass_kernel_spmd

    def by_feature(v):
        return np.ascontiguousarray(np.asarray(v).reshape(-1, P).T)

    laid = {
        "x": np.asarray(x).reshape(N, D),
        "ctx": ctx_1024,
        "ctxT": np.asarray(ctx_1024).transpose(0, 2, 1),
        "wcqT": by_feature(L0_xattn_w_cq), "wqT": by_feature(L0_xattn_w_q), "wcT": by_feature(L0_xattn_w_c),
        "b_cq": np.asarray(L0_xattn_b_cq).reshape(1, 1), "b_c": np.asarray(L0_xattn_b_c).reshape(1, 1),
        "b_q": np.asarray(L0_xattn_b_q).reshape(1, 1),
        "wlT": np.asarray(L0_xattn_W_l).T, "b_l": np.asarray(L0_xattn_b_l).reshape(1, D),
        "wqkvT": np.asarray(L0_attn_Wqkv_w).T, "qkv_bT": by_feature(L0_attn_Wqkv_b),
        "convT": np.asarray(L0_attn_conv_w).transpose(2, 1, 0).reshape(3 * D, D),
        "conv_bT": by_feature(L0_attn_conv_b),
        "woT": np.asarray(L0_attn_out_w).T, "out_b": np.asarray(L0_attn_out_b).reshape(1, D),
        "gateT": np.asarray(L0_ffn_gate_w).T,
        "w1": L0_ffn_w1, "b1T": np.asarray(L0_ffn_b1).reshape(E, FT, P).transpose(0, 2, 1),
        "w2": L0_ffn_w2, "b2": L0_ffn_b2,
    }
    nc = bacc.Bacc("TRN2", target_bir_lowering=False, num_devices=1)
    arrays, t = {}, {}
    for name in _NAMES:
        a = np.ascontiguousarray(laid[name])
        arrays["in_" + name] = a
        t[name] = nc.dram_tensor("in_" + name, a.shape, mybir.dt.from_np(a.dtype), kind="ExternalInput").ap()
    out = nc.dram_tensor("out", [N, D], F32, kind="ExternalOutput").ap()
    perceiver_kernel(nc, t, out)
    r = run_bass_kernel_spmd(nc, [arrays], core_ids=[0])
    return r.results[0]["out"].reshape(B, S, D)
```

```python
from contextlib import ExitStack

import concourse.bass as bass
from concourse import mybir

F32 = mybir.dt.float32
F32R = mybir.dt.float32r
I32 = mybir.dt.int32
U32 = mybir.dt.uint32
BF16 = mybir.dt.bfloat16
ALU = mybir.AluOpType
ACT = mybir.ActivationFunctionType
AX = mybir.AxisListType

P = 128
B, S = 8, 64
D = 512
Q = 512
KT = D // P
N = B * S
NT = N // P
H, DH = 16, 32
HR = P // DH
E, F = 14, 1024
FT = F // P
MAX_BLOCKS = E + (2 * N - 1) // P + 1
OVER = MAX_BLOCKS - E
EPS = 1e-5
MASKED = -1e30
CLIP = 100.0
CONSTS = 9
SCORE_PARAMS = 6
PARAMS = 6
Q2C = 300
SCALE = float(DH) ** -0.5


def perceiver_kernel(nc, t, out):
    ctx = ExitStack()
    with ctx:
        def sb(name, shape, dt=F32):
            return ctx.enter_context(nc.sbuf_tensor(name, shape, dt))

        def overlaid(name, rounded_name, shape):
            with nc.sbuf_tensor(name, shape, F32) as plain:
                pass
            return plain, sb(rounded_name, shape, F32R)

        def sem(name):
            return ctx.enter_context(nc.semaphore(name))

        rows_dram = nc.dram_tensor("rows_dram", [MAX_BLOCKS * P, D], F32).ap()

        ident = sb("ident", [P, P])
        ones = sb("ones", [P, E])
        ones_bf = sb("ones_bf", [P, P], BF16); before_bf = sb("before_bf", [P, P], BF16)
        before = sb("before", [P, P])
        expert_row_i = sb("expert_row_i", [P, E], I32); over_row_i = sb("over_row_i", [P, OVER], I32)
        causal = sb("causal", [P, S])
        eps = sb("eps", [P, 1])
        ident_bf = sb("ident_bf", [P, P], BF16)
        causal_bf = sb("causal_bf", [P, 8, S], BF16)
        expert_row = sb("expert_row", [P, E])
        over_row = sb("over_row", [P, OVER])
        slot_row = sb("slot_row", [P, 2 * P])

        wcq = sb("wcq", [P, KT]); wq = sb("wq", [P, KT]); wc = sb("wc", [P, KT])
        scal = sb("scal", [P, 3]); bsum = sb("bsum", [P, 1])
        qkv_b = sb("qkv_b", [P, 3 * KT]); conv_b = sb("conv_b", [P, KT])
        gate = sb("gate", [P, KT, E])
        bl_row = sb("bl_row", [P, D]); ob_row = sb("ob_row", [P, D])
        b2_sb = sb("b2_sb", [E, D])

        x_res = sb("x_res", [P, NT, D])
        cn = sb("cn", [P, NT, D])
        cT, xr = overlaid("cT", "xr", [P, KT, N])
        xr = xr[:, :, :].rearrange("p a (u n) -> p (a u) n", n=KT * P).rearrange(
            "p (a u) (k n) -> p a u k n", a=2, n=P)
        w1, w1_lo = overlaid("w1", "w1_lo", [P, 2, KT * F])
        w2 = sb("w2", [P, 2, FT * D])
        wl = w2[:, :, :].rearrange("p a (k n) -> p (a k) n", n=D)
        w1_tiles = w1[:, :, :].rearrange("p a (k n) -> p (a k) n", n=D)
        conv = w1_tiles[:, 0:3 * KT, :]
        wo = w1_tiles[:, 3 * KT:4 * KT, :]
        wqkv = sb("wqkv", [P, KT, 3 * D])

        A1, w1_hi = overlaid("A1", "w1_hi", [P, 2 * 2 * KT * Q])
        w1_hi = w1_hi[:, :].rearrange("p (u n) -> p u n", u=2)
        ctxT = A1[:, 0:2 * KT * Q].rearrange("p (j k q) -> p j k q", j=2, k=KT)
        ctxN = A1[:, 2 * KT * Q:].rearrange("p (j k d) -> p j k d", j=2, k=KT)
        qT = A1[:, 0:2048].rearrange("p (k n) -> p k n", k=KT)
        kT = A1[:, 2048:4096].rearrange("p (k n) -> p k n", k=KT)
        vN = A1[:, 4096:6144].rearrange("p (t n) -> p t n", t=NT)
        vX = A1[:, 6144:8192].rearrange("p (t n) -> p t n", t=NT)
        wqkv_flat = wqkv[:, :, :].rearrange("p k n -> p (k n)")
        got = wqkv_flat[:, 0:2 * NT * D].rearrange("p (t c d) -> p t c d", t=NT, c=2)
        last_w = wqkv_flat[:, 4096:5120].rearrange("p (t s) -> p t s", t=NT)
        last_wT = wqkv_flat[:, 5120:6144].rearrange("p (u t n) -> p u t n", u=2, t=NT)
        A2 = sb("A2", [P, 3 * KT * N + KT * B * (S + 2)])
        cwT = A2[:, 0:2048].rearrange("p (k n) -> p k n", k=KT)
        c2qT = A2[:, 2048:4096].rearrange("p (k n) -> p k n", k=KT)
        ccT = A2[:, 4096:6144].rearrange("p (k n) -> p k n", k=KT)
        cqT = A2[:, 6144:8192].rearrange("p (k n) -> p k n", k=KT)
        oT = A2[:, 6144:].rearrange("p (k b s) -> p k b s", k=KT, b=B)
        sco = A2[:, 0:2048].rearrange("p (u r k) -> p u r k", u=2, k=S)
        prb = A2[:, 2048:4096].rearrange("p (u r k) -> p u r k", u=2, k=S)
        prT = A2[:, 4096:6144].rearrange("p (u c n) -> p u c n", u=2, n=P)
        xg = A2[:, 0:1024].rearrange("p (u d) -> p u d", u=2)
        hpre = A2[:, 2048:3072]
        hT = A2[:, 3072:5120].rearrange("p (u f n) -> p u f n", u=2, f=FT)
        ysb = A2[:, 5120:6144].rearrange("p (u d) -> p u d", u=2)
        att = sb("att", [P, Q]); zero_rows = att
        attT = sb("attT", [P, KT, P]); c2q = sb("c2q", [P, D])
        slot_row_i = c2q[:, 0:2 * P].bitcast(I32); last_w2 = c2q[:, 2 * P:4 * P]

        st = sb("st", [P, NT, 6]); mv = sb("mv", [P, NT, 2])
        sd = sb("sd", [P, NT]); rstd = sb("rstd", [P, NT])
        nmax = sb("nmax", [P, NT]); asum = sb("asum", [P, NT]); arec = sb("arec", [P, NT])
        msum = sb("msum", [P, NT])
        mT = sb("mT", [1, 2, S]); mmax = sb("mmax", [1, 2]); msb = sb("msb", [1, 2])
        batt = sb("batt", [P, NT, 2]); q2cT = sb("q2cT", [P, KT, B])
        hmax = sb("hmax", [P, H]); hsum = sb("hsum", [P, 2, H]); hrec = sb("hrec", [P, 2, H])
        lg = sb("lg", [P, NT, E]); lgc = sb("lgc", [P, NT, E]); lneg = sb("lneg", [P, NT]); top2 = sb("top2", [P, NT, 2])
        lsum = sb("lsum", [P, NT])
        top = sb("top", [P, NT, 8]); topi = sb("topi", [P, NT, 8], U32); topf = sb("topf", [P, NT, 2])
        wsum = sb("wsum", [P, NT]); wk = sb("wk", [P, NT, 2])
        oh = sb("oh", [P, 2, NT, E]); wsel = sb("wsel", [P, NT, E])
        wtmp = sb("wtmp", [P, NT, E]); wselT = sb("wselT", [E, NT, P])
        sel = sb("sel", [P, NT, E], BF16); sel_before = sb("sel_before", [P, NT, E], BF16)
        limit = sb("limit", [P, E]); offset = sb("offset", [P, E]); more = sb("more", [P, NT, E])
        made = sb("made", [P, NT, E]); shift = sb("shift", [P, E]); far = sb("far", [P, E]); cnt = sb("cnt", [P, 2 * E])
        slot = sb("slot", [P, E])
        slot_c = sb("slot_c", [P, 2, E]); key = sb("key", [P, NT, E]); base_slot = sb("base_slot", [P, 1])
        slot_k = sb("slot_k", [P, 2, NT]); slot_i = sb("slot_i", [P, 2, NT], I32)
        rel = sb("rel", [P, 2, NT]); early = sb("early", [P, 2, NT]); wgot = sb("wgot", [P, 2, NT])
        bm = wqkv_flat[:, 4096:4096 + OVER * NT * E].rearrange("p (o t e) -> p o t e", o=OVER, t=NT)
        blk_f = sb("blk_f", [P, MAX_BLOCKS]); blk_i = sb("blk_i", [P, MAX_BLOCKS], I32)
        np_f = sb("np_f", [P, 4]); np_s = sb("np_s", [P, 2]); pairs_i = sb("pairs_i", [P, 2], I32)
        b1_sb = sb("b1_sb", [P, 2, FT])

        banks = ctx.enter_context(nc.psum_tensor("banks", [P, 8, 512], F32))
        pb = [banks[:, i, :] for i in range(8)]
        Z = pb[0:4]
        SC, TR, CQ, MI = pb[4:8]
        FB, PT, TB, PS, PO = pb[0:2], pb[2:4], pb[4], banks[:, 5:7, :], pb[7]
        LG = pb[6][:, 0:E]
        CNT = pb[5]
        HP, HT, XT, YP = (pb[0:2], pb[2:4]), pb[4:6], pb[6], pb[7]

        x_in = [sem(f"x_in{n}") for n in range(NT)]
        q2c_taken, score_params_in = sem("q2c_taken"), sem("score_params_in")
        wqkv_in, conv_in, wo_in, params_in = map(sem, ("wqkv_in", "conv_in", "wo_in", "params_in"))
        ctxT_in, ctxN_in = sem("ctxT_in"), sem("ctxN_in")
        wl_in = [sem(f"wl_in{i}") for i in range(4)]
        w1_in, w2_in, b1_in = ([sem(f"{w}_in{u}") for u in range(2)] for w in ("w1", "w2", "b1"))
        consts, pool_step = sem("consts"), sem("pool_step")
        dve_step, act_step = sem("dve_step"), sem("act_step")
        normed, var_ready, root_ready = sem("normed"), sem("var_ready"), sem("root_ready")
        cT_psum, cT_ready, cw_ready = sem("cT_psum"), sem("cT_ready"), sem("cw_ready")
        s_psum, nmax_ready, exp_done, r_psum = map(sem, ("s_psum", "nmax_ready", "exp_done", "r_psum"))
        aT_psum, aT_ready, cq_psum, c2q_ready = map(sem, ("aT_psum", "aT_ready", "cq_psum", "c2q_ready"))
        c2qT_psum, c2qT_ready, cc_ready = map(sem, ("c2qT_psum", "c2qT_ready", "cc_ready"))
        m_ready, mT_psum, msub_ready, mexp_done = map(sem, ("m_ready", "mT_psum", "msub_ready", "mexp_done"))
        mn_ready, mn_psum, batt_ready, q2c_psum = map(sem, ("mn_ready", "mn_psum", "batt_ready", "q2c_psum"))
        cqT_ready, z_psum, pads_ready = sem("cqT_ready"), sem("z_psum"), sem("pads_ready")
        v_ready, fill_taken = sem("v_ready"), sem("fill_taken")
        filled = sem("filled")
        vx_in = [sem(f"vx_in{n}") for n in range(NT)]
        half_scored, sc_psum, sub_ready, pexp_done = map(sem, ("half_scored", "sc_psum", "sub_ready", "pexp_done"))
        hrec_ready, pr_ready, pT_psum, pT_ready = map(sem, ("hrec_ready", "pr_ready", "pT_psum", "pT_ready"))
        o_psum, o_ready, out_psum, out_taken = map(sem, ("o_psum", "o_ready", "out_psum", "out_taken"))
        lg_psum, lg_taken, lexp_done = map(sem, ("lg_psum", "lg_taken", "lexp_done"))
        top_ready = sem("top_ready")
        before_ready, last_psum, last_taken = sem("before_ready"), sem("last_psum"), sem("last_taken")
        count_taken = sem("count_taken")
        lastT_psum, last_ready, slot_row_made = sem("lastT_psum"), sem("last_ready"), sem("slot_row_made")
        sel_ready, count_psum, wsel_ready, wselT_psum = map(sem, ("sel_ready", "count_psum", "wsel_ready", "wselT_psum"))
        slots_ready, blocks_ready, scattered = map(sem, ("slots_ready", "blocks_ready", "scattered"))
        zero_made, rows_zeroed = sem("zero_made"), sem("rows_zeroed")
        gather_turn = sem("gather_turn")
        xg_in = [sem(f"xg_in{u}") for u in range(2)]
        hi_ready, lo_ready, xT_hi = sem("hi_ready"), sem("lo_ready"), sem("xT_hi")
        xT_psum, xT_ready, h_psum, hpre_ready = map(sem, ("xT_psum", "xT_ready", "h_psum", "hpre_ready"))
        hT_psum, gelu_done, y_psum = map(sem, ("hT_psum", "gelu_done", "y_psum"))
        y_taken = sem("y_taken")
        y_free = [sem(f"y_free{u}") for u in range(2)]
        y_gathered = [sem(f"y_gathered{n}") for n in range(NT)]
        final_ready, out_stored = sem("final_ready"), sem("out_stored")

        block = ctx.enter_context(nc.Block())

        def tile(n):
            return slice(n * P, (n + 1) * P)

        def turn_bank(l, n):
            return TB if l == 2 else Z[n] if l == 1 or n >= 2 else (TR, CQ)[n]

        BEFORE = [("qk", 0, f) for f in range(0, 2 * KT, 2)]
        SLOTS = [
            [("v", 0), ("qk", 1, 0), ("qk", 1, 2), None],
            [("qk", 1, 4), ("qk", 1, 6), ("v", 1), None],
            [("v", 2), ("conv", 0, 0), ("conv", 0, 1), ("conv", 0, 2)],
            [("conv", 0, 3), ("v", 3), ("conv", 1, 0), ("conv", 1, 1)],
            [("conv", 1, 2), ("conv", 1, 3), ("conv", 2, 0), ("conv", 2, 1)],
            [("conv", 2, 2), ("conv", 2, 3), ("conv", 3, 0), ("conv", 3, 1)],
            [("conv", 3, 2), ("conv", 3, 3), ("out", 0), None],
            [("out", 1), None, None, None],
        ]
        FILLS = BEFORE + [f for slots in SLOTS for f in slots
                          if f and f[0] != "out" and not (f[0] == "conv" and f[2] < KT - 1)]

        def pair_count(eng):
            eng.wait_ge(blocks_ready, 1)
            return eng.value_load(pairs_i[0:1, 0:1], min_val=E // 2, max_val=MAX_BLOCKS // 2)

        def expert_of(eng, b):
            return eng.value_load(blk_i[0:1, bass.ds(b, 1)], min_val=0, max_val=E - 1)

        @block.sync
        def _(sp):
            def load_x(n):
                sp.dma_start(x_res[:, n, :], t["x"][tile(n), :]).then_inc(x_in[n], 16)

            def load_ctxT(n):
                if n:
                    sp.wait_ge(s_psum, n)
                for j in range(2):
                    sp.dma_start(ctxT[:, j], t["ctxT"][2 * n + j].rearrange("(k p) q -> p k q", p=P)) \
                        .then_inc(ctxT_in, 16)

            def load_ctxN(n):
                if n:
                    sp.wait_ge(cq_psum, n)
                for j in range(2):
                    sp.dma_start(ctxN[:, j], t["ctx"][2 * n + j].rearrange("(k p) d -> p k d", p=P)) \
                        .then_inc(ctxN_in, 16)

            def load_wl(part):
                sp.dma_start(wl[:, KT * part:KT * (part + 1), :],
                             t["wlT"][D * part:D * (part + 1), :].rearrange("(k p) n -> p k n", p=P)) \
                    .then_inc(wl_in[part], 16)

            load_x(0)
            load_x(1)
            load_ctxT(0)
            load_x(2)
            load_x(3)
            load_wl(0)
            load_ctxN(0)
            load_ctxT(1)
            load_wl(3)
            load_wl(1)
            load_wl(2)
            load_ctxN(1)
            load_ctxT(2)
            load_ctxN(2)
            load_ctxT(3)
            sp.dma_start(wqkv[:, :, :], t["wqkvT"].rearrange("(k p) n -> p k n", p=P)).then_inc(wqkv_in, 16)
            load_ctxN(3)
            sp.dma_start(conv, t["convT"].rearrange("(k p) n -> p k n", p=P)).then_inc(conv_in, 16)
            sp.dma_start(wo, t["woT"].rearrange("(k p) n -> p k n", p=P)).then_inc(wo_in, 16)
            sp.wait_ge(z_psum, NT)
            for u in range(2):
                sp.dma_start(w2[:, u, :].rearrange("p (k f) -> p k f", k=FT),
                             t["w2"][u].rearrange("(k p) f -> p k f", p=P)).then_inc(w2_in[u], 16)
            for n in range(NT):
                sp.wait_ge(v_ready, n + 1)
                for j in range(2):
                    sp.dma_start(vX[S * (1 - j):S * (2 - j), n, :], vN[S * j:S * (j + 1), n, :]) \
                        .then_inc(vx_in[n], 16)
            sp.wait_ge(zero_made, 1)
            sp.dma_start(rows_dram.rearrange("(b p) d -> p b d", p=P),
                         zero_rows[:, :].unsqueeze(1).to_broadcast([P, MAX_BLOCKS, D])).then_inc(rows_zeroed, 16)
            for u in range(2):
                if u == 0:
                    sp.wait_ge(filled, len(FILLS))
                else:
                    sp.wait_ge(out_psum, NT)
                sp.dma_start(w1[:, u, :].rearrange("p (k f) -> p k f", k=KT),
                             t["w1"][u].rearrange("(k p) f -> p k f", p=P)).then_inc(w1_in[u], 16)
                sp.dma_start(b1_sb[:, u, :], t["b1T"][u]).then_inc(b1_in[u], 16)
            sp.wait_ge(scattered, 16 * 2 * NT)
            for u in range(2):
                sp.dma_start(xg[:, u, :], rows_dram[u * P:(u + 1) * P, :]).then_inc(xg_in[u], 16)
            pairs = pair_count(sp)
            with sp.Fori(1, pairs) as i:
                for u in range(2):
                    sp.wait_ge(xT_psum, 2 * i + u - 1)
                    sp.dma_start(xg[:, u, :], rows_dram.rearrange("(b p) d -> b p d", p=P)[bass.ds(2 * i + u, 1)]
                                 .rearrange("o p d -> p (o d)")).then_inc(xg_in[u], 16)
                    e = expert_of(sp, 2 * i + u)
                    sp.wait_ge(h_psum, 2 * i + u - 1)
                    sp.dma_start(w1[:, u, :].rearrange("p (k f) -> p k f", k=KT),
                                 t["w1"][bass.ds(e, 1)].rearrange("o (k p) f -> p (o k) f", p=P)) \
                        .then_inc(w1_in[u], 16)
            for n in range(NT):
                sp.wait_ge(final_ready, n + 1)
                sp.dma_start(out[tile(n), :], got[:, n, 0, :]).then_inc(out_stored, 16)
            sp.wait_ge(out_stored, 16 * NT)

        @block.scalar
        def _(act):
            for dst, src in ((wcq, "wcqT"), (wq, "wqT"), (wc, "wcT")):
                act.dma_start(dst[:, :], t[src]).then_inc(score_params_in, 16)
            for i, name in enumerate(("b_cq", "b_c", "b_q")):
                act.dma_start(scal[:, i:i + 1], t[name].to_broadcast([P, 1])).then_inc(score_params_in, 16)
            def copy_cT(l, n):
                act.wait_ge(cT_psum, NT * l + n + 1)
                nc.scalar.activation(cT[:, :, tile(n)], turn_bank(l, n)[:, :].rearrange(
                    "p (k n) -> p k n", k=KT), ACT.Copy).then_inc(cT_ready, 1)

            copy_cT(0, 0)
            for n in range(NT):
                act.wait_ge(nmax_ready, n + 1)
                if n:
                    act.wait_ge(aT_psum, n)
                nc.scalar.activation(att[:, :], SC[:, :], ACT.Exp, bias=nmax[:, n:n + 1],
                                     accum_out=asum[:, n:n + 1]).then_inc(exp_done, 1)
                if n == 0:
                    copy_cT(0, 1)
                act.wait_ge(aT_psum, n + 1)
                if n:
                    act.wait_ge(cq_psum, n)
                nc.scalar.activation(attT[:, :, :], TR[:, :].rearrange("p (k n) -> p k n", k=KT),
                                     ACT.Copy).then_inc(aT_ready, 1)
                act.wait_ge(msub_ready, n + 1)
                nc.scalar.activation(mT[:, :, :], mT[:, :, :], ACT.Exp).then_inc(mexp_done, 1)
                if n == 0:
                    for later in range(2, NT):
                        copy_cT(0, later)
                act.wait_ge(c2qT_psum, n + 1)
                nc.scalar.activation(c2qT[:, :, tile(n)], TR[:, :].rearrange("p (k n) -> p k n", k=KT),
                                     ACT.Copy).then_inc(c2qT_ready, 1)
                if n:
                    copy_cT(1, n - 1)

            def take(g):
                act.wait_ge(filled, g + 1)
                what, n = FILLS[g][0:2]
                bank = FB[g % 2]
                if what == "v":
                    nc.scalar.activation(vN[:, n, :], bank[:, :], ACT.Copy).then_inc(fill_taken, 1)
                    act.wait_ge(fill_taken, g + 1)
                    act.sem_inc(v_ready, 1)
                    return
                for i in range(KT if what == "conv" else 2):
                    if what == "conv":
                        dst, src, bias = qT[:, i, tile(n)], bank[:, tile(i)], conv_b[:, i:i + 1]
                    else:
                        f = FILLS[g][2] + i
                        dst = (qT if f < KT else kT)[:, f % KT, 2 * P * n:2 * P * (n + 1)]
                        src, bias = bank[:, 2 * P * i:2 * P * (i + 1)], qkv_b[:, f:f + 1]
                    ins = nc.scalar.activation(dst, src, ACT.Identity, bias=bias)
                ins.then_inc(fill_taken, 1)

            def exponentials(m):
                act.wait_ge(sub_ready, m + 1)
                if m >= 2:
                    act.wait_ge(pT_psum, m - 1)
                nc.scalar.activation(prb[:, m % 2], sco[:, m % 2], ACT.Exp, scale=SCALE) \
                    .then_inc(pexp_done, 1)

            def copy_prT(m):
                act.wait_ge(pT_psum, m + 1)
                if m >= 2:
                    act.wait_ge(o_psum, 2 * m - 2)
                for i in range(2):
                    nc.scalar.activation(prT[:, m % 2, 4 * i:4 * i + 4, :],
                                         PT[i][:, :].rearrange("p (c n) -> p c n", n=P),
                                         ACT.Copy).then_inc(pT_ready, 1)

            def split_hi(b, u, loaded):
                act.wait_ge(w1_in[u], loaded)
                for k in range(KT):
                    nc.scalar.activation(w1_hi[:, u, k * F:(k + 1) * F], w1[:, u, k * F:(k + 1) * F],
                                         ACT.Copy).then_inc(hi_ready, 1)

            def exp_logits(n):
                act.wait_ge(top_ready, n + 1)
                nc.scalar.activation(lg[:, n, :], lgc[:, n, :], ACT.Exp, bias=lneg[:, n:n + 1],
                                     accum_out=lsum[:, n:n + 1]).then_inc(lexp_done, 1)
                nc.scalar.activation(top2[:, n, :], top[:, n, 0:2], ACT.Exp, bias=lneg[:, n:n + 1]) \
                    .then_inc(lexp_done, 1)

            for g in range(len(BEFORE)):
                take(g)
            copy_cT(1, NT - 1)
            for m in range(2 * NT):
                if SLOTS[m][0] in FILLS:
                    take(FILLS.index(SLOTS[m][0]))
                exponentials(m)
                if m:
                    copy_prT(m - 1)
                for what in SLOTS[m][1:]:
                    if what in FILLS:
                        take(FILLS.index(what))
            def root(n):
                act.wait_ge(var_ready, n + 1)
                nc.scalar.activation(sd[:, n:n + 1], mv[:, n, 1:2], ACT.Sqrt, bias=eps[:, 0:1]) \
                    .then_inc(root_ready, 1)

            root(0)
            copy_prT(2 * NT - 1)
            copy_cT(2, 0)
            root(1)
            split_hi(0, 0, 16)
            root(2)
            copy_cT(2, 1)
            root(3)
            copy_cT(2, 2)
            copy_cT(2, 3)
            for n in range(NT):
                exp_logits(n)

            def gelu(b, u, loaded):
                act.wait_ge(hT_psum, b + 1)
                for f in range(FT):
                    if f == 0:
                        act.wait_ge(b1_in[u], loaded)
                    ins = nc.scalar.activation(hT[:, u, f, :], HT[f // 4][:, tile(f % 4)], ACT.Gelu,
                                               bias=b1_sb[:, u, f:f + 1])
                ins.then_inc(gelu_done, 1)

            def store_y(b, u):
                act.wait_ge(y_taken, b + 2)
                act.dma_start(rows_dram.rearrange("(b p) d -> b p d", p=P)[bass.ds(b, 1)]
                              .rearrange("o p d -> p (o d)"), ysb[:, u, :]).then_inc(y_free[u], 16)

            act.wait_ge(o_psum, 4 * NT)
            split_hi(1, 1, 16)
            gelu(0, 0, 16)
            pairs = pair_count(act)
            with act.Fori(1, pairs) as i:
                for u in range(2):
                    split_hi(2 * i + u, u, 16 * i + 16)
                    store_y(2 * i - 2 + u, u)
                    e = expert_of(act, 2 * i + u)
                    act.dma_start(w2[:, u, :].rearrange("p (k f) -> p k f", k=FT),
                                  t["w2"][bass.ds(e, 1)].rearrange("o (k p) f -> p (o k) f", p=P)) \
                        .then_inc(w2_in[u], 16)
                    if u == 0:
                        gelu(2 * i - 1, 1, 16 * i)
                    else:
                        gelu(2 * i, 0, 16 * i + 16)
                    act.wait_ge(gelu_done, 2 * i + u - 1)
                    act.dma_start(b1_sb[:, u, :], t["b1T"][bass.ds(e, 1)].rearrange("o p f -> p (o f)")) \
                        .then_inc(b1_in[u], 16)
            last = act.value_load(pairs_i[0:1, 1:2], min_val=E // 2 - 1, max_val=MAX_BLOCKS // 2 - 1)
            gelu(2 * last + 1, 1, 16 * last + 16)

        @block.gpsimd
        def _(pool):
            nc.gpsimd.memset(ident[:, :], 0.0).then_inc(pool_step, 1)
            nc.gpsimd.memset(before[:, :], 1.0).then_inc(pool_step, 1)
            nc.gpsimd.memset(causal[:, :], 0.0).then_inc(pool_step, 1)
            pool.wait_ge(pool_step, 3)
            nc.gpsimd.affine_select(out=ident[:, :], in_=ident[:, :], pattern=[[-1, P]], compare_op=ALU.not_equal,
                                    fill=1.0, base=0, channel_multiplier=1).then_inc(consts, 1)
            pool.wait_ge(consts, 1)
            nc.gpsimd.affine_select(out=before[:, :], in_=before[:, :], pattern=[[1, P]], compare_op=ALU.is_gt,
                                    fill=0.0, base=0, channel_multiplier=-1).then_inc(consts, 1)
            for j in range(2):
                pool.wait_ge(consts, 2 + j)
                v = causal[S * j:S * (j + 1), :]
                nc.gpsimd.affine_select(out=v, in_=v, pattern=[[-1, S]], compare_op=ALU.is_ge, fill=MASKED,
                                        base=0, channel_multiplier=1).then_inc(consts, 1)
            pool.wait_ge(consts, 4)
            nc.gpsimd.memset(ones[:, :], 1.0).then_inc(consts, 1)
            nc.gpsimd.memset(ones_bf[:, :], 1.0).then_inc(consts, 1)
            nc.gpsimd.memset(batt[:, :, :], 0.0).then_inc(consts, 1)
            nc.gpsimd.iota(expert_row_i[:, :], pattern=[[1, E]], base=0, channel_multiplier=0).then_inc(consts, 1)
            pool.wait_ge(consts, CONSTS - 1)
            nc.gpsimd.iota(over_row_i[:, :], pattern=[[1, OVER]], base=1, channel_multiplier=0).then_inc(consts, 1)

            for dst, src in ((qkv_b, "qkv_bT"), (conv_b, "conv_bT")):
                pool.dma_start(dst[:, :], t[src]).then_inc(params_in, 16)
            pool.dma_start(bl_row[:, :], t["b_l"].to_broadcast([P, D])).then_inc(params_in, 16)
            pool.dma_start(ob_row[:, :], t["out_b"].to_broadcast([P, D])).then_inc(params_in, 16)
            pool.dma_start(gate[:, :, :], t["gateT"].rearrange("(k p) e -> p k e", p=P)).then_inc(params_in, 16)
            pool.dma_start(b2_sb[:, :], t["b2"]).then_inc(params_in, 16)

            def norm_probabilities(m):
                pool.wait_ge(hrec_ready, m + 1)
                nc.gpsimd.tensor_tensor(prb[:, m % 2], prb[:, m % 2],
                                        hrec[:, m % 2, :].unsqueeze(2).to_broadcast([P, H, S]),
                                        ALU.mult).then_inc(pr_ready, 1)

            pool.wait_ge(z_psum, NT)
            for side in (0, S + 1):
                nc.gpsimd.memset(oT[:, :, :, side:side + 1], 0.0).then_inc(pads_ready, 1)
            nc.gpsimd.memset(zero_rows[:, :], 0.0).then_inc(zero_made, 1)
            nc.gpsimd.iota(slot_row_i, pattern=[[1, 2 * P]], base=0, channel_multiplier=0).then_inc(slot_row_made, 1)
            for m in range(2 * NT):
                norm_probabilities(m)

            pool.wait_ge(rows_zeroed, 16)
            for n in range(NT):
                pool.wait_ge(slots_ready, n + 1)
                for c in range(2):
                    pool.indirect_dma_start(rows_dram, bass.IndirectOffsetOnAxis(ap=slot_i[:, c, n:n + 1], axis=0),
                                            cn[:, n, :], None).then_inc(scattered, 16)
            for u in range(2):
                nc.gpsimd.memset(ysb[:, u, :], 0.0).then_inc(y_free[u], 16)
            pairs = pair_count(pool)
            for u in range(2):
                pool.wait_ge(y_free[u], 16 * pairs)
                pool.sem_inc(gather_turn, 1)
            for n in range(NT):
                for c in range(2):
                    pool.indirect_dma_start(got[:, n, c, :], None, rows_dram,
                                            bass.IndirectOffsetOnAxis(ap=slot_i[:, c, n:n + 1], axis=0)) \
                        .then_inc(y_gathered[n], 16)

        @block.vector
        def _(dve):
            step = [0]

            def link(ins):
                step[0] += 1
                ins.then_inc(dve_step, 1)
                dve.wait_ge(dve_step, step[0])

            def norm(n, by_scalar=False):
                link(nc.vector.bn_stats(st[:, n, :], x_res[:, n, :]))
                var, r, h = mv[:, n, 1:2], rstd[:, n:n + 1], sd[:, n:n + 1]
                if by_scalar:
                    nc.vector.bn_aggr(mv[:, n, :], st[:, n, :]).then_inc(var_ready, 1)
                    dve.wait_ge(root_ready, n + 1)
                    link(nc.vector.reciprocal(r, h))
                    nc.vector.tensor_scalar(cn[:, n, :], x_res[:, n, :], mv[:, n, 0:1], r,
                                            ALU.subtract, ALU.mult).then_inc(normed, 1)
                    return
                link(nc.vector.bn_aggr(mv[:, n, :], st[:, n, :]))
                link(nc.vector.tensor_scalar(var, var, EPS, None, ALU.add))
                link(nc.vector.tensor_scalar(r.bitcast(I32), var.bitcast(I32), -0.5, 1597463007.0, ALU.mult, ALU.add))
                scale = 1.0
                for _ in range(3):
                    link(nc.vector.tensor_scalar(h, r, r, var, ALU.mult, ALU.mult))
                    link(nc.vector.scalar_tensor_tensor(r, h, 3.0 * scale * scale, r, ALU.subtract, ALU.mult))
                    scale = -2.0 * scale ** 3
                link(nc.vector.tensor_scalar(r, r, 1.0 / scale, None, ALU.mult))
                nc.vector.tensor_scalar(cn[:, n, :], x_res[:, n, :], mv[:, n, 0:1], r,
                                        ALU.subtract, ALU.mult).then_inc(normed, 1)

            dve.wait_ge(x_in[0], 16)
            norm(0)
            def widen(n):
                dve.wait_ge(cT_ready, n + 1)
                for k in range(KT):
                    nc.vector.tensor_scalar(cwT[:, k, tile(n)], cT[:, k, tile(n)], wcq[:, k:k + 1], wq[:, k:k + 1],
                                            ALU.mult, ALU.add).then_inc(cw_ready, 1)

            def score_maxima(n):
                dve.wait_ge(s_psum, n + 1)
                nc.vector.tensor_reduce(nmax[:, n:n + 1], SC[:, :], AX.X, ALU.max, negate=True) \
                    .then_inc(nmax_ready, 1)

            def token_weights_head(n):
                dve.wait_ge(r_psum, n + 1)
                dve.wait_ge(nmax_ready, n + 1)
                link(nc.vector.scalar_tensor_tensor(msum[:, n:n + 1], nmax[:, n:n + 1], -1.0, MI[:, 0:1],
                                                    ALU.mult, ALU.add))
                nc.vector.tensor_scalar(msum[:, n:n + 1], msum[:, n:n + 1], bsum[:, 0:1], None, ALU.add) \
                    .then_inc(m_ready, 1)
                dve.wait_ge(mT_psum, n + 1)
                link(nc.vector.tensor_copy(mT[:, :, :], MI[0:1, P:2 * P].rearrange("p (j s) -> p j s", j=2)))
                link(nc.vector.tensor_reduce(mmax[:, :], mT[:, :, :], AX.X, ALU.max))
                nc.vector.tensor_tensor(mT[:, :, :], mT[:, :, :], mmax[:, :].unsqueeze(2).to_broadcast([1, 2, S]),
                                        ALU.subtract).then_inc(msub_ready, 1)

            def token_weights_tail(n):
                dve.wait_ge(exp_done, n + 1)
                link(nc.vector.reciprocal(arec[:, n:n + 1], asum[:, n:n + 1]))
                dve.wait_ge(mexp_done, n + 1)
                link(nc.vector.tensor_reduce(msb[:, :], mT[:, :, :], AX.X, ALU.add))
                link(nc.vector.reciprocal(msb[:, :], msb[:, :]))
                nc.vector.tensor_tensor(mT[:, :, :], mT[:, :, :], msb[:, :].unsqueeze(2).to_broadcast([1, 2, S]),
                                        ALU.mult).then_inc(mn_ready, 1)
                dve.wait_ge(mn_psum, n + 1)
                for j in range(2):
                    nc.vector.tensor_copy(batt[S * j:S * (j + 1), n, j:j + 1],
                                          MI[S * j:S * (j + 1), 2 * P:2 * P + 1]).then_inc(batt_ready, 1)

            def norm_sums(n):
                dve.wait_ge(cq_psum, n + 1)
                if n:
                    dve.wait_ge(c2qT_psum, n)
                nc.vector.tensor_scalar(c2q[:, :], CQ[:, :], arec[:, n:n + 1], None, ALU.mult) \
                    .then_inc(c2q_ready, 1)

            def times_batch_sum(n):
                dve.wait_ge(q2c_psum, n + 1)
                nc.vector.tensor_copy(q2cT[:, :, 2 * n:2 * n + 2],
                                      MI[:, Q2C:Q2C + 2 * KT].rearrange("p (k b) -> p k b", k=KT)) \
                    .then_inc(q2c_taken, 1)
                dve.wait_ge(q2c_taken, n + 1)
                nc.vector.tensor_tensor(cqT[:, :, tile(n)].rearrange("p k (b s) -> p k b s", b=2),
                                        cT[:, :, tile(n)].rearrange("p k (b s) -> p k b s", b=2),
                                        q2cT[:, :, 2 * n:2 * n + 2].unsqueeze(3).to_broadcast([P, KT, 2, S]),
                                        ALU.mult).then_inc(cqT_ready, 1)

            def times_c2q(n):
                dve.wait_ge(c2qT_ready, n + 1)
                nc.vector.tensor_tensor(ccT[:, :, tile(n)], c2qT[:, :, tile(n)], cT[:, :, tile(n)],
                                        ALU.mult).then_inc(cc_ready, 1)

            def add_z(n):
                dve.wait_ge(z_psum, n + 1)
                link(nc.vector.tensor_tensor(x_res[:, n, :], Z[n][:, :], x_res[:, n, :], ALU.add))
                norm(n)

            def add_bias(n):
                dve.wait_ge(normed, n + 1)
                link(nc.vector.tensor_tensor(x_res[:, n, :], x_res[:, n, :], bl_row[:, :], ALU.add))

            dve.wait_ge(score_params_in, 16 * SCORE_PARAMS)
            widen(0)
            for n in range(1, NT - 1):
                dve.wait_ge(x_in[n], 16)
                norm(n)
            score_maxima(0)
            link(nc.vector.tensor_reduce(bsum[:, :], scal[:, :], AX.X, ALU.add))
            token_weights_head(0)
            dve.wait_ge(x_in[NT - 1], 16)
            norm(NT - 1)
            token_weights_tail(0)
            for n in range(1, NT):
                widen(n)
            dve.wait_ge(consts, CONSTS)
            link(nc.vector.tensor_copy(ident_bf[:, :], ident[:, :]))
            link(nc.vector.tensor_copy(before_bf[:, :], before[:, :]))
            link(nc.vector.tensor_copy(causal_bf[:, :, :], causal[:, :].unsqueeze(1).to_broadcast([P, 8, S])))
            link(nc.vector.tensor_copy(expert_row[:, :], expert_row_i[:, :]))
            link(nc.vector.tensor_copy(over_row[:, :], over_row_i[:, :]))
            link(nc.vector.tensor_scalar(offset[:, :], expert_row[:, :], float(P), None, ALU.mult))
            link(nc.vector.memset(limit[:, :], float(P)))
            link(nc.vector.memset(eps[:, :], EPS))

            dve.wait_ge(params_in, 16 * PARAMS)
            add_bias(0)
            for n in range(NT):
                if n:
                    token_weights_head(n)
                    token_weights_tail(n)
                norm_sums(n)
                if 0 < n < NT - 1:
                    add_z(n - 1)
                if n + 1 < NT:
                    score_maxima(n + 1)
                    add_bias(n + 1)
                times_batch_sum(n)
                times_c2q(n)
            add_z(NT - 2)
            add_z(NT - 1)

            def softmax(m):
                u = m % 2
                dve.wait_ge(sc_psum, m + 1)
                if m >= 2:
                    dve.wait_ge(pexp_done, m - 1)
                scores = PS.rearrange("p b (g k) -> p (b g) k", k=S)
                link(nc.vector.tensor_reduce(hmax[:, :], scores, AX.X, ALU.max))
                nc.vector.tensor_tensor(sco[:, u], scores, hmax[:, :].unsqueeze(2).to_broadcast([P, H, S]),
                                        ALU.subtract).then_inc(sub_ready, 1)

            def sums(m):
                dve.wait_ge(pexp_done, m + 1)
                if m >= 2:
                    dve.wait_ge(pr_ready, m - 1)
                link(nc.vector.tensor_reduce(hsum[:, m % 2, :], prb[:, m % 2], AX.X, ALU.add))
                nc.vector.reciprocal(hrec[:, m % 2, :], hsum[:, m % 2, :]).then_inc(hrec_ready, 1)

            def take_out(m):
                n = m % NT
                dve.wait_ge(o_psum, 2 * m + 2)
                for w in range(2):
                    src = PO[:, 2 * P * w:2 * P * (w + 1)].rearrange("p (h b s) -> p h b s", h=2, b=2)
                    bias = qkv_b[:, 2 * KT + w:3 * KT:2].unsqueeze(2).unsqueeze(3).to_broadcast([P, 2, 2, S])
                    if m < NT:
                        dst = oT[:, w:KT:2, 2 * n:2 * n + 2, 1:S + 1]
                    else:
                        dst = cT[:, w:KT:2, tile(n)].rearrange("p h (b s) -> p h b s", b=2)
                    nc.vector.tensor_tensor(dst, src, bias, ALU.add).then_inc(o_ready, 1)

            def finish(n):
                dve.wait_ge(out_psum, n + 1)
                nc.vector.tensor_tensor(x_res[:, n, :], pb[(len(FILLS) + n) % 2][:, :], x_res[:, n, :], ALU.add) \
                    .then_inc(out_taken, 1)
                dve.wait_ge(out_taken, n + 1)
                norm(n, by_scalar=True)

            every = expert_row[:, :]

            def choose(n):
                dve.wait_ge(lg_psum, n + 1)
                nc.vector.tensor_copy(lgc[:, n, :], LG).then_inc(lg_taken, 1)
                dve.wait_ge(lg_taken, n + 1)
                link(nc.vector.max(top[:, n, :], lgc[:, n, :]))
                nc.vector.tensor_scalar(lneg[:, n:n + 1], top[:, n, 0:1], -1.0, None, ALU.mult).then_inc(top_ready, 1)
                link(nc.vector.max_index(topi[:, n, :], top[:, n, :], lgc[:, n, :]))
                link(nc.vector.tensor_copy(topf[:, n, :], topi[:, n, 0:2]))
                for c in range(2):
                    link(nc.vector.tensor_scalar(oh[:, c, n, :], every, topf[:, n, c:c + 1], None, ALU.is_equal))
                nc.vector.tensor_tensor(sel[:, n, :], oh[:, 0, n, :], oh[:, 1, n, :], ALU.add).then_inc(sel_ready, 1)
                if n + 1 < NT:
                    dve.wait_ge(sel_ready, n + 1)
                    if n == 0:
                        ins = nc.vector.tensor_copy(sel_before[:, 1, :], sel[:, 0, :])
                    else:
                        ins = nc.vector.tensor_tensor(sel_before[:, n + 1, :], sel_before[:, n, :], sel[:, n, :],
                                                      ALU.add)
                    ins.then_inc(before_ready, 1)
                    dve.wait_ge(before_ready, n + 1)

            def place(n):
                dve.wait_ge(count_psum, n + 1)
                nc.vector.tensor_copy(cnt[:, :], CNT[:, 0:2 * E]).then_inc(count_taken, 1)
                dve.wait_ge(count_taken, n + 1)
                pos, upto = cnt[:, 0:E], cnt[:, E:2 * E]
                link(nc.vector.tensor_tensor(more[:, n, :], upto, limit[:, :], ALU.is_gt))
                link(nc.vector.tensor_tensor_scan(made[:, n, :], ones[:, :], more[:, n, :],
                                                  made[:, n - 1, E - 1:E] if n else 0.0, ALU.mult, ALU.add))
                link(nc.vector.scalar_tensor_tensor(shift[:, :], made[:, n, :], float(P), limit[:, :],
                                                    ALU.mult, ALU.subtract))
                link(nc.vector.scalar_tensor_tensor(shift[:, :], shift[:, :], float(P * (E - 1)), offset[:, :],
                                                    ALU.add, ALU.subtract))
                link(nc.vector.tensor_tensor(far[:, :], pos, limit[:, :], ALU.is_ge))
                link(nc.vector.tensor_tensor(far[:, :], far[:, :], shift[:, :], ALU.mult))
                link(nc.vector.tensor_tensor(slot[:, :], pos, offset[:, :], ALU.add))
                link(nc.vector.tensor_tensor(slot[:, :], slot[:, :], far[:, :], ALU.add))
                link(nc.vector.tensor_tensor(slot_c[:, :, :], oh[:, :, n, :],
                                             slot[:, :].unsqueeze(1).to_broadcast([P, 2, E]), ALU.mult))
                link(nc.vector.tensor_reduce(slot_k[:, :, n], slot_c[:, :, :], AX.X, ALU.add))
                nc.vector.tensor_copy(slot_i[:, :, n], slot_k[:, :, n]).then_inc(slots_ready, 1)
                if n + 1 < NT:
                    link(nc.vector.tensor_tensor(shift[:, :], shift[:, :], more[:, n, :], ALU.mult))
                    link(nc.vector.tensor_tensor(offset[:, :], offset[:, :], shift[:, :], ALU.add))
                    link(nc.vector.scalar_tensor_tensor(limit[:, :], more[:, n, :], float(P), limit[:, :],
                                                        ALU.mult, ALU.add))

            def split_lo(b, u, parts):
                for k in parts:
                    dve.wait_ge(hi_ready, KT * b + k + 1)
                    part = slice(k * F, (k + 1) * F)
                    nc.vector.tensor_tensor(w1_lo[:, u, part], w1[:, u, part], w1_hi[:, u, part].bitcast(F32),
                                            ALU.subtract).then_inc(lo_ready, 1)

            def take_xT(b, u):
                dve.wait_ge(xT_psum, b + 1)
                if not isinstance(b, int):
                    dve.wait_ge(h_psum, b - 1)
                turned = XT[:, :].rearrange("p (k n) -> p k n", k=KT)
                nc.vector.tensor_copy(xr[:, 0, u], turned).then_inc(xT_hi, 1)
                dve.wait_ge(xT_hi, b + 1)
                nc.vector.tensor_tensor(xr[:, 1, u], turned, xr[:, 0, u].bitcast(F32), ALU.subtract) \
                    .then_inc(xT_ready, 1)

            for m in range(2 * NT):
                softmax(m)
                sums(m)
                if m < NT:
                    dve.wait_ge(normed, 2 * NT)
                    link(nc.vector.tensor_tensor(x_res[:, m, :], x_res[:, m, :], ob_row[:, :], ALU.add))
                if m:
                    take_out(m - 1)
            finish(0)
            take_out(2 * NT - 1)
            finish(1)
            choose(0)
            split_lo(0, 0, range(KT))
            finish(2)
            choose(1)
            place(0)
            finish(3)
            place(1)
            choose(2)
            choose(3)
            place(2)
            place(3)
            link(nc.vector.tensor_tensor(key[:, :, :], made[:, :, :], more[:, :, :], ALU.mult))
            for n in range(NT):
                link(nc.vector.tensor_tensor(bm[:, :, n, :], over_row[:, :].unsqueeze(2).to_broadcast([P, OVER, E]),
                                             key[:, n, :].unsqueeze(1).to_broadcast([P, OVER, E]), ALU.is_equal))
                link(nc.vector.tensor_tensor(bm[:, :, n, :], bm[:, :, n, :], expert_row[:, :].unsqueeze(1)
                                             .to_broadcast([P, OVER, E]), ALU.mult))
            link(nc.vector.tensor_copy(blk_f[:, 0:E], expert_row[:, :]))
            link(nc.vector.tensor_reduce(blk_f[:, E:MAX_BLOCKS], bm.rearrange("p o t e -> p o (t e)"), AX.X, ALU.add))
            link(nc.vector.tensor_copy(blk_i[:, :], blk_f[:, :]))
            for c in range(4):
                link(nc.vector.tensor_scalar(np_f[:, c:c + 1], made[:, NT - 1, E - 1:E], 2.0 * c, None, ALU.is_gt))
            link(nc.vector.tensor_reduce(np_s[:, 0:1], np_f[:, :], AX.X, ALU.add))
            link(nc.vector.tensor_scalar(np_s[:, 1:2], np_s[:, 0:1], float(E // 2 - 1), None, ALU.add))
            link(nc.vector.tensor_scalar(np_s[:, 0:1], np_s[:, 0:1], float(E // 2), None, ALU.add))
            nc.vector.tensor_copy(pairs_i[:, :], np_s[:, :]).then_inc(blocks_ready, 1)
            split_lo(1, 1, range(2))
            take_xT(0, 0)
            take_xT(1, 1)
            split_lo(1, 1, range(2, KT))
            dve.wait_ge(lexp_done, 2 * NT)
            link(nc.vector.reciprocal(lsum[:, :], lsum[:, :]))
            link(nc.vector.tensor_tensor(top2[:, :, :], top2[:, :, :], lsum[:, :].unsqueeze(2)
                                         .to_broadcast([P, NT, 2]), ALU.mult))
            link(nc.vector.tensor_reduce(wsum[:, :], top2[:, :, :], AX.X, ALU.add))
            link(nc.vector.tensor_scalar(wsum[:, :], wsum[:, :], 1e-10, None, ALU.max))
            link(nc.vector.reciprocal(wsum[:, :], wsum[:, :]))
            link(nc.vector.tensor_tensor(wk[:, :, :], top2[:, :, :], wsum[:, :].unsqueeze(2)
                                         .to_broadcast([P, NT, 2]), ALU.mult))
            link(nc.vector.tensor_tensor(wtmp[:, :, :], oh[:, 0], wk[:, :, 0:1].to_broadcast([P, NT, E]), ALU.mult))
            link(nc.vector.tensor_tensor(wsel[:, :, :], oh[:, 1], wk[:, :, 1:2].to_broadcast([P, NT, E]), ALU.mult))
            nc.vector.tensor_tensor(wsel[:, :, :], wsel[:, :, :], wtmp[:, :, :], ALU.add).then_inc(wsel_ready, 1)
            def take_h(b, u):
                dve.wait_ge(h_psum, b + 1)
                if not isinstance(b, int) or b:
                    dve.wait_ge(hT_psum, b)
                for c in range(2):
                    nc.vector.tensor_copy(hpre[:, c * 512:(c + 1) * 512], HP[u][c][:, :]).then_inc(hpre_ready, 1)

            def take_y(b, u, turn):
                dve.wait_ge(y_psum, b + 1)
                dve.wait_ge(y_free[u], 16 * turn)
                nc.vector.tensor_copy(ysb[:, u, :], YP[:, :]).then_inc(y_taken, 1)

            take_h(0, 0)
            dve.wait_ge(wselT_psum, 1)
            nc.vector.tensor_copy(wselT[:, :, :], pb[7][0:E, :].rearrange("e (t n) -> e t n", t=NT)) \
                .then_inc(y_taken, 1)
            take_h(1, 1)
            pairs = pair_count(dve)
            with dve.Fori(1, pairs) as i:
                for u in range(2):
                    take_xT(2 * i + u, u)
                    split_lo(2 * i + u, u, range(KT))
                    take_y(2 * i + u - 2, u, i)
                    take_h(2 * i + u, u)
            last = dve.value_load(pairs_i[0:1, 1:2], min_val=E // 2 - 1, max_val=MAX_BLOCKS // 2 - 1)
            link(nc.vector.tensor_scalar(base_slot[:, :], np_s[:, 1:2], 2.0 * P, None, ALU.mult))
            link(nc.vector.tensor_scalar(rel[:, :, :], slot_k[:, :, :], base_slot[:, 0:1], None, ALU.subtract))
            link(nc.vector.tensor_scalar(early[:, :, :], rel[:, :, :], 0.0, None, ALU.is_lt))
            link(nc.vector.tensor_tensor(wgot[:, :, :], early[:, :, :], wk[:, :, :].rearrange("p t c -> p c t"),
                                         ALU.mult))
            dve.wait_ge(slot_row_made, 1)
            link(nc.vector.tensor_copy(slot_row[:, :], slot_row_i))
            for n in range(NT):
                link(nc.vector.tensor_scalar(last_w[:, n, :], slot_row[:, :], rel[:, 0, n:n + 1], wk[:, n, 0:1],
                                             ALU.is_equal, ALU.mult))
                link(nc.vector.tensor_scalar(last_w2[:, :], slot_row[:, :], rel[:, 1, n:n + 1], wk[:, n, 1:2],
                                             ALU.is_equal, ALU.mult))
                ins = nc.vector.tensor_tensor(last_w[:, n, :], last_w[:, n, :], last_w2[:, :], ALU.add)
                if n < NT - 1:
                    link(ins)
            ins.then_inc(last_ready, 1)
            take_y(2 * last, 0, last + 1)
            for u in range(2):
                dve.wait_ge(lastT_psum, u + 1)
                nc.vector.tensor_copy(last_wT[:, u], XT[:, :].rearrange("p (t n) -> p t n", t=NT)) \
                    .then_inc(last_taken, 1)

            def add_gathered(n):
                dve.wait_ge(y_gathered[n], 32)
                for c in range(2):
                    link(nc.vector.scalar_tensor_tensor(cn[:, n, :], got[:, n, c, :], wgot[:, c, n:n + 1],
                                                        cn[:, n, :], ALU.mult, ALU.add))

            for n in range(NT):
                add_gathered(n)
            take_y(2 * last + 1, 1, last + 1)
            for n in range(NT):
                y = got[:, n, 0, :]
                dve.wait_ge(last_psum, n + 1)
                link(nc.vector.tensor_tensor(y, pb[n][:, :], cn[:, n, :], ALU.add))
                link(nc.vector.tensor_scalar(y, y, CLIP, -CLIP, ALU.min, ALU.max))
                nc.vector.tensor_tensor(y, y, x_res[:, n, :], ALU.add).then_inc(final_ready, 1)

        @block.tensor
        def _(pe):
            mm = nc.tensor.matmul

            def transposes(bank, src):
                for k in range(KT):
                    ins = nc.tensor.transpose(bank[:, tile(k)], src[:, tile(k)], ident[:, :])
                return ins

            def turn_normed(l, n):
                pe.wait_ge(normed, NT * l + n + 1)
                transposes(turn_bank(l, n), cn[:, n, :]).then_inc(cT_psum, 1)

            pe.wait_ge(consts, CONSTS)

            def scores(n):
                pe.wait_ge(cw_ready, KT * (n + 1))
                pe.wait_ge(ctxT_in, 32 * (n + 1))
                if n:
                    pe.wait_ge(exp_done, n)
                for k in range(KT):
                    for j in range(2):
                        ins = mm(SC[S * j:S * (j + 1), :], cwT[:, k, n * P + S * j:n * P + S * (j + 1)],
                                 ctxT[:, j, k, :], start=(k == 0), stop=(k == KT - 1))
                ins.then_inc(s_psum, 1)

            def project(n, part, src):
                if n == 0:
                    pe.wait_ge(wl_in[part], 16)
                for k in range(KT):
                    ins = mm(Z[n][:, :], src[:, k, tile(n)], wl[:, KT * part + k, :],
                             start=(part == 0 and k == 0), stop=(part == 2 and k == KT - 1))
                return ins

            def row_terms(n):
                if n:
                    pe.wait_ge(q2c_taken, n)
                for k in range(KT):
                    ins = mm(MI[:, 0:1], cT[:, k, tile(n)], wc[:, k:k + 1], start=(k == 0), stop=(k == KT - 1))
                ins.then_inc(r_psum, 1)

            def project_c2q(n):
                pe.wait_ge(c2qT_ready, n + 1)
                project(n, 1, c2qT)
                pe.wait_ge(cc_ready, n + 1)
                project(n, 2, ccT).then_inc(z_psum, 1)

            turn_normed(0, 0)
            scores(0)
            turn_normed(0, 1)
            row_terms(0)
            project(0, 0, cT)
            for n in range(NT):
                pe.wait_ge(exp_done, n + 1)
                if n:
                    pe.wait_ge(c2qT_ready, n)
                transposes(TR, att[:, :]).then_inc(aT_psum, 1)
                pe.wait_ge(m_ready, n + 1)
                nc.tensor.transpose(MI[0:1, P:2 * P], msum[:, n:n + 1], ident[:, :]).then_inc(mT_psum, 1)
                if n:
                    project_c2q(n - 1)
                else:
                    turn_normed(0, 2)
                pe.wait_ge(aT_ready, n + 1)
                pe.wait_ge(ctxN_in, 32 * (n + 1))
                if n:
                    pe.wait_ge(c2q_ready, n)
                for k in range(KT):
                    for j in range(2):
                        ins = mm(CQ[S * j:S * (j + 1), :], attT[:, k, S * j:S * (j + 1)], ctxN[:, j, k, :],
                                 start=(k == 0), stop=(k == KT - 1))
                ins.then_inc(cq_psum, 1)
                pe.wait_ge(mn_ready, n + 1)
                nc.tensor.transpose(MI[:, 2 * P:2 * P + 1], mT[:, :, :].rearrange("n j s -> n (j s)"),
                                    ident[0:1, 0:1]).then_inc(mn_psum, 1)
                if n == 0:
                    turn_normed(0, 3)
                if n + 1 < NT:
                    scores(n + 1)
                pe.wait_ge(batt_ready, 2 * n + 2)
                for k in range(KT):
                    ins = mm(MI[:, Q2C + 2 * k:Q2C + 2 * k + 2], cn[:, n, tile(k)], batt[:, n, :],
                             start=True, stop=True)
                ins.then_inc(q2c_psum, 1)
                if n + 1 < NT:
                    project(n + 1, 0, cT)
                    row_terms(n + 1)
                pe.wait_ge(c2q_ready, n + 1)
                transposes(TR, c2q[:, :]).then_inc(c2qT_psum, 1)
                pe.wait_ge(cqT_ready, n + 1)
                project(n, 3, cqT)
                if 0 < n < NT - 1:
                    turn_normed(1, n - 1)
            project_c2q(NT - 1)
            turn_normed(1, NT - 2)

            def fill(slot):
                if slot is None:
                    return
                what, n = slot[0:2]
                if what == "out":
                    out_project(n)
                    return
                g = FILLS.index(("conv", n, KT - 1) if what == "conv" else slot)
                bank = FB[g % 2]
                if g >= 2:
                    pe.wait_ge(fill_taken, g - 1)
                if g == 0:
                    pe.wait_ge(wqkv_in, 16)
                if what == "qk":
                    pe.wait_ge(cT_ready, NT + 2 * n + 2)
                    for i in range(2):
                        f = slot[2] + i
                        for k in range(KT):
                            ins = mm(bank[:, 2 * P * i:2 * P * (i + 1)], wqkv[:, k, tile(f)],
                                     cT[:, k, 2 * P * n:2 * P * (n + 1)], start=(k == 0), stop=(k == KT - 1))
                elif what == "v":
                    pe.wait_ge(cT_ready, NT + n + 1)
                    for k in range(KT):
                        ins = mm(bank[:, :], cT[:, k, tile(n)], wqkv[:, k, 2 * D:3 * D],
                                 start=(k == 0), stop=(k == KT - 1))
                else:
                    f = slot[2]
                    pe.wait_ge(o_ready, 2 * n + 2)
                    if n == 0:
                        pe.wait_ge(conv_in, 16)
                        pe.wait_ge(pads_ready, 2)
                    for tap in range(3):
                        for k in range(KT):
                            ins = mm(bank[:, tile(f)].rearrange("p (b s) -> p b s", b=2),
                                     conv[:, KT * tap + k, tile(f)], oT[:, k, 2 * n:2 * n + 2, tap:tap + S],
                                     start=(tap == 0 and k == 0), stop=(tap == 2 and k == KT - 1))
                    if f < KT - 1:
                        return
                ins.then_inc(filled, 1)

            def scores(m, half):
                n = m % NT
                if half == 0:
                    if m:
                        pe.wait_ge(sub_ready, m)
                    if m >= NT:
                        last = ("conv", n, KT - 1)
                    else:
                        last = BEFORE[-1] if n < 2 else ("qk", 1, 6)
                    pe.wait_ge(fill_taken, FILLS.index(last) + 1)
                    for b in range(2):
                        mm(PS[:, b, :], ident_bf[:, :], causal_bf[:, :, :].rearrange("p h k -> p (h k)"),
                           start=True, stop=False, skip_group_check=True)
                else:
                    pe.wait_ge(half_scored, m + 1)
                for c in range(KT):
                    for b in range(2):
                        r = 2 * half + b
                        for j in range(2):
                            rows = slice(DH * r, DH * (r + 1))
                            cols = slice(n * P + S * j, n * P + S * (j + 1))
                            at = 2 * P * half + S * c
                            ins = mm(PS[S * j:S * (j + 1), b, at:at + S], qT[rows, c, cols],
                                     kT[rows, c, cols], start=False, stop=True, skip_group_check=True)
                ins.then_inc(sc_psum if half else half_scored, 1)

            def values(m):
                pe.wait_ge(pr_ready, m + 1)
                if m:
                    pe.wait_ge(pT_ready, 2 * m)
                for g in range(2 * HR):
                    ins = nc.tensor.transpose(PT[g // 4][:, tile(g % 4)],
                                              prb[:, m % 2, 2 * g:2 * g + 2, :].rearrange("p h k -> p (h k)"),
                                              ident[:, :])
                ins.then_inc(pT_psum, 1)

            def outputs(m, w):
                n, u = m % NT, m % 2
                if w == 0:
                    pe.wait_ge(pT_ready, 2 * m + 2)
                    if m:
                        pe.wait_ge(o_ready, 2 * m)
                    if m < NT:
                        pe.wait_ge(vx_in[n], 32)
                else:
                    pe.wait_ge(o_psum, 2 * m + 1)
                for r in range(HR):
                    for hp in range(2):
                        h = HR * (2 * hp + w) + r
                        for j in range(2):
                            v = vN if w == j else vX
                            at = 2 * P * w + P * hp + S * j
                            ins = mm(PO[DH * r:DH * (r + 1), at:at + S],
                                     v[S * w:S * (w + 1), n, DH * h:DH * (h + 1)],
                                     prT[S * w:S * (w + 1), u, 4 * (r % 2) + 2 * (r // 2) + hp, S * j:S * (j + 1)],
                                     start=True, stop=True)
                ins.then_inc(o_psum, 1)

            def out_project(n):
                g = len(FILLS) + n
                if n >= 2:
                    pe.wait_ge(out_taken, n - 1)
                else:
                    pe.wait_ge(fill_taken, g - 1)
                pe.wait_ge(o_ready, 2 * (NT + n) + 2)
                if n == 0:
                    pe.wait_ge(wo_in, 16)
                for k in range(KT):
                    ins = mm(FB[g % 2][:, :], cT[:, k, tile(n)], wo[:, k, :], start=(k == 0), stop=(k == KT - 1))
                ins.then_inc(out_psum, 1)

            def turn_gate(n):
                pe.wait_ge(normed, 2 * NT + n + 1)
                if n:
                    pe.wait_ge(cT_ready, 2 * NT + n)
                transposes(TB, cn[:, n, :]).then_inc(cT_psum, 1)

            def gate_logits(n):
                pe.wait_ge(cT_ready, 2 * NT + n + 1)
                if n:
                    pe.wait_ge(lg_taken, n)
                for k in range(KT):
                    ins = mm(LG, cT[:, k, tile(n)], gate[:, k, :], start=(k == 0), stop=(k == KT - 1))
                ins.then_inc(lg_psum, 1)

            def counts(n):
                pe.wait_ge(sel_ready, n + 1)
                if n:
                    pe.wait_ge(before_ready, n)
                    pe.wait_ge(count_taken, n)
                for i, own in enumerate((before_bf, ones_bf)):
                    at = i * E
                    if n:
                        mm(CNT[:, at:at + E], ones_bf[:, :], sel_before[:, n, :], start=True, stop=False)
                    ins = mm(CNT[:, at:at + E], own[:, :], sel[:, n, :], start=(n == 0), stop=True)
                ins.then_inc(count_psum, 1)

            for what in BEFORE:
                fill(what)
            turn_normed(1, NT - 1)
            for m in range(2 * NT):
                scores(m, 0)
                fill(SLOTS[m][0])
                scores(m, 1)
                fill(SLOTS[m][1])
                if m:
                    values(m - 1)
                fill(SLOTS[m][2])
                if m:
                    outputs(m - 1, 0)
                fill(SLOTS[m][3])
                if m:
                    outputs(m - 1, 1)
            last = 2 * NT - 1
            values(last)
            outputs(last, 0)
            outputs(last, 1)
            turn_gate(0)
            gate_logits(0)
            out_project(2)
            turn_gate(1)
            counts(0)
            gate_logits(1)
            out_project(3)
            counts(1)
            turn_gate(2)
            gate_logits(2)
            turn_gate(3)
            gate_logits(3)
            counts(2)
            counts(3)
            def turn_x(b, u, loaded):
                pe.wait_ge(xg_in[u], loaded)
                if not isinstance(b, int) or b:
                    pe.wait_ge(xT_ready, b)
                transposes(XT, xg[:, u, :]).then_inc(xT_psum, 1)

            def hidden(b, u):
                pe.wait_ge(xT_ready, b + 1)
                if not isinstance(b, int):
                    pe.wait_ge(hpre_ready, 2 * b - 2)
                for k in range(KT):
                    pe.wait_ge(lo_ready, KT * b + k + 1)
                    for c in range(2):
                        at = slice(k * F + c * 512, k * F + (c + 1) * 512)
                        mm(HP[u][c][:, :], xr[:, 0, u, k, :], w1_hi[:, u, at], start=(k == 0), stop=False)
                        mm(HP[u][c][:, :], xr[:, 0, u, k, :], w1_lo[:, u, at], start=False, stop=False)
                        ins = mm(HP[u][c][:, :], xr[:, 1, u, k, :], w1_hi[:, u, at], start=False,
                                 stop=(k == KT - 1))
                ins.then_inc(h_psum, 1)

            def turn_hidden(b):
                pe.wait_ge(hpre_ready, 2 * b + 2)
                if not isinstance(b, int):
                    pe.wait_ge(gelu_done, b)
                for f in range(FT):
                    ins = nc.tensor.transpose(HT[f // 4][:, tile(f % 4)], hpre[:, tile(f)], ident[:, :])
                ins.then_inc(hT_psum, 1)

            def output(b, u, loaded):
                pe.wait_ge(gelu_done, b + 1)
                pe.wait_ge(w2_in[u], loaded)
                pe.wait_ge(y_taken, b + 1)
                for f in range(FT):
                    ins = mm(YP[:, :], hT[:, u, f, :], w2[:, u, f * D:(f + 1) * D], start=(f == 0), stop=(f == FT - 1))
                ins.then_inc(y_psum, 1)

            turn_x(0, 0, 16)
            turn_x(1, 1, 16)
            hidden(0, 0)
            turn_hidden(0)
            hidden(1, 1)
            pe.wait_ge(wsel_ready, 1)
            for n in range(NT):
                ins = nc.tensor.transpose(pb[7][0:E, tile(n)], wsel[:, n, :], ident[:, :])
            ins.then_inc(wselT_psum, 1)
            pairs = pair_count(pe)
            with pe.Fori(1, pairs) as i:
                for u in range(2):
                    turn_x(2 * i + u, u, 16 * i + 16)
                    output(2 * i + u - 2, u, 16 * i)
                    turn_hidden(2 * i + u - 1)
                    hidden(2 * i + u, u)
            last = pe.value_load(pairs_i[0:1, 1:2], min_val=E // 2 - 1, max_val=MAX_BLOCKS // 2 - 1)
            output(2 * last, 0, 16 * last + 16)

            def turn_last(u):
                if u:
                    pe.wait_ge(last_taken, u)
                else:
                    pe.wait_ge(last_ready, 1)
                for n in range(NT):
                    ins = nc.tensor.transpose(XT[:, tile(n)], last_w[:, n, tile(u)], ident[:, :])
                ins.then_inc(lastT_psum, 1)

            turn_last(0)
            turn_hidden(2 * last + 1)
            turn_last(1)

            def add_last(u):
                for n in range(NT):
                    ins = mm(pb[n][:, :], last_wT[:, u, n, :], ysb[:, u, :], start=False, stop=(u == 1))
                    if u:
                        ins.then_inc(last_psum, 1)

            for n in range(NT):
                mm(pb[n][:, :], wselT[:, n, :], b2_sb[:, :], start=True, stop=False)
            pe.wait_ge(y_taken, 2 * last + 2)
            pe.wait_ge(last_taken, 2)
            add_last(0)
            output(2 * last + 1, 1, 16 * last + 16)
            pe.wait_ge(y_taken, 2 * last + 3)
            add_last(1)


_NAMES = ["x", "ctx", "ctxT", "wcqT", "wqT", "wcT", "b_cq", "b_c", "b_q", "wlT", "b_l", "wqkvT", "qkv_bT", "convT",
          "conv_bT", "woT", "out_b", "gateT", "w1", "b1T", "w2", "b2"]


def kernel(x, ctx_1024, L0_xattn_w_cq, L0_xattn_b_cq, L0_xattn_w_c, L0_xattn_b_c, L0_xattn_w_q, L0_xattn_b_q,
           L0_xattn_W_l, L0_xattn_b_l, L0_attn_Wqkv_w, L0_attn_Wqkv_b, L0_attn_conv_w, L0_attn_conv_b,
           L0_attn_out_w, L0_attn_out_b, L0_ffn_gate_w, L0_ffn_w1, L0_ffn_b1, L0_ffn_w2, L0_ffn_b2):
    import numpy as np
    import concourse.bacc as bacc
    from concourse.bass_utils import run_bass_kernel_spmd

    def by_feature(v):
        return np.ascontiguousarray(np.asarray(v).reshape(-1, P).T)

    laid = {
        "x": np.asarray(x).reshape(N, D),
        "ctx": ctx_1024,
        "ctxT": np.asarray(ctx_1024).transpose(0, 2, 1),
        "wcqT": by_feature(L0_xattn_w_cq), "wqT": by_feature(L0_xattn_w_q), "wcT": by_feature(L0_xattn_w_c),
        "b_cq": np.asarray(L0_xattn_b_cq).reshape(1, 1), "b_c": np.asarray(L0_xattn_b_c).reshape(1, 1),
        "b_q": np.asarray(L0_xattn_b_q).reshape(1, 1),
        "wlT": np.asarray(L0_xattn_W_l).T, "b_l": np.asarray(L0_xattn_b_l).reshape(1, D),
        "wqkvT": np.asarray(L0_attn_Wqkv_w).T, "qkv_bT": by_feature(L0_attn_Wqkv_b),
        "convT": np.asarray(L0_attn_conv_w).transpose(2, 1, 0).reshape(3 * D, D),
        "conv_bT": by_feature(L0_attn_conv_b),
        "woT": np.asarray(L0_attn_out_w).T, "out_b": np.asarray(L0_attn_out_b).reshape(1, D),
        "gateT": np.asarray(L0_ffn_gate_w).T,
        "w1": L0_ffn_w1, "b1T": np.asarray(L0_ffn_b1).reshape(E, FT, P).transpose(0, 2, 1),
        "w2": L0_ffn_w2, "b2": L0_ffn_b2,
    }
    nc = bacc.Bacc("TRN2", target_bir_lowering=False, num_devices=1)
    arrays, t = {}, {}
    for name in _NAMES:
        a = np.ascontiguousarray(laid[name])
        arrays["in_" + name] = a
        t[name] = nc.dram_tensor("in_" + name, a.shape, mybir.dt.from_np(a.dtype), kind="ExternalInput").ap()
    out = nc.dram_tensor("out", [N, D], F32, kind="ExternalOutput").ap()
    perceiver_kernel(nc, t, out)
    r = run_bass_kernel_spmd(nc, [arrays], core_ids=[0])
    return r.results[0]["out"].reshape(B, S, D)
```

```python
from contextlib import ExitStack

import concourse.bass as bass
from concourse import mybir

F32 = mybir.dt.float32
F32R = mybir.dt.float32r
I32 = mybir.dt.int32
U32 = mybir.dt.uint32
BF16 = mybir.dt.bfloat16
ALU = mybir.AluOpType
ACT = mybir.ActivationFunctionType
AX = mybir.AxisListType

P = 128
B, S = 8, 64
D = 512
Q = 512
KT = D // P
N = B * S
NT = N // P
H, DH = 16, 32
HR = P // DH
E, F = 14, 1024
FT = F // P
MAX_BLOCKS = E + (2 * N - 1) // P + 1
OVER = MAX_BLOCKS - E
EPS = 1e-5
MASKED = -1e30
CLIP = 100.0
CONSTS = 9
SCORE_PARAMS = 6
PARAMS = 6
Q2C = 300
SCALE = float(DH) ** -0.5


def perceiver_kernel(nc, t, out):
    ctx = ExitStack()
    with ctx:
        def sb(name, shape, dt=F32):
            return ctx.enter_context(nc.sbuf_tensor(name, shape, dt))

        def overlaid(name, rounded_name, shape):
            with nc.sbuf_tensor(name, shape, F32) as plain:
                pass
            return plain, sb(rounded_name, shape, F32R)

        def sem(name):
            return ctx.enter_context(nc.semaphore(name))

        rows_dram = nc.dram_tensor("rows_dram", [MAX_BLOCKS * P, D], F32).ap()

        ident = sb("ident", [P, P])
        ones = sb("ones", [P, E])
        ones_bf = sb("ones_bf", [P, P], BF16); before_bf = sb("before_bf", [P, P], BF16)
        before = sb("before", [P, P])
        expert_row_i = sb("expert_row_i", [P, E], I32); over_row_i = sb("over_row_i", [P, OVER], I32)
        causal = sb("causal", [P, S])
        eps = sb("eps", [P, 1])
        ident_bf = sb("ident_bf", [P, P], BF16)
        causal_bf = sb("causal_bf", [P, 8, S], BF16)
        expert_row = sb("expert_row", [P, E])
        over_row = sb("over_row", [P, OVER])
        slot_row = sb("slot_row", [P, P])

        wcq = sb("wcq", [P, KT]); wq = sb("wq", [P, KT]); wc = sb("wc", [P, KT])
        scal = sb("scal", [P, 3]); bsum = sb("bsum", [P, 1])
        qkv_b = sb("qkv_b", [P, 3 * KT]); conv_b = sb("conv_b", [P, KT])
        gate = sb("gate", [P, KT, E])
        bl_row = sb("bl_row", [P, D]); ob_row = sb("ob_row", [P, D])
        b2_sb = sb("b2_sb", [E, D])

        x_res = sb("x_res", [P, NT, D])
        cn = sb("cn", [P, NT, D])
        cT, xr = overlaid("cT", "xr", [P, KT, N])
        xr = xr[:, :, :].rearrange("p a (u n) -> p (a u) n", n=KT * P).rearrange(
            "p (a u) (k n) -> p a u k n", a=2, n=P)
        w1, w1_lo = overlaid("w1", "w1_lo", [P, 2, KT * F])
        w2, w2_lo = overlaid("w2", "w2_lo", [P, 2, FT * D])
        wl = w2[:, :, :].rearrange("p a (k n) -> p (a k) n", n=D)
        w1_tiles = w1[:, :, :].rearrange("p a (k n) -> p (a k) n", n=D)
        conv = w1_tiles[:, 0:3 * KT, :]
        wo = w1_tiles[:, 3 * KT:4 * KT, :]
        wqkv, wqkv_lo = overlaid("wqkv", "wqkv_lo", [P, KT, 3 * D])
        wqkv_hi = w2_lo[:, :, :].rearrange("p a n -> p (a n)")[:, 0:KT * 3 * D].rearrange("p (k n) -> p k n", k=KT)
        c_hi = sb("c_hi", [P, KT, N], F32R)

        A1, w1_hi = overlaid("A1", "w1_hi", [P, 2 * 2 * KT * Q])
        w1_hi = w1_hi[:, :].rearrange("p (u n) -> p u n", u=2)
        ctxT = A1[:, 0:2 * KT * Q].rearrange("p (j k q) -> p j k q", j=2, k=KT)
        ctxN = A1[:, 2 * KT * Q:].rearrange("p (j k d) -> p j k d", j=2, k=KT)
        qT = A1[:, 0:2048].rearrange("p (k n) -> p k n", k=KT)
        kT = A1[:, 2048:4096].rearrange("p (k n) -> p k n", k=KT)
        vN = A1[:, 4096:6144].rearrange("p (t n) -> p t n", t=NT)
        vX = A1[:, 6144:8192].rearrange("p (t n) -> p t n", t=NT)
        wqkv_flat = wqkv[:, :, :].rearrange("p k n -> p (k n)")
        got = wqkv_flat[:, 0:2 * NT * D].rearrange("p (t c d) -> p t c d", t=NT, c=2)
        last_w = wqkv_flat[:, 4096:4608].rearrange("p (t s) -> p t s", t=NT)
        last_wT = wqkv_flat[:, 5120:5632].rearrange("p (t n) -> p t n", t=NT)
        A2, A2r = overlaid("A2", "A2r", [P, 3 * KT * N + KT * B * (S + 2)])
        cwT = A2[:, 0:2048].rearrange("p (k n) -> p k n", k=KT)
        c2qT, ccT, cqT = (A2[:, at:at + D].rearrange("p (k n) -> p k n", k=KT) for at in (2048, 2560, 3072))
        parts = A2r[:, 3584:7680].rearrange("p (q a n) -> p q a n", q=4, a=2).rearrange(
            "p q a (k n) -> p q a k n", k=KT)
        wl_hi = w1_lo[:, :, :].rearrange("p a (k n) -> p (a k) n", n=D)
        wl_lo = w2_lo[:, :, :].rearrange("p a (k n) -> p (a k) n", n=D)
        oT = A2[:, 6144:].rearrange("p (k b s) -> p k b s", k=KT, b=B)
        c_lo = A2r[:, 0:2048].rearrange("p (k n) -> p k n", k=KT)
        sco = w2[:, 1, 2048:4096].rearrange("p (u r k) -> p u r k", u=2, k=S)
        prb = A2[:, 2048:4096].rearrange("p (u r k) -> p u r k", u=2, k=S)
        prT = A2[:, 4096:6144].rearrange("p (u c n) -> p u c n", u=2, n=P)
        xg = A2[:, 0:1024].rearrange("p (u d) -> p u d", u=2)
        hpre = A2[:, 2048:3072]
        hT = A2[:, 3072:5120].rearrange("p (u f n) -> p u f n", u=2, f=FT)
        ysb = A2[:, 5120:6144].rearrange("p (u d) -> p u d", u=2)
        att = sb("att", [P, Q]); zero_rows = att
        attT = sb("attT", [P, KT, P]); c2q = sb("c2q", [P, D])
        slot_row_i = c2q[:, 0:P].bitcast(I32); last_w2 = c2q[:, P:2 * P]

        st = sb("st", [P, NT, 6]); mv = sb("mv", [P, NT, 2])
        sd = sb("sd", [P, NT]); rstd = sb("rstd", [P, NT])
        nmax = sb("nmax", [P, NT]); asum = sb("asum", [P, NT]); arec = sb("arec", [P, NT])
        msum = sb("msum", [P, NT])
        mT = sb("mT", [1, 2, S]); mmax = sb("mmax", [1, 2]); msb = sb("msb", [1, 2])
        batt = sb("batt", [P, NT, 2]); q2cT = sb("q2cT", [P, KT, B])
        hmax = sb("hmax", [P, H]); hsum = sb("hsum", [P, 2, H]); hrec = sb("hrec", [P, 2, H])
        lg = sb("lg", [P, NT, E]); lgc = sb("lgc", [P, NT, E]); lneg = sb("lneg", [P, NT]); top2 = sb("top2", [P, NT, 2])
        lsum = sb("lsum", [P, NT])
        top = sb("top", [P, NT, 8]); topi = sb("topi", [P, NT, 8], U32); topf = sb("topf", [P, NT, 2])
        wsum = sb("wsum", [P, NT]); wk = sb("wk", [P, NT, 2])
        oh = sb("oh", [P, 2, NT, E]); wsel = sb("wsel", [P, NT, E])
        wtmp = sb("wtmp", [P, NT, E]); wselT = sb("wselT", [E, NT, P])
        sel = sb("sel", [P, NT, E], BF16); sel_before = sb("sel_before", [P, NT, E], BF16)
        limit = sb("limit", [P, E]); offset = sb("offset", [P, E]); more = sb("more", [P, NT, E])
        made = sb("made", [P, NT, E]); shift = sb("shift", [P, E]); far = sb("far", [P, E]); cnt = sb("cnt", [P, 2 * E])
        slot = sb("slot", [P, E])
        slot_c = sb("slot_c", [P, 2, E]); key = sb("key", [P, NT, E]); base_slot = sb("base_slot", [P, 1])
        slot_k = sb("slot_k", [P, 2, NT]); slot_i = sb("slot_i", [P, 2, NT], I32)
        rel = sb("rel", [P, 2, NT]); early = sb("early", [P, 2, NT]); wgot = sb("wgot", [P, 2, NT])
        bm = wqkv_flat[:, 4096:4096 + OVER * NT * E].rearrange("p (o t e) -> p o t e", o=OVER, t=NT)
        blk_f = sb("blk_f", [P, MAX_BLOCKS]); blk_i = sb("blk_i", [P, MAX_BLOCKS], I32)
        np_f = sb("np_f", [P, 4]); np_s = sb("np_s", [P, 2]); pairs_i = sb("pairs_i", [P, 2], I32)
        b1_sb = sb("b1_sb", [P, 2, FT])

        banks = ctx.enter_context(nc.psum_tensor("banks", [P, 8, 512], F32))
        pb = [banks[:, i, :] for i in range(8)]
        Z = pb[0:4]
        SC, TR, CQ, MI = pb[4:8]
        FB, PT, TB, PS, PO = pb[0:2], pb[2:4], pb[4], banks[:, 5:7, :], pb[7]
        LG = pb[6][:, 0:E]
        CNT = pb[5]
        HALF = (pb[7][:, 0:D // 2], pb[6][:, 0:D // 2])
        HP, HT, XT, YP = (pb[0:2], pb[2:4]), pb[4:6], pb[6], pb[7]

        x_in = [sem(f"x_in{n}") for n in range(NT)]
        qkv_high, qkv_low_first, qkv_low, c_low = map(sem, ("qkv_high", "qkv_low_first", "qkv_low", "c_low"))
        wl_high, wl_low = sem("wl_high"), sem("wl_low")
        part_high = [sem(f"part_high{q}") for q in range(4)]; part_low = [sem(f"part_low{q}") for q in range(4)]
        q2c_taken, score_params_in = sem("q2c_taken"), sem("score_params_in")
        wqkv_in, conv_in, wo_in, params_in = map(sem, ("wqkv_in", "conv_in", "wo_in", "params_in"))
        ctxT_in, ctxN_in = sem("ctxT_in"), sem("ctxN_in")
        wl_in = [sem(f"wl_in{i}") for i in range(4)]
        w1_in, w2_in, b1_in = ([sem(f"{w}_in{u}") for u in range(2)] for w in ("w1", "w2", "b1"))
        consts, pool_step = sem("consts"), sem("pool_step")
        dve_step = sem("dve_step")
        normed, var_ready, root_ready = sem("normed"), sem("var_ready"), sem("root_ready")
        cT_psum, cT_ready, cw_ready = sem("cT_psum"), sem("cT_ready"), sem("cw_ready")
        s_psum, nmax_ready, exp_done, r_psum = map(sem, ("s_psum", "nmax_ready", "exp_done", "r_psum"))
        aT_psum, aT_ready, cq_psum, c2q_ready = map(sem, ("aT_psum", "aT_ready", "cq_psum", "c2q_ready"))
        c2qT_psum, c2qT_ready, cc_ready = map(sem, ("c2qT_psum", "c2qT_ready", "cc_ready"))
        m_ready, mT_psum, msub_ready, mexp_done = map(sem, ("m_ready", "mT_psum", "msub_ready", "mexp_done"))
        mn_ready, mn_psum, batt_ready, q2c_psum = map(sem, ("mn_ready", "mn_psum", "batt_ready", "q2c_psum"))
        cqT_ready, z_psum, pads_ready = sem("cqT_ready"), sem("z_psum"), sem("pads_ready")
        v_ready, fill_taken = sem("v_ready"), sem("fill_taken")
        filled = sem("filled")
        vx_in = [sem(f"vx_in{n}") for n in range(NT)]
        half_scored, sc_psum, sub_ready, pexp_done = map(sem, ("half_scored", "sc_psum", "sub_ready", "pexp_done"))
        hrec_ready, pr_ready, pT_psum, pT_ready = map(sem, ("hrec_ready", "pr_ready", "pT_psum", "pT_ready"))
        o_psum, o_ready, out_psum, out_taken = map(sem, ("o_psum", "o_ready", "out_psum", "out_taken"))
        lg_psum, lg_taken, lexp_done = map(sem, ("lg_psum", "lg_taken", "lexp_done"))
        top_ready = sem("top_ready")
        before_ready, last_psum, last_taken = sem("before_ready"), sem("last_psum"), sem("last_taken")
        count_taken = sem("count_taken")
        lastT_psum, last_ready, slot_row_made = sem("lastT_psum"), sem("last_ready"), sem("slot_row_made")
        sel_ready, count_psum, wsel_ready, wselT_psum = map(sem, ("sel_ready", "count_psum", "wsel_ready", "wselT_psum"))
        slots_ready, blocks_ready, scattered = map(sem, ("slots_ready", "blocks_ready", "scattered"))
        zero_made, rows_zeroed = sem("zero_made"), sem("rows_zeroed")
        gather_turn = sem("gather_turn")
        xg_in = [sem(f"xg_in{u}") for u in range(2)]
        hi_ready, lo_ready, xT_hi = sem("hi_ready"), sem("lo_ready"), sem("xT_hi")
        xT_psum, xT_ready, h_psum, hpre_ready = map(sem, ("xT_psum", "xT_ready", "h_psum", "hpre_ready"))
        hT_psum, gelu_done, y_psum = map(sem, ("hT_psum", "gelu_done", "y_psum"))
        y_taken = sem("y_taken")
        y_free = [sem(f"y_free{u}") for u in range(2)]
        y_gathered = [sem(f"y_gathered{n}") for n in range(NT)]
        half_psum, half_taken = sem("half_psum"), sem("half_taken")
        clipped, out_stored = sem("clipped"), sem("out_stored")
        final_ready = [sem(f"final_ready{n}") for n in range(NT)]

        block = ctx.enter_context(nc.Block())

        def tile(n):
            return slice(n * P, (n + 1) * P)

        def turn_bank(l, n):
            return TB if l == 2 else Z[n] if l == 1 or n >= 2 else (TR, CQ)[n]

        BEFORE = [("qk", 0, f) for f in range(0, 2 * KT, 2)]
        SLOTS = [
            [("v", 0), ("qk", 1, 0), ("qk", 1, 2), None],
            [("qk", 1, 4), ("qk", 1, 6), ("v", 1), None],
            [("v", 2), ("conv", 0, 0), ("conv", 0, 1), ("conv", 0, 2)],
            [("conv", 0, 3), ("v", 3), ("conv", 1, 0), ("conv", 1, 1)],
            [("conv", 1, 2), ("conv", 1, 3), ("conv", 2, 0), ("conv", 2, 1)],
            [("conv", 2, 2), ("conv", 2, 3), ("conv", 3, 0), ("conv", 3, 1)],
            [("conv", 3, 2), ("conv", 3, 3), ("out", 0), None],
            [("out", 1), None, None, None],
        ]
        FILLS = BEFORE + [f for slots in SLOTS for f in slots
                          if f and f[0] != "out" and not (f[0] == "conv" and f[2] < KT - 1)]

        def source(part, n):
            return (cT[:, :, tile(n)], c2qT, ccT, cqT)[part]

        def sixth(i):
            return slice(D * i // 2, D * (i + 1) // 2)

        WL_ORDER = (0, 3, 1, 2)

        def pair_count(eng):
            eng.wait_ge(blocks_ready, 1)
            return eng.value_load(pairs_i[0:1, 0:1], min_val=E // 2, max_val=MAX_BLOCKS // 2)

        def expert_of(eng, b):
            return eng.value_load(blk_i[0:1, bass.ds(b, 1)], min_val=0, max_val=E - 1)

        @block.sync
        def _(sp):
            def load_x(n):
                sp.dma_start(x_res[:, n, :], t["x"][tile(n), :]).then_inc(x_in[n], 16)

            def load_ctxT(n):
                if n:
                    sp.wait_ge(s_psum, n)
                for j in range(2):
                    sp.dma_start(ctxT[:, j], t["ctxT"][2 * n + j].rearrange("(k p) q -> p k q", p=P)) \
                        .then_inc(ctxT_in, 16)

            def load_ctxN(n):
                if n:
                    sp.wait_ge(cq_psum, n)
                for j in range(2):
                    sp.dma_start(ctxN[:, j], t["ctx"][2 * n + j].rearrange("(k p) d -> p k d", p=P)) \
                        .then_inc(ctxN_in, 16)

            def load_wl(part):
                sp.dma_start(wl[:, KT * part:KT * (part + 1), :],
                             t["wlT"][D * part:D * (part + 1), :].rearrange("(k p) n -> p k n", p=P)) \
                    .then_inc(wl_in[part], 16)

            load_x(0)
            load_x(1)
            load_ctxT(0)
            load_x(2)
            load_x(3)
            load_wl(0)
            load_ctxN(0)
            load_ctxT(1)
            load_wl(3)
            load_wl(1)
            load_wl(2)
            load_ctxN(1)
            load_ctxT(2)
            load_ctxN(2)
            load_ctxT(3)
            sp.dma_start(wqkv[:, :, :], t["wqkvT"].rearrange("(k p) n -> p k n", p=P)).then_inc(wqkv_in, 16)
            load_ctxN(3)
            sp.wait_ge(z_psum, NT)
            sp.dma_start(conv, t["convT"].rearrange("(k p) n -> p k n", p=P)).then_inc(conv_in, 16)
            sp.dma_start(wo, t["woT"].rearrange("(k p) n -> p k n", p=P)).then_inc(wo_in, 16)
            for n in range(NT):
                sp.wait_ge(v_ready, n + 1)
                for j in range(2):
                    sp.dma_start(vX[S * (1 - j):S * (2 - j), n, :], vN[S * j:S * (j + 1), n, :]) \
                        .then_inc(vx_in[n], 16)
            sp.wait_ge(zero_made, 1)
            sp.dma_start(rows_dram.rearrange("(b p) d -> p b d", p=P),
                         zero_rows[:, :].unsqueeze(1).to_broadcast([P, MAX_BLOCKS, D])).then_inc(rows_zeroed, 16)
            for u in range(2):
                if u == 0:
                    sp.wait_ge(filled, len(FILLS))
                else:
                    sp.wait_ge(out_psum, NT)
                sp.dma_start(w1[:, u, :].rearrange("p (k f) -> p k f", k=KT),
                             t["w1"][u].rearrange("(k p) f -> p k f", p=P)).then_inc(w1_in[u], 16)
                sp.dma_start(b1_sb[:, u, :], t["b1T"][u]).then_inc(b1_in[u], 16)
                if u == 0:
                    for v in range(2):
                        if v == 1:
                            sp.wait_ge(pexp_done, 2 * NT)
                        sp.dma_start(w2[:, v, :].rearrange("p (k f) -> p k f", k=FT),
                                     t["w2"][v].rearrange("(k p) f -> p k f", p=P)).then_inc(w2_in[v], 16)
            sp.wait_ge(scattered, 16 * 2 * NT)
            for u in range(2):
                sp.dma_start(xg[:, u, :], rows_dram[u * P:(u + 1) * P, :]).then_inc(xg_in[u], 16)
            pairs = pair_count(sp)
            with sp.Fori(1, pairs) as i:
                for u in range(2):
                    sp.wait_ge(xT_psum, 2 * i + u - 1)
                    sp.dma_start(xg[:, u, :], rows_dram.rearrange("(b p) d -> b p d", p=P)[bass.ds(2 * i + u, 1)]
                                 .rearrange("o p d -> p (o d)")).then_inc(xg_in[u], 16)
                    e = expert_of(sp, 2 * i + u)
                    sp.wait_ge(h_psum, 2 * i + u - 1)
                    sp.dma_start(w1[:, u, :].rearrange("p (k f) -> p k f", k=KT),
                                 t["w1"][bass.ds(e, 1)].rearrange("o (k p) f -> p (o k) f", p=P)) \
                        .then_inc(w1_in[u], 16)
            for n in (0, 2, 1, 3):
                sp.wait_ge(final_ready[n], 1)
                sp.dma_start(out[tile(n), :], got[:, n, 0, :]).then_inc(out_stored, 16)
            sp.wait_ge(out_stored, 16 * NT)

        @block.scalar
        def _(act):
            for dst, src in ((wcq, "wcqT"), (wq, "wqT"), (wc, "wcT")):
                act.dma_start(dst[:, :], t[src]).then_inc(score_params_in, 16)
            for i, name in enumerate(("b_cq", "b_c", "b_q")):
                act.dma_start(scal[:, i:i + 1], t[name].to_broadcast([P, 1])).then_inc(score_params_in, 16)
            def copy_cT(l, n):
                act.wait_ge(cT_psum, NT * l + n + 1)
                nc.scalar.activation((c_hi if l == 1 else cT)[:, :, tile(n)], turn_bank(l, n)[:, :].rearrange(
                    "p (k n) -> p k n", k=KT), ACT.Copy).then_inc(cT_ready, 1)

            def high_wl(i):
                part = WL_ORDER[i]
                act.wait_ge(wl_in[part], 16)
                quarter = slice(KT * part, KT * (part + 1))
                nc.scalar.activation(wl_hi[:, quarter, :], wl[:, quarter, :], ACT.Copy).then_inc(wl_high, 1)

            def high_part(part, n):
                if part == 0:
                    act.wait_ge(cT_ready, n + 1)
                elif part == 1:
                    act.wait_ge(c2qT_ready, n + 1)
                else:
                    act.wait_ge(cc_ready if part == 2 else cqT_ready, n + 1)
                nc.scalar.activation(parts[:, part, 0], source(part, n), ACT.Copy).then_inc(part_high[part], 1)

            def exp_scores(n):
                act.wait_ge(nmax_ready, n + 1)
                if n:
                    act.wait_ge(aT_psum, n)
                nc.scalar.activation(att[:, :], SC[:, :], ACT.Exp, bias=nmax[:, n:n + 1],
                                     accum_out=asum[:, n:n + 1]).then_inc(exp_done, 1)

            copy_cT(0, 0)
            high_part(0, 0)
            high_wl(0)
            copy_cT(0, 1)
            exp_scores(0)
            for n in range(NT):
                act.wait_ge(aT_psum, n + 1)
                if n:
                    act.wait_ge(cq_psum, n)
                nc.scalar.activation(attT[:, :, :], TR[:, :].rearrange("p (k n) -> p k n", k=KT),
                                     ACT.Copy).then_inc(aT_ready, 1)
                act.wait_ge(msub_ready, n + 1)
                nc.scalar.activation(mT[:, :, :], mT[:, :, :], ACT.Exp).then_inc(mexp_done, 1)
                if n == 0:
                    for later in range(2, NT):
                        copy_cT(0, later)
                if n + 1 < NT:
                    high_part(0, n + 1)
                if n == 0:
                    for i in range(1, 4):
                        high_wl(i)
                high_part(3, n)
                act.wait_ge(c2qT_psum, n + 1)
                nc.scalar.activation(c2qT, TR[:, :].rearrange("p (k n) -> p k n", k=KT),
                                     ACT.Copy).then_inc(c2qT_ready, 1)
                if n + 1 < NT:
                    exp_scores(n + 1)
                high_part(1, n)
                high_part(2, n)
                if 0 < n < NT - 1:
                    copy_cT(1, n - 1)

            def take(g):
                act.wait_ge(filled, g + 1)
                what, n = FILLS[g][0:2]
                bank = FB[g % 2]
                if what == "v":
                    nc.scalar.activation(vN[:, n, :], bank[:, :], ACT.Copy).then_inc(fill_taken, 1)
                    act.wait_ge(fill_taken, g + 1)
                    act.sem_inc(v_ready, 1)
                    return
                for i in range(KT if what == "conv" else 2):
                    if what == "conv":
                        dst, src, bias = qT[:, i, tile(n)], bank[:, tile(i)], conv_b[:, i:i + 1]
                    else:
                        f = FILLS[g][2] + i
                        dst = (qT if f < KT else kT)[:, f % KT, 2 * P * n:2 * P * (n + 1)]
                        src, bias = bank[:, 2 * P * i:2 * P * (i + 1)], qkv_b[:, f:f + 1]
                    ins = nc.scalar.activation(dst, src, ACT.Identity, bias=bias)
                ins.then_inc(fill_taken, 1)

            def exponentials(m):
                act.wait_ge(sub_ready, m + 1)
                if m >= 2:
                    act.wait_ge(pT_psum, m - 1)
                nc.scalar.activation(prb[:, m % 2], sco[:, m % 2], ACT.Exp, scale=SCALE) \
                    .then_inc(pexp_done, 1)

            def copy_prT(m):
                act.wait_ge(pT_psum, m + 1)
                if m >= 2:
                    act.wait_ge(o_psum, 2 * m - 2)
                for i in range(2):
                    nc.scalar.activation(prT[:, m % 2, 4 * i:4 * i + 4, :],
                                         PT[i][:, :].rearrange("p (c n) -> p c n", n=P),
                                         ACT.Copy).then_inc(pT_ready, 1)

            def split_hi(b, u, loaded):
                act.wait_ge(w1_in[u], loaded)
                for k in range(KT):
                    nc.scalar.activation(w1_hi[:, u, k * F:(k + 1) * F], w1[:, u, k * F:(k + 1) * F],
                                         ACT.Copy).then_inc(hi_ready, 1)

            def exp_logits(n):
                act.wait_ge(top_ready, n + 1)
                nc.scalar.activation(lg[:, n, :], lgc[:, n, :], ACT.Exp, bias=lneg[:, n:n + 1],
                                     accum_out=lsum[:, n:n + 1]).then_inc(lexp_done, 1)
                nc.scalar.activation(top2[:, n, :], top[:, n, 0:2], ACT.Exp, bias=lneg[:, n:n + 1]) \
                    .then_inc(lexp_done, 1)

            def high_qkv(i):
                if i == 0:
                    act.wait_ge(wqkv_in, 16)
                    act.wait_ge(z_psum, NT)
                nc.scalar.activation(wqkv_hi[:, :, sixth(i)], wqkv[:, :, sixth(i)], ACT.Copy).then_inc(qkv_high, 1)

            high_qkv(0)
            high_qkv(1)
            copy_cT(1, NT - 2)
            high_qkv(2)
            high_qkv(3)
            high_qkv(4)
            high_qkv(5)
            for g in range(len(BEFORE)):
                take(g)
            copy_cT(1, NT - 1)
            for m in range(2 * NT):
                if SLOTS[m][0] in FILLS:
                    take(FILLS.index(SLOTS[m][0]))
                exponentials(m)
                if m:
                    copy_prT(m - 1)
                for what in SLOTS[m][1:]:
                    if what in FILLS:
                        take(FILLS.index(what))
            def root(n):
                act.wait_ge(var_ready, n + 1)
                nc.scalar.activation(sd[:, n:n + 1], mv[:, n, 1:2], ACT.Sqrt, bias=eps[:, 0:1]) \
                    .then_inc(root_ready, 1)

            root(0)
            copy_prT(2 * NT - 1)
            copy_cT(2, 0)
            root(1)
            split_hi(0, 0, 16)
            copy_cT(2, 1)
            root(2)
            root(3)
            copy_cT(2, 2)
            copy_cT(2, 3)
            for n in range(NT):
                exp_logits(n)

            def gelu(b, u, loaded):
                act.wait_ge(hT_psum, b + 1)
                for f in range(FT):
                    if f == 0:
                        act.wait_ge(b1_in[u], loaded)
                    ins = nc.scalar.activation(hT[:, u, f, :], HT[f // 4][:, tile(f % 4)], ACT.Gelu,
                                               bias=b1_sb[:, u, f:f + 1])
                ins.then_inc(gelu_done, 1)

            def store_y(b, u):
                act.wait_ge(y_taken, b + 2)
                act.dma_start(rows_dram.rearrange("(b p) d -> b p d", p=P)[bass.ds(b, 1)]
                              .rearrange("o p d -> p (o d)"), ysb[:, u, :]).then_inc(y_free[u], 16)

            act.wait_ge(o_psum, 4 * NT)
            split_hi(1, 1, 16)
            gelu(0, 0, 16)
            pairs = pair_count(act)
            with act.Fori(1, pairs) as i:
                for u in range(2):
                    split_hi(2 * i + u, u, 16 * i + 16)
                    store_y(2 * i - 2 + u, u)
                    e = expert_of(act, 2 * i + u)
                    act.dma_start(w2[:, u, :].rearrange("p (k f) -> p k f", k=FT),
                                  t["w2"][bass.ds(e, 1)].rearrange("o (k p) f -> p (o k) f", p=P)) \
                        .then_inc(w2_in[u], 16)
                    if u == 0:
                        gelu(2 * i - 1, 1, 16 * i)
                    else:
                        gelu(2 * i, 0, 16 * i + 16)
                    act.wait_ge(gelu_done, 2 * i + u - 1)
                    act.dma_start(b1_sb[:, u, :], t["b1T"][bass.ds(e, 1)].rearrange("o p f -> p (o f)")) \
                        .then_inc(b1_in[u], 16)
            last = act.value_load(pairs_i[0:1, 1:2], min_val=E // 2 - 1, max_val=MAX_BLOCKS // 2 - 1)
            store_y(2 * last, 0)
            gelu(2 * last + 1, 1, 16 * last + 16)

        @block.gpsimd
        def _(pool):
            nc.gpsimd.memset(ident[:, :], 0.0).then_inc(pool_step, 1)
            nc.gpsimd.memset(before[:, :], 1.0).then_inc(pool_step, 1)
            nc.gpsimd.memset(causal[:, :], 0.0).then_inc(pool_step, 1)
            pool.wait_ge(pool_step, 3)
            nc.gpsimd.affine_select(out=ident[:, :], in_=ident[:, :], pattern=[[-1, P]], compare_op=ALU.not_equal,
                                    fill=1.0, base=0, channel_multiplier=1).then_inc(consts, 1)
            pool.wait_ge(consts, 1)
            nc.gpsimd.affine_select(out=before[:, :], in_=before[:, :], pattern=[[1, P]], compare_op=ALU.is_gt,
                                    fill=0.0, base=0, channel_multiplier=-1).then_inc(consts, 1)
            for j in range(2):
                pool.wait_ge(consts, 2 + j)
                v = causal[S * j:S * (j + 1), :]
                nc.gpsimd.affine_select(out=v, in_=v, pattern=[[-1, S]], compare_op=ALU.is_ge, fill=MASKED,
                                        base=0, channel_multiplier=1).then_inc(consts, 1)
            pool.wait_ge(consts, 4)
            nc.gpsimd.memset(ones[:, :], 1.0).then_inc(consts, 1)
            nc.gpsimd.memset(ones_bf[:, :], 1.0).then_inc(consts, 1)
            nc.gpsimd.memset(batt[:, :, :], 0.0).then_inc(consts, 1)
            nc.gpsimd.iota(expert_row_i[:, :], pattern=[[1, E]], base=0, channel_multiplier=0).then_inc(consts, 1)
            pool.wait_ge(consts, CONSTS - 1)
            nc.gpsimd.iota(over_row_i[:, :], pattern=[[1, OVER]], base=1, channel_multiplier=0).then_inc(consts, 1)

            for dst, src in ((qkv_b, "qkv_bT"), (conv_b, "conv_bT")):
                pool.dma_start(dst[:, :], t[src]).then_inc(params_in, 16)
            pool.dma_start(bl_row[:, :], t["b_l"].to_broadcast([P, D])).then_inc(params_in, 16)
            pool.dma_start(ob_row[:, :], t["out_b"].to_broadcast([P, D])).then_inc(params_in, 16)
            pool.dma_start(gate[:, :, :], t["gateT"].rearrange("(k p) e -> p k e", p=P)).then_inc(params_in, 16)
            pool.dma_start(b2_sb[:, :], t["b2"]).then_inc(params_in, 16)

            def norm_probabilities(m):
                pool.wait_ge(hrec_ready, m + 1)
                nc.gpsimd.tensor_tensor(prb[:, m % 2], prb[:, m % 2],
                                        hrec[:, m % 2, :].unsqueeze(2).to_broadcast([P, H, S]),
                                        ALU.mult).then_inc(pr_ready, 1)

            for i, part in enumerate(WL_ORDER):
                pool.wait_ge(wl_high, i + 1)
                quarter = slice(KT * part, KT * (part + 1))
                nc.gpsimd.tensor_tensor(wl_lo[:, quarter, :], wl[:, quarter, :], wl_hi[:, quarter, :].bitcast(F32),
                                        ALU.subtract).then_inc(wl_low, 1)
            for i in range(1, 6):
                pool.wait_ge(qkv_high, i + 1)
                nc.gpsimd.tensor_tensor(wqkv_lo[:, :, sixth(i)], wqkv[:, :, sixth(i)],
                                        wqkv_hi[:, :, sixth(i)].bitcast(F32), ALU.subtract).then_inc(qkv_low, 1)
            pool.wait_ge(z_psum, NT)
            for side in (0, S + 1):
                nc.gpsimd.memset(oT[:, :, :, side:side + 1], 0.0).then_inc(pads_ready, 1)
            nc.gpsimd.memset(zero_rows[:, :], 0.0).then_inc(zero_made, 1)
            nc.gpsimd.iota(slot_row_i, pattern=[[1, P]], base=0, channel_multiplier=0).then_inc(slot_row_made, 1)
            for m in range(2 * NT):
                norm_probabilities(m)

            pool.wait_ge(rows_zeroed, 16)
            for n in range(NT):
                pool.wait_ge(slots_ready, n + 1)
                for c in range(2):
                    pool.indirect_dma_start(rows_dram, bass.IndirectOffsetOnAxis(ap=slot_i[:, c, n:n + 1], axis=0),
                                            cn[:, n, :], None).then_inc(scattered, 16)
            for u in range(2):
                nc.gpsimd.memset(ysb[:, u, :], 0.0).then_inc(y_free[u], 16)
            pairs = pair_count(pool)
            pool.wait_ge(y_free[0], 16 * pairs + 16)
            pool.sem_inc(gather_turn, 1)
            pool.wait_ge(y_free[1], 16 * pairs)
            pool.sem_inc(gather_turn, 1)
            for n in range(NT):
                for c in range(2):
                    pool.indirect_dma_start(got[:, n, c, :], None, rows_dram,
                                            bass.IndirectOffsetOnAxis(ap=slot_i[:, c, n:n + 1], axis=0)) \
                        .then_inc(y_gathered[n], 16)
            for n in range(NT // 2):
                pool.wait_ge(clipped, n + 1)
                nc.gpsimd.tensor_tensor(got[:, n, 0, :], got[:, n, 0, :], x_res[:, n, :], ALU.add) \
                    .then_inc(final_ready[n], 1)

        @block.vector
        def _(dve):
            step = [0]

            def link(ins):
                step[0] += 1
                ins.then_inc(dve_step, 1)
                dve.wait_ge(dve_step, step[0])

            def norm(n, by_scalar=False):
                link(nc.vector.bn_stats(st[:, n, :], x_res[:, n, :]))
                var, r, h = mv[:, n, 1:2], rstd[:, n:n + 1], sd[:, n:n + 1]
                if by_scalar:
                    nc.vector.bn_aggr(mv[:, n, :], st[:, n, :]).then_inc(var_ready, 1)
                    dve.wait_ge(root_ready, n + 1)
                    link(nc.vector.reciprocal(r, h))
                    nc.vector.tensor_scalar(cn[:, n, :], x_res[:, n, :], mv[:, n, 0:1], r,
                                            ALU.subtract, ALU.mult).then_inc(normed, 1)
                    return
                link(nc.vector.bn_aggr(mv[:, n, :], st[:, n, :]))
                link(nc.vector.tensor_scalar(var, var, EPS, None, ALU.add))
                link(nc.vector.tensor_scalar(r.bitcast(I32), var.bitcast(I32), -0.5, 1597463007.0, ALU.mult, ALU.add))
                scale = 1.0
                for _ in range(3):
                    link(nc.vector.tensor_scalar(h, r, r, var, ALU.mult, ALU.mult))
                    link(nc.vector.scalar_tensor_tensor(r, h, 3.0 * scale * scale, r, ALU.subtract, ALU.mult))
                    scale = -2.0 * scale ** 3
                link(nc.vector.tensor_scalar(r, r, 1.0 / scale, None, ALU.mult))
                nc.vector.tensor_scalar(cn[:, n, :], x_res[:, n, :], mv[:, n, 0:1], r,
                                        ALU.subtract, ALU.mult).then_inc(normed, 1)

            dve.wait_ge(x_in[0], 16)
            norm(0)
            def widen(n):
                dve.wait_ge(cT_ready, n + 1)
                for k in range(KT):
                    nc.vector.tensor_scalar(cwT[:, k, tile(n)], cT[:, k, tile(n)], wcq[:, k:k + 1], wq[:, k:k + 1],
                                            ALU.mult, ALU.add).then_inc(cw_ready, 1)

            def score_maxima(n):
                dve.wait_ge(s_psum, n + 1)
                nc.vector.tensor_reduce(nmax[:, n:n + 1], SC[:, :], AX.X, ALU.max, negate=True) \
                    .then_inc(nmax_ready, 1)

            def token_weights_head(n):
                dve.wait_ge(r_psum, n + 1)
                dve.wait_ge(nmax_ready, n + 1)
                link(nc.vector.scalar_tensor_tensor(msum[:, n:n + 1], nmax[:, n:n + 1], -1.0, MI[:, 0:1],
                                                    ALU.mult, ALU.add))
                nc.vector.tensor_scalar(msum[:, n:n + 1], msum[:, n:n + 1], bsum[:, 0:1], None, ALU.add) \
                    .then_inc(m_ready, 1)
                dve.wait_ge(mT_psum, n + 1)
                link(nc.vector.tensor_copy(mT[:, :, :], MI[0:1, P:2 * P].rearrange("p (j s) -> p j s", j=2)))
                link(nc.vector.tensor_reduce(mmax[:, :], mT[:, :, :], AX.X, ALU.max))
                nc.vector.tensor_tensor(mT[:, :, :], mT[:, :, :], mmax[:, :].unsqueeze(2).to_broadcast([1, 2, S]),
                                        ALU.subtract).then_inc(msub_ready, 1)

            def token_weights_tail(n):
                dve.wait_ge(exp_done, n + 1)
                link(nc.vector.reciprocal(arec[:, n:n + 1], asum[:, n:n + 1]))
                dve.wait_ge(mexp_done, n + 1)
                link(nc.vector.tensor_reduce(msb[:, :], mT[:, :, :], AX.X, ALU.add))
                link(nc.vector.reciprocal(msb[:, :], msb[:, :]))
                nc.vector.tensor_tensor(mT[:, :, :], mT[:, :, :], msb[:, :].unsqueeze(2).to_broadcast([1, 2, S]),
                                        ALU.mult).then_inc(mn_ready, 1)
                dve.wait_ge(mn_psum, n + 1)
                for j in range(2):
                    nc.vector.tensor_copy(batt[S * j:S * (j + 1), n, j:j + 1],
                                          MI[S * j:S * (j + 1), 2 * P:2 * P + 1]).then_inc(batt_ready, 1)

            def norm_sums(n):
                dve.wait_ge(cq_psum, n + 1)
                if n:
                    dve.wait_ge(c2qT_psum, n)
                nc.vector.tensor_scalar(c2q[:, :], CQ[:, :], arec[:, n:n + 1], None, ALU.mult) \
                    .then_inc(c2q_ready, 1)

            def low_part(part, n):
                dve.wait_ge(part_high[part], n + 1)
                nc.vector.tensor_tensor(parts[:, part, 1], source(part, n), parts[:, part, 0].bitcast(F32),
                                        ALU.subtract).then_inc(part_low[part], 1)

            def times_batch_sum(n):
                dve.wait_ge(q2c_psum, n + 1)
                nc.vector.tensor_copy(q2cT[:, :, 2 * n:2 * n + 2],
                                      MI[:, Q2C:Q2C + 2 * KT].rearrange("p (k b) -> p k b", k=KT)) \
                    .then_inc(q2c_taken, 1)
                dve.wait_ge(q2c_taken, n + 1)
                nc.vector.tensor_tensor(cqT.rearrange("p k (b s) -> p k b s", b=2),
                                        cT[:, :, tile(n)].rearrange("p k (b s) -> p k b s", b=2),
                                        q2cT[:, :, 2 * n:2 * n + 2].unsqueeze(3).to_broadcast([P, KT, 2, S]),
                                        ALU.mult).then_inc(cqT_ready, 1)

            def times_c2q(n):
                dve.wait_ge(c2qT_ready, n + 1)
                nc.vector.tensor_tensor(ccT, c2qT, cT[:, :, tile(n)], ALU.mult).then_inc(cc_ready, 1)

            def add_z(n):
                dve.wait_ge(z_psum, n + 1)
                link(nc.vector.tensor_tensor(x_res[:, n, :], Z[n][:, :], x_res[:, n, :], ALU.add))
                norm(n)

            def low_c(n):
                dve.wait_ge(cT_ready, NT + n + 1)
                nc.vector.tensor_tensor(c_lo[:, :, tile(n)], turn_bank(1, n)[:, :].rearrange("p (k n) -> p k n", k=KT),
                                        c_hi[:, :, tile(n)].bitcast(F32), ALU.subtract).then_inc(c_low, 1)

            def add_bias(n):
                dve.wait_ge(normed, n + 1)
                link(nc.vector.tensor_tensor(x_res[:, n, :], x_res[:, n, :], bl_row[:, :], ALU.add))

            dve.wait_ge(score_params_in, 16 * SCORE_PARAMS)
            widen(0)
            low_part(0, 0)
            for n in range(1, NT - 1):
                dve.wait_ge(x_in[n], 16)
                norm(n)
            score_maxima(0)
            link(nc.vector.tensor_reduce(bsum[:, :], scal[:, :], AX.X, ALU.add))
            token_weights_head(0)
            dve.wait_ge(x_in[NT - 1], 16)
            norm(NT - 1)
            token_weights_tail(0)
            for n in range(1, NT):
                widen(n)
            dve.wait_ge(consts, CONSTS)
            link(nc.vector.tensor_copy(ident_bf[:, :], ident[:, :]))
            link(nc.vector.tensor_copy(before_bf[:, :], before[:, :]))
            link(nc.vector.tensor_copy(causal_bf[:, :, :], causal[:, :].unsqueeze(1).to_broadcast([P, 8, S])))
            link(nc.vector.tensor_copy(expert_row[:, :], expert_row_i[:, :]))
            link(nc.vector.tensor_copy(over_row[:, :], over_row_i[:, :]))
            link(nc.vector.tensor_scalar(offset[:, :], expert_row[:, :], float(P), None, ALU.mult))
            link(nc.vector.memset(limit[:, :], float(P)))
            link(nc.vector.memset(eps[:, :], EPS))

            dve.wait_ge(params_in, 16 * PARAMS)
            add_bias(0)
            for n in range(NT):
                if n:
                    token_weights_head(n)
                    token_weights_tail(n)
                if n + 1 < NT:
                    low_part(0, n + 1)
                norm_sums(n)
                if 0 < n < NT - 1:
                    add_z(n - 1)
                if n + 1 < NT:
                    score_maxima(n + 1)
                    add_bias(n + 1)
                times_batch_sum(n)
                low_part(3, n)
                times_c2q(n)
                low_part(1, n)
                low_part(2, n)
                if n >= 2:
                    low_c(n - 2)
            add_z(NT - 2)
            dve.wait_ge(qkv_high, 1)
            nc.vector.tensor_tensor(wqkv_lo[:, :, sixth(0)], wqkv[:, :, sixth(0)], wqkv_hi[:, :, sixth(0)].bitcast(F32),
                                    ALU.subtract).then_inc(qkv_low_first, 1)
            add_z(NT - 1)
            low_c(NT - 2)
            low_c(NT - 1)

            def softmax(m):
                u = m % 2
                dve.wait_ge(sc_psum, m + 1)
                if m >= 2:
                    dve.wait_ge(pexp_done, m - 1)
                scores = PS.rearrange("p b (g k) -> p (b g) k", k=S)
                link(nc.vector.tensor_reduce(hmax[:, :], scores, AX.X, ALU.max))
                nc.vector.tensor_tensor(sco[:, u], scores, hmax[:, :].unsqueeze(2).to_broadcast([P, H, S]),
                                        ALU.subtract).then_inc(sub_ready, 1)

            def sums(m):
                dve.wait_ge(pexp_done, m + 1)
                if m >= 2:
                    dve.wait_ge(pr_ready, m - 1)
                link(nc.vector.tensor_reduce(hsum[:, m % 2, :], prb[:, m % 2], AX.X, ALU.add))
                nc.vector.reciprocal(hrec[:, m % 2, :], hsum[:, m % 2, :]).then_inc(hrec_ready, 1)

            def take_out(m):
                n = m % NT
                dve.wait_ge(o_psum, 2 * m + 2)
                for w in range(2):
                    src = PO[:, 2 * P * w:2 * P * (w + 1)].rearrange("p (h b s) -> p h b s", h=2, b=2)
                    bias = qkv_b[:, 2 * KT + w:3 * KT:2].unsqueeze(2).unsqueeze(3).to_broadcast([P, 2, 2, S])
                    if m < NT:
                        dst = oT[:, w:KT:2, 2 * n:2 * n + 2, 1:S + 1]
                    else:
                        dst = cT[:, w:KT:2, tile(n)].rearrange("p h (b s) -> p h b s", b=2)
                    nc.vector.tensor_tensor(dst, src, bias, ALU.add).then_inc(o_ready, 1)

            def finish(n):
                dve.wait_ge(out_psum, n + 1)
                nc.vector.tensor_tensor(x_res[:, n, :], pb[(len(FILLS) + n) % 2][:, :], x_res[:, n, :], ALU.add) \
                    .then_inc(out_taken, 1)
                dve.wait_ge(out_taken, n + 1)
                norm(n, by_scalar=True)

            every = expert_row[:, :]

            def choose(n):
                dve.wait_ge(lg_psum, n + 1)
                nc.vector.tensor_copy(lgc[:, n, :], LG).then_inc(lg_taken, 1)
                dve.wait_ge(lg_taken, n + 1)
                link(nc.vector.max(top[:, n, :], lgc[:, n, :]))
                nc.vector.tensor_scalar(lneg[:, n:n + 1], top[:, n, 0:1], -1.0, None, ALU.mult).then_inc(top_ready, 1)
                link(nc.vector.max_index(topi[:, n, :], top[:, n, :], lgc[:, n, :]))
                link(nc.vector.tensor_copy(topf[:, n, :], topi[:, n, 0:2]))
                for c in range(2):
                    link(nc.vector.tensor_scalar(oh[:, c, n, :], every, topf[:, n, c:c + 1], None, ALU.is_equal))
                nc.vector.tensor_tensor(sel[:, n, :], oh[:, 0, n, :], oh[:, 1, n, :], ALU.add).then_inc(sel_ready, 1)
                if n + 1 < NT:
                    dve.wait_ge(sel_ready, n + 1)
                    if n == 0:
                        ins = nc.vector.tensor_copy(sel_before[:, 1, :], sel[:, 0, :])
                    else:
                        ins = nc.vector.tensor_tensor(sel_before[:, n + 1, :], sel_before[:, n, :], sel[:, n, :],
                                                      ALU.add)
                    ins.then_inc(before_ready, 1)
                    dve.wait_ge(before_ready, n + 1)

            def place(n):
                dve.wait_ge(count_psum, n + 1)
                nc.vector.tensor_copy(cnt[:, :], CNT[:, 0:2 * E]).then_inc(count_taken, 1)
                dve.wait_ge(count_taken, n + 1)
                pos, upto = cnt[:, 0:E], cnt[:, E:2 * E]
                link(nc.vector.tensor_tensor(more[:, n, :], upto, limit[:, :], ALU.is_gt))
                link(nc.vector.tensor_tensor_scan(made[:, n, :], ones[:, :], more[:, n, :],
                                                  made[:, n - 1, E - 1:E] if n else 0.0, ALU.mult, ALU.add))
                link(nc.vector.scalar_tensor_tensor(shift[:, :], made[:, n, :], float(P), limit[:, :],
                                                    ALU.mult, ALU.subtract))
                link(nc.vector.scalar_tensor_tensor(shift[:, :], shift[:, :], float(P * (E - 1)), offset[:, :],
                                                    ALU.add, ALU.subtract))
                link(nc.vector.tensor_tensor(far[:, :], pos, limit[:, :], ALU.is_ge))
                link(nc.vector.tensor_tensor(far[:, :], far[:, :], shift[:, :], ALU.mult))
                link(nc.vector.tensor_tensor(slot[:, :], pos, offset[:, :], ALU.add))
                link(nc.vector.tensor_tensor(slot[:, :], slot[:, :], far[:, :], ALU.add))
                link(nc.vector.tensor_tensor(slot_c[:, :, :], oh[:, :, n, :],
                                             slot[:, :].unsqueeze(1).to_broadcast([P, 2, E]), ALU.mult))
                link(nc.vector.tensor_reduce(slot_k[:, :, n], slot_c[:, :, :], AX.X, ALU.add))
                nc.vector.tensor_copy(slot_i[:, :, n], slot_k[:, :, n]).then_inc(slots_ready, 1)
                if n + 1 < NT:
                    link(nc.vector.tensor_tensor(shift[:, :], shift[:, :], more[:, n, :], ALU.mult))
                    link(nc.vector.tensor_tensor(offset[:, :], offset[:, :], shift[:, :], ALU.add))
                    link(nc.vector.scalar_tensor_tensor(limit[:, :], more[:, n, :], float(P), limit[:, :],
                                                        ALU.mult, ALU.add))

            def split_lo(b, u, parts):
                for k in parts:
                    dve.wait_ge(hi_ready, KT * b + k + 1)
                    part = slice(k * F, (k + 1) * F)
                    nc.vector.tensor_tensor(w1_lo[:, u, part], w1[:, u, part], w1_hi[:, u, part].bitcast(F32),
                                            ALU.subtract).then_inc(lo_ready, 1)

            def take_xT(b, u):
                dve.wait_ge(xT_psum, b + 1)
                if not isinstance(b, int):
                    dve.wait_ge(h_psum, b - 1)
                turned = XT[:, :].rearrange("p (k n) -> p k n", k=KT)
                nc.vector.tensor_copy(xr[:, 0, u], turned).then_inc(xT_hi, 1)
                dve.wait_ge(xT_hi, b + 1)
                nc.vector.tensor_tensor(xr[:, 1, u], turned, xr[:, 0, u].bitcast(F32), ALU.subtract) \
                    .then_inc(xT_ready, 1)

            for m in range(2 * NT):
                softmax(m)
                sums(m)
                if m < NT:
                    dve.wait_ge(normed, 2 * NT)
                    link(nc.vector.tensor_tensor(x_res[:, m, :], x_res[:, m, :], ob_row[:, :], ALU.add))
                if m:
                    take_out(m - 1)
            finish(0)
            take_out(2 * NT - 1)
            finish(1)
            choose(0)
            split_lo(0, 0, range(KT))
            finish(2)
            choose(1)
            place(0)
            finish(3)
            place(1)
            choose(2)
            choose(3)
            place(2)
            place(3)
            link(nc.vector.tensor_tensor(key[:, :, :], made[:, :, :], more[:, :, :], ALU.mult))
            for n in range(NT):
                link(nc.vector.tensor_tensor(bm[:, :, n, :], over_row[:, :].unsqueeze(2).to_broadcast([P, OVER, E]),
                                             key[:, n, :].unsqueeze(1).to_broadcast([P, OVER, E]), ALU.is_equal))
                link(nc.vector.tensor_tensor(bm[:, :, n, :], bm[:, :, n, :], expert_row[:, :].unsqueeze(1)
                                             .to_broadcast([P, OVER, E]), ALU.mult))
            link(nc.vector.tensor_copy(blk_f[:, 0:E], expert_row[:, :]))
            link(nc.vector.tensor_reduce(blk_f[:, E:MAX_BLOCKS], bm.rearrange("p o t e -> p o (t e)"), AX.X, ALU.add))
            link(nc.vector.tensor_copy(blk_i[:, :], blk_f[:, :]))
            for c in range(4):
                link(nc.vector.tensor_scalar(np_f[:, c:c + 1], made[:, NT - 1, E - 1:E], 2.0 * c, None, ALU.is_gt))
            link(nc.vector.tensor_reduce(np_s[:, 0:1], np_f[:, :], AX.X, ALU.add))
            link(nc.vector.tensor_scalar(np_s[:, 1:2], np_s[:, 0:1], float(E // 2 - 1), None, ALU.add))
            link(nc.vector.tensor_scalar(np_s[:, 0:1], np_s[:, 0:1], float(E // 2), None, ALU.add))
            nc.vector.tensor_copy(pairs_i[:, :], np_s[:, :]).then_inc(blocks_ready, 1)
            split_lo(1, 1, range(2))
            take_xT(0, 0)
            take_xT(1, 1)
            split_lo(1, 1, range(2, KT))
            dve.wait_ge(lexp_done, 2 * NT)
            link(nc.vector.reciprocal(lsum[:, :], lsum[:, :]))
            link(nc.vector.tensor_tensor(top2[:, :, :], top2[:, :, :], lsum[:, :].unsqueeze(2)
                                         .to_broadcast([P, NT, 2]), ALU.mult))
            link(nc.vector.tensor_reduce(wsum[:, :], top2[:, :, :], AX.X, ALU.add))
            link(nc.vector.tensor_scalar(wsum[:, :], wsum[:, :], 1e-10, None, ALU.max))
            link(nc.vector.reciprocal(wsum[:, :], wsum[:, :]))
            link(nc.vector.tensor_tensor(wk[:, :, :], top2[:, :, :], wsum[:, :].unsqueeze(2)
                                         .to_broadcast([P, NT, 2]), ALU.mult))
            link(nc.vector.tensor_tensor(wtmp[:, :, :], oh[:, 0], wk[:, :, 0:1].to_broadcast([P, NT, E]), ALU.mult))
            link(nc.vector.tensor_tensor(wsel[:, :, :], oh[:, 1], wk[:, :, 1:2].to_broadcast([P, NT, E]), ALU.mult))
            nc.vector.tensor_tensor(wsel[:, :, :], wsel[:, :, :], wtmp[:, :, :], ALU.add).then_inc(wsel_ready, 1)
            def take_h(b, u):
                dve.wait_ge(h_psum, b + 1)
                if not isinstance(b, int) or b:
                    dve.wait_ge(hT_psum, b)
                for c in range(2):
                    nc.vector.tensor_copy(hpre[:, c * 512:(c + 1) * 512], HP[u][c][:, :]).then_inc(hpre_ready, 1)

            def take_y(b, u, turn):
                dve.wait_ge(y_psum, b + 1)
                dve.wait_ge(y_free[u], 16 * turn)
                nc.vector.tensor_copy(ysb[:, u, :], YP[:, :]).then_inc(y_taken, 1)

            take_h(0, 0)
            dve.wait_ge(wselT_psum, 1)
            nc.vector.tensor_copy(wselT[:, :, :], pb[7][0:E, :].rearrange("e (t n) -> e t n", t=NT)) \
                .then_inc(y_taken, 1)
            take_h(1, 1)
            pairs = pair_count(dve)
            with dve.Fori(1, pairs) as i:
                for u in range(2):
                    take_xT(2 * i + u, u)
                    split_lo(2 * i + u, u, range(KT))
                    take_y(2 * i + u - 2, u, i)
                    take_h(2 * i + u, u)
            last = dve.value_load(pairs_i[0:1, 1:2], min_val=E // 2 - 1, max_val=MAX_BLOCKS // 2 - 1)
            link(nc.vector.tensor_scalar(base_slot[:, :], np_s[:, 1:2], 2.0 * P, float(P), ALU.mult, ALU.add))
            link(nc.vector.tensor_scalar(rel[:, :, :], slot_k[:, :, :], base_slot[:, 0:1], None, ALU.subtract))
            link(nc.vector.tensor_scalar(early[:, :, :], rel[:, :, :], 0.0, None, ALU.is_lt))
            link(nc.vector.tensor_tensor(wgot[:, :, :], early[:, :, :], wk[:, :, :].rearrange("p t c -> p c t"),
                                         ALU.mult))
            dve.wait_ge(slot_row_made, 1)
            link(nc.vector.tensor_copy(slot_row[:, :], slot_row_i))
            for n in range(NT):
                link(nc.vector.tensor_scalar(last_w[:, n, :], slot_row[:, :], rel[:, 0, n:n + 1], wk[:, n, 0:1],
                                             ALU.is_equal, ALU.mult))
                link(nc.vector.tensor_scalar(last_w2[:, :], slot_row[:, :], rel[:, 1, n:n + 1], wk[:, n, 1:2],
                                             ALU.is_equal, ALU.mult))
                ins = nc.vector.tensor_tensor(last_w[:, n, :], last_w[:, n, :], last_w2[:, :], ALU.add)
                if n < NT - 1:
                    link(ins)
            ins.then_inc(last_ready, 1)
            take_y(2 * last, 0, last + 1)
            dve.wait_ge(lastT_psum, 1)
            nc.vector.tensor_copy(last_wT, XT[:, :].rearrange("p (t n) -> p t n", t=NT)).then_inc(last_taken, 1)

            def add_gathered(n):
                dve.wait_ge(y_gathered[n], 32)
                for c in range(2):
                    link(nc.vector.scalar_tensor_tensor(cn[:, n, :], got[:, n, c, :], wgot[:, c, n:n + 1],
                                                        cn[:, n, :], ALU.mult, ALU.add))

            for n in range(NT - 1):
                add_gathered(n)
            for c in range(2):
                dve.wait_ge(half_psum, c + 1)
                if c == 0:
                    dve.wait_ge(y_free[1], 16 * last + 16)
                nc.vector.tensor_copy(ysb[:, 1, c * D // 2:(c + 1) * D // 2], HALF[c]).then_inc(half_taken, 1)
            add_gathered(NT - 1)
            for n in range(NT):
                y = got[:, n, 0, :]
                dve.wait_ge(last_psum, n + 1)
                link(nc.vector.tensor_tensor(y, pb[n][:, :], cn[:, n, :], ALU.add))
                nc.vector.tensor_scalar(y, y, CLIP, -CLIP, ALU.min, ALU.max).then_inc(clipped, 1)
                if n >= NT // 2:
                    dve.wait_ge(clipped, n + 1)
                    nc.vector.tensor_tensor(y, y, x_res[:, n, :], ALU.add).then_inc(final_ready[n], 1)

        @block.tensor
        def _(pe):
            mm = nc.tensor.matmul

            def transposes(bank, src):
                for k in range(KT):
                    ins = nc.tensor.transpose(bank[:, tile(k)], src[:, tile(k)], ident[:, :])
                return ins

            def turn_normed(l, n):
                pe.wait_ge(normed, NT * l + n + 1)
                transposes(turn_bank(l, n), cn[:, n, :]).then_inc(cT_psum, 1)

            pe.wait_ge(consts, CONSTS)

            def scores(n):
                pe.wait_ge(cw_ready, KT * (n + 1))
                pe.wait_ge(ctxT_in, 32 * (n + 1))
                if n:
                    pe.wait_ge(exp_done, n)
                for k in range(KT):
                    for j in range(2):
                        ins = mm(SC[S * j:S * (j + 1), :], cwT[:, k, n * P + S * j:n * P + S * (j + 1)],
                                 ctxT[:, j, k, :], start=(k == 0), stop=(k == KT - 1))
                ins.then_inc(s_psum, 1)

            def project(n, part):
                if n == 0:
                    pe.wait_ge(wl_low, WL_ORDER.index(part) + 1)
                pe.wait_ge(part_low[part], n + 1)
                for k in range(KT):
                    at = KT * part + k
                    mm(Z[n][:, :], parts[:, part, 0, k, :], wl_hi[:, at, :], start=(part == 0 and k == 0), stop=False)
                    mm(Z[n][:, :], parts[:, part, 0, k, :], wl_lo[:, at, :], start=False, stop=False)
                    ins = mm(Z[n][:, :], parts[:, part, 1, k, :], wl_hi[:, at, :], start=False,
                             stop=(part == 2 and k == KT - 1))
                return ins

            def row_terms(n):
                if n:
                    pe.wait_ge(q2c_taken, n)
                for k in range(KT):
                    ins = mm(MI[:, 0:1], cT[:, k, tile(n)], wc[:, k:k + 1], start=(k == 0), stop=(k == KT - 1))
                ins.then_inc(r_psum, 1)

            def project_c2q(n):
                project(n, 1)
                project(n, 2).then_inc(z_psum, 1)

            turn_normed(0, 0)
            scores(0)
            turn_normed(0, 1)
            row_terms(0)
            project(0, 0)
            for n in range(NT):
                pe.wait_ge(exp_done, n + 1)
                if n:
                    pe.wait_ge(c2qT_ready, n)
                transposes(TR, att[:, :]).then_inc(aT_psum, 1)
                pe.wait_ge(m_ready, n + 1)
                nc.tensor.transpose(MI[0:1, P:2 * P], msum[:, n:n + 1], ident[:, :]).then_inc(mT_psum, 1)
                if n:
                    project_c2q(n - 1)
                else:
                    turn_normed(0, 2)
                pe.wait_ge(aT_ready, n + 1)
                pe.wait_ge(ctxN_in, 32 * (n + 1))
                if n:
                    pe.wait_ge(c2q_ready, n)
                for k in range(KT):
                    for j in range(2):
                        ins = mm(CQ[S * j:S * (j + 1), :], attT[:, k, S * j:S * (j + 1)], ctxN[:, j, k, :],
                                 start=(k == 0), stop=(k == KT - 1))
                ins.then_inc(cq_psum, 1)
                pe.wait_ge(mn_ready, n + 1)
                nc.tensor.transpose(MI[:, 2 * P:2 * P + 1], mT[:, :, :].rearrange("n j s -> n (j s)"),
                                    ident[0:1, 0:1]).then_inc(mn_psum, 1)
                if n == 0:
                    turn_normed(0, 3)
                if n + 1 < NT:
                    scores(n + 1)
                pe.wait_ge(batt_ready, 2 * n + 2)
                for k in range(KT):
                    ins = mm(MI[:, Q2C + 2 * k:Q2C + 2 * k + 2], cn[:, n, tile(k)], batt[:, n, :],
                             start=True, stop=True)
                ins.then_inc(q2c_psum, 1)
                if n + 1 < NT:
                    project(n + 1, 0)
                    row_terms(n + 1)
                pe.wait_ge(c2q_ready, n + 1)
                transposes(TR, c2q[:, :]).then_inc(c2qT_psum, 1)
                project(n, 3)
                if 0 < n < NT - 1:
                    turn_normed(1, n - 1)
            project_c2q(NT - 1)
            turn_normed(1, NT - 2)

            def fill(slot):
                if slot is None:
                    return
                what, n = slot[0:2]
                if what == "out":
                    out_project(n)
                    return
                g = FILLS.index(("conv", n, KT - 1) if what == "conv" else slot)
                bank = FB[g % 2]
                if g >= 2:
                    pe.wait_ge(fill_taken, g - 1)
                if what == "qk":
                    pe.wait_ge(c_low, 2 * n + 2)
                    pe.wait_ge(qkv_low_first, 1)
                    if slot[2]:
                        pe.wait_ge(qkv_low, slot[2] // 2)
                    tokens = slice(2 * P * n, 2 * P * (n + 1))
                    for i in range(2):
                        f = slot[2] + i
                        onto = bank[:, 2 * P * i:2 * P * (i + 1)]
                        for k in range(KT):
                            mm(onto, wqkv_hi[:, k, tile(f)], c_hi[:, k, tokens], start=(k == 0), stop=False)
                            mm(onto, wqkv_hi[:, k, tile(f)], c_lo[:, k, tokens], start=False, stop=False)
                            ins = mm(onto, wqkv_lo[:, k, tile(f)], c_hi[:, k, tokens], start=False,
                                     stop=(k == KT - 1))
                elif what == "v":
                    pe.wait_ge(c_low, n + 1)
                    pe.wait_ge(qkv_low, 5)
                    for k in range(KT):
                        mm(bank[:, :], c_hi[:, k, tile(n)], wqkv_hi[:, k, 2 * D:3 * D], start=(k == 0), stop=False)
                        mm(bank[:, :], c_hi[:, k, tile(n)], wqkv_lo[:, k, 2 * D:3 * D], start=False, stop=False)
                        ins = mm(bank[:, :], c_lo[:, k, tile(n)], wqkv_hi[:, k, 2 * D:3 * D], start=False,
                                 stop=(k == KT - 1))
                else:
                    f = slot[2]
                    pe.wait_ge(o_ready, 2 * n + 2)
                    if n == 0:
                        pe.wait_ge(conv_in, 16)
                        pe.wait_ge(pads_ready, 2)
                    for tap in range(3):
                        for k in range(KT):
                            ins = mm(bank[:, tile(f)].rearrange("p (b s) -> p b s", b=2),
                                     conv[:, KT * tap + k, tile(f)], oT[:, k, 2 * n:2 * n + 2, tap:tap + S],
                                     start=(tap == 0 and k == 0), stop=(tap == 2 and k == KT - 1))
                    if f < KT - 1:
                        return
                ins.then_inc(filled, 1)

            def scores(m, half):
                n = m % NT
                if half == 0:
                    if m:
                        pe.wait_ge(sub_ready, m)
                    if m >= NT:
                        last = ("conv", n, KT - 1)
                    else:
                        last = BEFORE[-1] if n < 2 else ("qk", 1, 6)
                    pe.wait_ge(fill_taken, FILLS.index(last) + 1)
                    for b in range(2):
                        mm(PS[:, b, :], ident_bf[:, :], causal_bf[:, :, :].rearrange("p h k -> p (h k)"),
                           start=True, stop=False, skip_group_check=True)
                else:
                    pe.wait_ge(half_scored, m + 1)
                for c in range(KT):
                    for b in range(2):
                        r = 2 * half + b
                        for j in range(2):
                            rows = slice(DH * r, DH * (r + 1))
                            cols = slice(n * P + S * j, n * P + S * (j + 1))
                            at = 2 * P * half + S * c
                            ins = mm(PS[S * j:S * (j + 1), b, at:at + S], qT[rows, c, cols],
                                     kT[rows, c, cols], start=False, stop=True, skip_group_check=True)
                ins.then_inc(sc_psum if half else half_scored, 1)

            def values(m):
                pe.wait_ge(pr_ready, m + 1)
                if m:
                    pe.wait_ge(pT_ready, 2 * m)
                for g in range(2 * HR):
                    ins = nc.tensor.transpose(PT[g // 4][:, tile(g % 4)],
                                              prb[:, m % 2, 2 * g:2 * g + 2, :].rearrange("p h k -> p (h k)"),
                                              ident[:, :])
                ins.then_inc(pT_psum, 1)

            def outputs(m, w):
                n, u = m % NT, m % 2
                if w == 0:
                    pe.wait_ge(pT_ready, 2 * m + 2)
                    if m:
                        pe.wait_ge(o_ready, 2 * m)
                    if m < NT:
                        pe.wait_ge(vx_in[n], 32)
                else:
                    pe.wait_ge(o_psum, 2 * m + 1)
                for r in range(HR):
                    for hp in range(2):
                        h = HR * (2 * hp + w) + r
                        for j in range(2):
                            v = vN if w == j else vX
                            at = 2 * P * w + P * hp + S * j
                            ins = mm(PO[DH * r:DH * (r + 1), at:at + S],
                                     v[S * w:S * (w + 1), n, DH * h:DH * (h + 1)],
                                     prT[S * w:S * (w + 1), u, 4 * (r % 2) + 2 * (r // 2) + hp, S * j:S * (j + 1)],
                                     start=True, stop=True)
                ins.then_inc(o_psum, 1)

            def out_project(n):
                g = len(FILLS) + n
                if n >= 2:
                    pe.wait_ge(out_taken, n - 1)
                else:
                    pe.wait_ge(fill_taken, g - 1)
                pe.wait_ge(o_ready, 2 * (NT + n) + 2)
                if n == 0:
                    pe.wait_ge(wo_in, 16)
                for k in range(KT):
                    ins = mm(FB[g % 2][:, :], cT[:, k, tile(n)], wo[:, k, :], start=(k == 0), stop=(k == KT - 1))
                ins.then_inc(out_psum, 1)

            def turn_gate(n):
                pe.wait_ge(normed, 2 * NT + n + 1)
                if n:
                    pe.wait_ge(cT_ready, 2 * NT + n)
                transposes(TB, cn[:, n, :]).then_inc(cT_psum, 1)

            def gate_logits(n):
                pe.wait_ge(cT_ready, 2 * NT + n + 1)
                if n:
                    pe.wait_ge(lg_taken, n)
                for k in range(KT):
                    ins = mm(LG, cT[:, k, tile(n)], gate[:, k, :], start=(k == 0), stop=(k == KT - 1))
                ins.then_inc(lg_psum, 1)

            def counts(n):
                pe.wait_ge(sel_ready, n + 1)
                if n:
                    pe.wait_ge(before_ready, n)
                    pe.wait_ge(count_taken, n)
                for i, own in enumerate((before_bf, ones_bf)):
                    at = i * E
                    if n:
                        mm(CNT[:, at:at + E], ones_bf[:, :], sel_before[:, n, :], start=True, stop=False)
                    ins = mm(CNT[:, at:at + E], own[:, :], sel[:, n, :], start=(n == 0), stop=True)
                ins.then_inc(count_psum, 1)

            for what in BEFORE:
                fill(what)
            turn_normed(1, NT - 1)
            for m in range(2 * NT):
                scores(m, 0)
                fill(SLOTS[m][0])
                scores(m, 1)
                fill(SLOTS[m][1])
                if m:
                    values(m - 1)
                fill(SLOTS[m][2])
                if m:
                    outputs(m - 1, 0)
                fill(SLOTS[m][3])
                if m:
                    outputs(m - 1, 1)
            last = 2 * NT - 1
            values(last)
            outputs(last, 0)
            outputs(last, 1)
            turn_gate(0)
            gate_logits(0)
            out_project(2)
            turn_gate(1)
            counts(0)
            gate_logits(1)
            out_project(3)
            counts(1)
            turn_gate(2)
            gate_logits(2)
            turn_gate(3)
            gate_logits(3)
            counts(2)
            counts(3)
            def turn_x(b, u, loaded):
                pe.wait_ge(xg_in[u], loaded)
                if not isinstance(b, int) or b:
                    pe.wait_ge(xT_ready, b)
                transposes(XT, xg[:, u, :]).then_inc(xT_psum, 1)

            def hidden(b, u):
                pe.wait_ge(xT_ready, b + 1)
                if not isinstance(b, int):
                    pe.wait_ge(hpre_ready, 2 * b - 2)
                for k in range(KT):
                    pe.wait_ge(lo_ready, KT * b + k + 1)
                    for c in range(2):
                        at = slice(k * F + c * 512, k * F + (c + 1) * 512)
                        mm(HP[u][c][:, :], xr[:, 0, u, k, :], w1_hi[:, u, at], start=(k == 0), stop=False)
                        mm(HP[u][c][:, :], xr[:, 0, u, k, :], w1_lo[:, u, at], start=False, stop=False)
                        ins = mm(HP[u][c][:, :], xr[:, 1, u, k, :], w1_hi[:, u, at], start=False,
                                 stop=(k == KT - 1))
                ins.then_inc(h_psum, 1)

            def turn_hidden(b):
                pe.wait_ge(hpre_ready, 2 * b + 2)
                if not isinstance(b, int):
                    pe.wait_ge(gelu_done, b)
                for f in range(FT):
                    ins = nc.tensor.transpose(HT[f // 4][:, tile(f % 4)], hpre[:, tile(f)], ident[:, :])
                ins.then_inc(hT_psum, 1)

            def output(b, u, loaded):
                pe.wait_ge(gelu_done, b + 1)
                pe.wait_ge(w2_in[u], loaded)
                pe.wait_ge(y_taken, b + 1)
                for f in range(FT):
                    ins = mm(YP[:, :], hT[:, u, f, :], w2[:, u, f * D:(f + 1) * D], start=(f == 0), stop=(f == FT - 1))
                ins.then_inc(y_psum, 1)

            turn_x(0, 0, 16)
            turn_x(1, 1, 16)
            hidden(0, 0)
            turn_hidden(0)
            hidden(1, 1)
            pe.wait_ge(wsel_ready, 1)
            for n in range(NT):
                ins = nc.tensor.transpose(pb[7][0:E, tile(n)], wsel[:, n, :], ident[:, :])
            ins.then_inc(wselT_psum, 1)
            pairs = pair_count(pe)
            with pe.Fori(1, pairs) as i:
                for u in range(2):
                    turn_x(2 * i + u, u, 16 * i + 16)
                    output(2 * i + u - 2, u, 16 * i)
                    turn_hidden(2 * i + u - 1)
                    hidden(2 * i + u, u)
            last = pe.value_load(pairs_i[0:1, 1:2], min_val=E // 2 - 1, max_val=MAX_BLOCKS // 2 - 1)
            output(2 * last, 0, 16 * last + 16)
            turn_hidden(2 * last + 1)
            pe.wait_ge(last_ready, 1)
            for n in range(NT):
                ins = nc.tensor.transpose(XT[:, tile(n)], last_w[:, n, :], ident[:, :])
            ins.then_inc(lastT_psum, 1)
            for n in range(NT):
                mm(pb[n][:, :], wselT[:, n, :], b2_sb[:, :], start=True, stop=False, skip_group_check=True)
            pe.wait_ge(gelu_done, 2 * last + 2)
            pe.wait_ge(w2_in[1], 16 * last + 16)
            pe.wait_ge(y_taken, 2 * last + 2)
            pe.wait_ge(last_taken, 1)
            for c in range(2):
                for f in range(FT):
                    at = f * D + c * D // 2
                    ins = mm(HALF[c], hT[:, 1, f, :], w2[:, 1, at:at + D // 2], start=(f == 0), stop=(f == FT - 1))
                ins.then_inc(half_psum, 1)
            for n, c in ((0, 0), (1, 0), (0, 1), (1, 1), (2, 0), (2, 1), (3, 0), (3, 1)):
                pe.wait_ge(half_taken, c + 1)
                half = slice(c * D // 2, (c + 1) * D // 2)
                ins = mm(pb[n][:, half], last_wT[:, n, :], ysb[:, 1, half], start=False, stop=True,
                         skip_group_check=True)
                if c:
                    ins.then_inc(last_psum, 1)


_NAMES = ["x", "ctx", "ctxT", "wcqT", "wqT", "wcT", "b_cq", "b_c", "b_q", "wlT", "b_l", "wqkvT", "qkv_bT", "convT",
          "conv_bT", "woT", "out_b", "gateT", "w1", "b1T", "w2", "b2"]


def kernel(x, ctx_1024, L0_xattn_w_cq, L0_xattn_b_cq, L0_xattn_w_c, L0_xattn_b_c, L0_xattn_w_q, L0_xattn_b_q,
           L0_xattn_W_l, L0_xattn_b_l, L0_attn_Wqkv_w, L0_attn_Wqkv_b, L0_attn_conv_w, L0_attn_conv_b,
           L0_attn_out_w, L0_attn_out_b, L0_ffn_gate_w, L0_ffn_w1, L0_ffn_b1, L0_ffn_w2, L0_ffn_b2):
    import numpy as np
    import concourse.bacc as bacc
    from concourse.bass_utils import run_bass_kernel_spmd

    def by_feature(v):
        return np.ascontiguousarray(np.asarray(v).reshape(-1, P).T)

    laid = {
        "x": np.asarray(x).reshape(N, D),
        "ctx": ctx_1024,
        "ctxT": np.asarray(ctx_1024).transpose(0, 2, 1),
        "wcqT": by_feature(L0_xattn_w_cq), "wqT": by_feature(L0_xattn_w_q), "wcT": by_feature(L0_xattn_w_c),
        "b_cq": np.asarray(L0_xattn_b_cq).reshape(1, 1), "b_c": np.asarray(L0_xattn_b_c).reshape(1, 1),
        "b_q": np.asarray(L0_xattn_b_q).reshape(1, 1),
        "wlT": np.asarray(L0_xattn_W_l).T, "b_l": np.asarray(L0_xattn_b_l).reshape(1, D),
        "wqkvT": np.asarray(L0_attn_Wqkv_w).T, "qkv_bT": by_feature(L0_attn_Wqkv_b),
        "convT": np.asarray(L0_attn_conv_w).transpose(2, 1, 0).reshape(3 * D, D),
        "conv_bT": by_feature(L0_attn_conv_b),
        "woT": np.asarray(L0_attn_out_w).T, "out_b": np.asarray(L0_attn_out_b).reshape(1, D),
        "gateT": np.asarray(L0_ffn_gate_w).T,
        "w1": L0_ffn_w1, "b1T": np.asarray(L0_ffn_b1).reshape(E, FT, P).transpose(0, 2, 1),
        "w2": L0_ffn_w2, "b2": L0_ffn_b2,
    }
    nc = bacc.Bacc("TRN2", target_bir_lowering=False, num_devices=1)
    arrays, t = {}, {}
    for name in _NAMES:
        a = np.ascontiguousarray(laid[name])
        arrays["in_" + name] = a
        t[name] = nc.dram_tensor("in_" + name, a.shape, mybir.dt.from_np(a.dtype), kind="ExternalInput").ap()
    out = nc.dram_tensor("out", [N, D], F32, kind="ExternalOutput").ap()
    perceiver_kernel(nc, t, out)
    r = run_bass_kernel_spmd(nc, [arrays], core_ids=[0])
    return r.results[0]["out"].reshape(B, S, D)
```
